# Optimizing a Trainium2 kernel written in Bass

```python
import numpy as np
import jax
import jax.numpy as jnp

def _softmax(x, axis=-1):
    return jax.nn.softmax(x, axis=axis)

def _gelu(x):
    return jax.nn.gelu(x, approximate=True)

def _silu(x):
    return jax.nn.silu(x)

def _sigmoid(x):
    return jax.nn.sigmoid(x)

def _layernorm(x, axis=-1, eps=1e-05):
    m = jnp.mean(x, axis=axis, keepdims=True)
    v = jnp.var(x, axis=axis, keepdims=True)
    return (x - m) / jnp.sqrt(v + eps)

def _scatter_add(tgt, idx, src, axis=0):
    return tgt.at[idx].add(src)

def _segment_sum(src, seg, n):
    return jax.ops.segment_sum(src, seg, n)
kernel_name = 'mk_adaln_ffn_d2_seqx_r4_b8ac17'

def setup_inputs(seed: int=0):
    np.random.seed(seed)
    _w = jnp.asarray

    def _rec_inputs():
        import jax
        import jax.numpy as jnp
        _rk = jax.random.key(seed)
        x = -7.109e-05 + 0.9999 * jax.random.normal(jax.random.fold_in(_rk, 1), (32, 64, 512), jnp.float32)
        _lenS = 64 - jax.random.randint(jax.random.fold_in(_rk, 7), (32,), 0, max(1, 64 // 4) + 1, jnp.int32)
        _lenS2 = 64 - jax.random.randint(jax.random.fold_in(_rk, 8), (32,), 0, max(1, 64 // 4) + 1, jnp.int32)
        itok_B_1_198 = jax.random.randint(jax.random.fold_in(_rk, 11), (32,), 1, 199, jnp.int32)
        itok_B_0_7 = jax.random.randint(jax.random.fold_in(_rk, 12), (32,), 0, 8, jnp.int32)
        fside_8xS_0 = -0.00162727 + 0.0609077 * jax.random.normal(jax.random.fold_in(_rk, 13), (8, 64), jnp.float32)
        return (x, itok_B_1_198, itok_B_0_7, fside_8xS_0)
    x, itok_B_1_198, itok_B_0_7, fside_8xS_0 = _rec_inputs()

    def _L0_cond_setup():
        import jax, jax.numpy as jnp
        import numpy as np
        B, C, T = (128, 64, 512)
        S, D = (200, 64)
        key = jax.random.key(seed)
        k1, k2, k3 = jax.random.split(key, 3)
        x = jax.random.normal(k1, (B, C, T), dtype=jnp.float32)
        conditions = jax.random.randint(k2, (B,), 0, S, dtype=jnp.int64)
        weights = jax.random.normal(k3, (S, C, D), dtype=jnp.float32) / jnp.sqrt(jnp.float32(C))
        return {'x': x, 'conditions': conditions, 'weights': weights}
    _L0_cond_all = _L0_cond_setup()
    _L0_cond_in = {k: v for k, v in _L0_cond_all.items() if k in ('weights',)}
    del _L0_cond_all

    def _L0_ffn_setup():
        import jax, jax.numpy as jnp
        import numpy as np
        E, R, K = (8, 8, 2)
        D, F = (512, 2048)
        B, S = (2, 512)
        SCALING = 16.0 / 8.0

        def act(x):
            return jax.nn.gelu(x, approximate=True)
        key = jax.random.key(seed)
        ks = jax.random.split(key, 12)
        return {'hidden_states': jax.random.normal(ks[0], (B, S, D), jnp.float32), 'W_r': jax.random.normal(ks[1], (E, D), jnp.float32) * 0.02, 'b_r': jnp.zeros((E,), jnp.float32), 'W1': jax.random.normal(ks[2], (F, D), jnp.float32) * 0.02, 'b1': jnp.zeros((F,), jnp.float32), 'W2': jax.random.normal(ks[3], (D, F), jnp.float32) * 0.02, 'b2': jnp.zeros((D,), jnp.float32), 'A1': jax.random.normal(ks[4], (E, R, D), jnp.float32) * 0.02, 'B1': jax.random.normal(ks[5], (F, R) * 1 + ()).reshape(1, F, R).repeat(1, 0) * 0.0 + jax.random.normal(ks[5], (E, F, R), jnp.float32) * 0.02, 'A2': jax.random.normal(ks[6], (E, R, F), jnp.float32) * 0.02, 'B2': jax.random.normal(ks[7], (E, D, R), jnp.float32) * 0.02}
    _L0_ffn_all = _L0_ffn_setup()
    _L0_ffn_in = {k: v for k, v in _L0_ffn_all.items() if k in ('W_r', 'b_r', 'W1', 'b1', 'W2', 'b2', 'A1', 'B1', 'A2', 'B2')}
    del _L0_ffn_all

    def _L1_cond_setup():
        import jax, jax.numpy as jnp
        import numpy as np
        B, C, T = (64, 64, 512)
        D, N = (64, 8)
        key = jax.random.key(seed)
        k_x, k_s, k_w, k_b = jax.random.split(key, 4)
        scale = 1.0 / np.sqrt(C)
        x = jax.random.normal(k_x, (B, C, T), dtype=jnp.float32)
        subjects = jax.random.randint(k_s, (B,), 0, N, dtype=jnp.int64)
        weights = jax.random.normal(k_w, (N, C, D), dtype=jnp.float32) * scale
        bias = jax.random.normal(k_b, (N, D), dtype=jnp.float32) * scale
        return {'x': x, 'subjects': subjects, 'weights': weights, 'bias': bias}
    _L1_cond_all = _L1_cond_setup()
    _L1_cond_in = {k: v for k, v in _L1_cond_all.items() if k in ('weights',)}
    del _L1_cond_all

    def _L1_ffn_setup():
        import jax, jax.numpy as jnp
        import numpy as np
        B, S, D = (4, 128, 512)
        E, K, H = (8, 2, 352)
        HS = 2 * 352
        ALPHA = 0.001
        W_SCALE = 0.02

        def _moe_forward(hidden_states, gate_w, w_gate, w_up, w_down, sw_gate, sw_up, sw_down):
            b, s, d = hidden_states.shape
            x = hidden_states.reshape(-1, d)
            T = x.shape[0]
            logits = x @ gate_w
            scores = jax.nn.softmax(logits, axis=-1)
            topk_w, topk_idx = jax.lax.top_k(scores, K)
            mask = jax.nn.one_hot(topk_idx, E, dtype=scores.dtype).sum(axis=1)
            ce = mask.mean(axis=0)
            Pi = scores.mean(axis=0)
            aux_loss = (Pi * ce * E).sum() * ALPHA
            comb = jnp.zeros((T, E), dtype=x.dtype)
            comb = comb.at[jnp.arange(T)[:, None], topk_idx].add(topk_w)
            g = jax.nn.silu(jnp.einsum('td,edh->teh', x, w_gate)) * jnp.einsum('td,edh->teh', x, w_up)
            routed = jnp.einsum('teh,ehd,te->td', g, w_down, comb)
            shared = jax.nn.silu(x @ sw_gate) * (x @ sw_up) @ sw_down
            out = (routed + shared).reshape(b, s, d)
            return (out, aux_loss)
        key = jax.random.key(seed)
        ks = jax.random.split(key, 8)
        rn = lambda k, sh: jax.random.normal(k, sh, dtype=jnp.float32)
        return {'hidden_states': rn(ks[0], (B, S, D)), 'gate_w': rn(ks[1], (D, E)) * W_SCALE, 'w_gate': rn(ks[2], (E, D, H)) * W_SCALE, 'w_up': rn(ks[3], (E, D, H)) * W_SCALE, 'w_down': rn(ks[4], (E, H, D)) * W_SCALE, 'sw_gate': rn(ks[5], (D, HS)) * W_SCALE, 'sw_up': rn(ks[6], (D, HS)) * W_SCALE, 'sw_down': rn(ks[7], (HS, D)) * W_SCALE}
    _L1_ffn_all = _L1_ffn_setup()
    _L1_ffn_in = {k: v for k, v in _L1_ffn_all.items() if k in ('gate_w', 'w_gate', 'w_up', 'w_down', 'sw_gate', 'sw_up', 'sw_down')}
    del _L1_ffn_all
    return {'x': x, 'itok_B_1_198': itok_B_1_198, 'itok_B_0_7': itok_B_0_7, 'fside_8xS_0': fside_8xS_0, 'L0_cond_weights': _L0_cond_in['weights'], 'L0_ffn_W_r': _L0_ffn_in['W_r'], 'L0_ffn_b_r': _L0_ffn_in['b_r'], 'L0_ffn_W1': _L0_ffn_in['W1'], 'L0_ffn_b1': _L0_ffn_in['b1'], 'L0_ffn_W2': _L0_ffn_in['W2'], 'L0_ffn_b2': _L0_ffn_in['b2'], 'L0_ffn_A1': _L0_ffn_in['A1'], 'L0_ffn_B1': _L0_ffn_in['B1'], 'L0_ffn_A2': _L0_ffn_in['A2'], 'L0_ffn_B2': _L0_ffn_in['B2'], 'L1_cond_weights': _L1_cond_in['weights'], 'L1_ffn_gate_w': _L1_ffn_in['gate_w'], 'L1_ffn_w_gate': _L1_ffn_in['w_gate'], 'L1_ffn_w_up': _L1_ffn_in['w_up'], 'L1_ffn_w_down': _L1_ffn_in['w_down'], 'L1_ffn_sw_gate': _L1_ffn_in['sw_gate'], 'L1_ffn_sw_up': _L1_ffn_in['sw_up'], 'L1_ffn_sw_down': _L1_ffn_in['sw_down']}

def reference(x, itok_B_1_198, itok_B_0_7, fside_8xS_0, L0_cond_weights, L0_ffn_W_r, L0_ffn_b_r, L0_ffn_W1, L0_ffn_b1, L0_ffn_W2, L0_ffn_b2, L0_ffn_A1, L0_ffn_B1, L0_ffn_A2, L0_ffn_B2, L1_cond_weights, L1_ffn_gate_w, L1_ffn_w_gate, L1_ffn_w_up, L1_ffn_w_down, L1_ffn_sw_gate, L1_ffn_sw_up, L1_ffn_sw_down):
    import jax
    import jax.numpy as jnp

    def _L0_cond_ref(x, conditions, weights):
        import jax, jax.numpy as jnp
        import numpy as np
        B, C, T = (128, 64, 512)
        S, D = (200, 64)
        w = weights[conditions]
        return jnp.einsum('bct,bcd->bdt', x, w)

    def _L0_ffn_ref(hidden_states, W_r, b_r, W1, b1, W2, b2, A1, B1, A2, B2):
        import jax, jax.numpy as jnp
        import numpy as np
        E, R, K = (8, 8, 2)
        D, F = (512, 2048)
        B, S = (2, 512)
        SCALING = 16.0 / 8.0

        def act(x):
            return jax.nn.gelu(x, approximate=True)
        b, s, d = hidden_states.shape
        N = b * s
        x = hidden_states.reshape(N, d)
        probs = jax.nn.softmax(x @ W_r.T + b_r, axis=-1)
        w_topk, idx_topk = jax.lax.top_k(probs, K)
        base1 = x @ W1.T + b1
        u1 = jnp.einsum('nd,erd->ner', x, A1)
        B1_rf = B1.transpose(0, 2, 1).reshape(E * R, F)
        B2_rf = B2.transpose(0, 2, 1).reshape(E * R, d)
        res = jnp.zeros((N, d), hidden_states.dtype)
        for k in range(K):
            oh = jax.nn.one_hot(idx_topk[:, k], E, dtype=x.dtype)
            z1 = (u1 * oh[:, :, None]).reshape(N, E * R)
            h = act(base1 + z1 @ B1_rf * SCALING)
            u2 = jnp.einsum('nf,erf->ner', h, A2)
            z2 = (u2 * oh[:, :, None]).reshape(N, E * R)
            y = h @ W2.T + b2 + z2 @ B2_rf * SCALING
            res = res + w_topk[:, k:k + 1] * y
        return res.reshape(b, s, d)

    def _L1_cond_ref(x, subjects, weights, bias):
        import jax, jax.numpy as jnp
        import numpy as np
        B, C, T = (64, 64, 512)
        D, N = (64, 8)
        w = weights[subjects]
        b = bias[subjects]
        out = jnp.einsum('bct,bcd->bdt', x, w)
        out = out + b[:, :, None]
        return out

    def _L1_ffn_ref(hidden_states, gate_w, w_gate, w_up, w_down, sw_gate, sw_up, sw_down):
        import jax, jax.numpy as jnp
        import numpy as np
        B, S, D = (4, 128, 512)
        E, K, H = (8, 2, 352)
        HS = 2 * 352
        ALPHA = 0.001
        W_SCALE = 0.02

        def _moe_forward(hidden_states, gate_w, w_gate, w_up, w_down, sw_gate, sw_up, sw_down):
            b, s, d = hidden_states.shape
            x = hidden_states.reshape(-1, d)
            T = x.shape[0]
            logits = x @ gate_w
            scores = jax.nn.softmax(logits, axis=-1)
            topk_w, topk_idx = jax.lax.top_k(scores, K)
            mask = jax.nn.one_hot(topk_idx, E, dtype=scores.dtype).sum(axis=1)
            ce = mask.mean(axis=0)
            Pi = scores.mean(axis=0)
            aux_loss = (Pi * ce * E).sum() * ALPHA
            comb = jnp.zeros((T, E), dtype=x.dtype)
            comb = comb.at[jnp.arange(T)[:, None], topk_idx].add(topk_w)
            g = jax.nn.silu(jnp.einsum('td,edh->teh', x, w_gate)) * jnp.einsum('td,edh->teh', x, w_up)
            routed = jnp.einsum('teh,ehd,te->td', g, w_down, comb)
            shared = jax.nn.silu(x @ sw_gate) * (x @ sw_up) @ sw_down
            out = (routed + shared).reshape(b, s, d)
            return (out, aux_loss)
        out, _aux = _moe_forward(hidden_states, gate_w, w_gate, w_up, w_down, sw_gate, sw_up, sw_down)
        return out
    x = x + _L0_ffn_ref(_L0_cond_ref(x, itok_B_1_198, L0_cond_weights), L0_ffn_W_r, L0_ffn_b_r, L0_ffn_W1, L0_ffn_b1, L0_ffn_W2, L0_ffn_b2, L0_ffn_A1, L0_ffn_B1, L0_ffn_A2, L0_ffn_B2)
    x = x + _L1_ffn_ref(_L1_cond_ref(x, itok_B_0_7, L1_cond_weights, fside_8xS_0), L1_ffn_gate_w, L1_ffn_w_gate, L1_ffn_w_up, L1_ffn_w_down, L1_ffn_sw_gate, L1_ffn_sw_up, L1_ffn_sw_down)
    return x

_drawn_inputs = setup_inputs


def setup_inputs(seed=0):
    import zlib

    import numpy as np

    out = dict(_drawn_inputs(seed))
    spreads = {'L0_ffn_b_r': (0.0, 0.8), 'L0_ffn_b1': (0.0, 0.369), 'L0_ffn_b2': (0.0, 0.284)}
    factors = {'fside_8xS_0': 8.0,
     'L0_ffn_W_r': 2.941,
     'L0_ffn_A1': 6.769,
     'L0_ffn_B1': 6.736,
     'L0_ffn_A2': 6.819,
     'L0_ffn_B2': 6.926,
     'L1_ffn_gate_w': 5.295,
     'L1_ffn_w_gate': 4.686,
     'L1_ffn_w_up': 4.589,
     'L1_ffn_w_down': 4.583,
     'L1_ffn_sw_gate': 4.501,
     'L1_ffn_sw_up': 3.94,
     'L1_ffn_sw_down': 3.973}
    for name, (base, spread) in spreads.items():
        noise = np.random.default_rng([zlib.crc32(name.encode()), seed]).standard_normal(out[name].shape)
        drawn = base * np.exp(spread * noise) if base else spread * noise
        out[name] = jnp.asarray(drawn.astype(out[name].dtype))
    for name, factor in factors.items():
        out[name] = (out[name] * factor).astype(out[name].dtype)
    return out
```

```python
from contextlib import ExitStack

import concourse.bass as bass
from concourse import mybir

F32 = mybir.dt.float32
F32R = mybir.dt.float32r
BF16 = mybir.dt.bfloat16
I32 = mybir.dt.int32
ALU = mybir.AluOpType
ACT = mybir.ActivationFunctionType
AX = mybir.AxisListType

P = 128
D = 512
DC = D // P
SEQ = 64
E = 8
SUP = 512
TPS = SUP // P
LORA_SCALE = 2.0


def adaln_ffn(nc, x, itok0, itok1, side, cond0, router0, router0_b, w1b, w2, b2, a2, b2s,
              cond1, gate1, wgu1, wdn1, sgu1, sdn1, out, debug=None):
    N = x.shape[0]
    J = N // P
    NS = N // SUP
    FT = w1b.shape[0]
    ER = a2.shape[1]
    R = ER // E
    STEPS = NS * FT
    H1 = wdn1.shape[1]
    HC = -(-H1 // P)
    HP = sdn1.shape[0]
    SH = -(-HP // P)
    SLOT_TILES = 2 * J + E - 1
    ETAB = SLOT_TILES + 1
    WT = (DC + 1) * P
    WROW = w1b.shape[2]

    scr = lambda name, shape, dt=F32: nc.dram_tensor(name, shape, dt, kind="Internal").ap()
    xt_hi_d = scr("xt_hi_d", (NS, P, DC * SUP))
    xt_lo_d = scr("xt_lo_d", (NS, P, DC * SUP))
    wrow_d = scr("wrow_d", (2 * J, P))
    xc_d = scr("xc_d", (N, D))
    slot_d = scr("slot_d", (ETAB * P, 1), I32)
    yg_d = scr("yg_d", (SLOT_TILES * P, D))
    x1_d = out if debug == "x1" else scr("x1_d", (N, D))

    with ExitStack() as top:
        def sem(name):
            return top.enter_context(nc.semaphore(name))

        def tensors(stack):
            return lambda name, shape, dt=F32: stack.enter_context(nc.sbuf_tensor(name, shape, dt))

        psum = lambda name, shape, dt=F32: top.enter_context(nc.psum_tensor(name, shape, dt))

        ps_h = psum("ps_h", [P, 2, SUP])
        ps_y = psum("ps_y", [P, TPS, D])
        ps_u = psum("ps_u", [P, TPS, 2, ER])
        ps_t = psum("ps_t", [P, TPS, P])

        sb = tensors(top)
        ident = sb("ident", [P, P])
        zero16 = sb("zero16", [P, SUP], BF16)
        rev8 = sb("rev8", [P, E])
        tri = sb("tri", [P, P], BF16)
        ones16 = sb("ones16", [P, P], BF16)
        tok_id = sb("tok_id", [P, J], I32)
        cw1 = sb("cw1", [P, J, SEQ])
        side_col = sb("side_col", [P, J])
        it1_ix = sb("it1_ix", [P, J], I32)

        l0 = ExitStack()
        sb = tensors(l0)
        w2_hi = sb("w2_hi", [P, FT, D], F32R)
        w2_lo = sb("w2_lo", [P, FT, D], F32R)
        a2_hi = sb("a2_hi", [P, FT, ER], F32R)
        a2_lo = sb("a2_lo", [P, FT, ER], F32R)
        z_base = sb("z_base", [P, N], F32R)
        z_step = sb("z_step", [P, N], F32R)
        xt_hi = [sb(f"xt_hi{u}", [P, DC, SUP], F32R) for u in range(2)]
        xt_lo = [sb(f"xt_lo{u}", [P, DC, SUP], F32R) for u in range(2)]
        w_raw = [sb(f"w_raw{u}", [P, WROW]) for u in range(2)]
        w_hi = [sb(f"w_hi{u}", [P, DC + 1, P], F32R) for u in range(2)]
        w_lo = [sb(f"w_lo{u}", [P, DC + 1, P], F32R) for u in range(2)]
        b2s_hi = sb("b2s_hi", [P, D], F32R)
        b2s_lo = sb("b2s_lo", [P, D], F32R)
        b2_rows = sb("b2_rows", [P, D])
        bias1 = [sb(f"bias1{u}", [P, 1]) for u in range(2)]
        ra_hi = sb("ra_hi", [P, DC, E + ER], F32R)
        ra_lo = sb("ra_lo", [P, DC, E + ER], F32R)
        rb_rows = sb("rb_rows", [P, E])
        lu = sb("lu", [P, J, E + ER])
        rt = {n: sb(f"rt_{n}", [P, J, E]) for n in ("l", "p", "q", "oh0", "oh1", "oh0x", "ohdx")}
        rc = {n: sb(f"rc_{n}", [P, J]) for n in ("m", "s")}
        w01 = sb("w01", [P, 2, J])
        wsum = sb("wsum", [P, J])
        w01_t = sb("w01_t", [2 * J, P])
        zz = sb("zz", [P, TPS, ER])
        zq = sb("zq", [P, TPS, ER])
        z2c = sb("z2c", [P, TPS, 2 * ER], F32R)
        z2t = sb("z2t", [P, TPS, P], F32R)

        prep = ExitStack()
        sb = tensors(prep)
        pos64 = sb("pos64", [P, 1], I32)
        posf = sb("posf", [P, 1])
        it_in = sb("it_in", [P, J], I32)
        it_ix = sb("it_ix", [P, J], I32)
        it1_in = sb("it1_in", [P, J], I32)
        cw = sb("cw", [P, J, SEQ])
        bd = sb("bd", [P, J, P])
        x_in = sb("x_in", [P, TPS, D])
        a2_raw = sb("a2_raw", [P, FT, ER])
        ra_raw = sb("ra_raw", [P, DC, E + ER])
        b2s_raw = sb("b2s_raw", [P, D])
        zc = sb("zc", [P, 2, J, 2 * ER], F32R)
        uhi = z_step[:, 0:J * ER].rearrange("p (j n) -> p j n", j=J)
        prep.close()

        mainp = ExitStack()
        sb = tensors(mainp)
        h0 = [sb(f"h0{u}", [P, SUP]) for u in range(2)]
        h1 = [sb(f"h1{u}", [P, SUP]) for u in range(2)]
        g_hi = [sb(f"g_hi{u}", [P, SUP], F32R) for u in range(2)]
        g_lo = [sb(f"g_lo{u}", [P, SUP], F32R) for u in range(2)]
        g1_hi = [sb(f"g1_hi{u}", [P, SUP], F32R) for u in range(2)]
        g1_lo = [sb(f"g1_lo{u}", [P, SUP], F32R) for u in range(2)]
        wb = sb("wb", [P, 2, 2, SUP])
        xres = sb("xres", [P, TPS, D])
        mainp.close()
        l0.close()

        l1 = ExitStack()
        sb = tensors(l1)
        acc = sb("acc", [P, J, D])
        gate_hi = sb("gate_hi", [P, DC, E], F32R)
        gate_lo = sb("gate_lo", [P, DC, E], F32R)
        gate_raw = sb("gate_raw", [P, DC, E])
        lg1 = sb("lg1", [P, J, E])
        q1 = {n: sb(f"q1_{n}", [P, J, E]) for n in ("l", "p", "q", "oh0", "oh1")}
        c1 = {n: sb(f"c1_{n}", [P, J]) for n in ("m", "s")}
        w1k = sb("w1k", [P, 2, J])
        pos_i = sb("pos_i", [P, 2, J], I32)
        cnt = [sb(f"cnt{u}", [P, J, E]) for u in range(2)]
        rank = sb("rank", [P, J, E])
        mask16 = sb("mask16", [P, J, E], BF16)
        ex = {n: sb(f"ex_{n}", [P, E]) for n in ("t", "a", "b")}
        ex_i = sb("ex_i", [P, E], I32)
        etile = sb("etile", [P, ETAB])
        etab3 = sb("etab3", [P, ETAB, E])
        etab_f = sb("etab_f", [P, ETAB])
        etab = sb("etab", [P, ETAB], I32)
        zero_i = sb("zero_i", [ETAB, P], I32)
        slot_i = sb("slot_i", [ETAB, P], I32)
        slot_f = sb("slot_f", [ETAB, P])
        slot_tok = sb("slot_tok", [P, ETAB], I32)

        shared = ExitStack()
        sb = tensors(shared)
        bdq = [sb(f"bdq{u}", [P, TPS, P]) for u in range(2)]
        xc = sb("xc", [P, TPS, D])
        xs_hi = [sb(f"xs_hi{u}", [P, DC, SUP], F32R) for u in range(2)]
        xs_lo = [sb(f"xs_lo{u}", [P, DC, SUP], F32R) for u in range(2)]
        sg_hi = sb("sg_hi", [P, DC, 2, SH * P], F32R)
        sg_lo = sb("sg_lo", [P, DC, 2, SH * P], F32R)
        s_raw = [sb(f"s_raw{u}", [P, 2 * SH * P]) for u in range(2)]
        shared_a = ExitStack()
        shared.enter_context(shared_a)
        sd_hi = sb("sd_hi", [P, SH, D], F32R)
        sd_lo = sb("sd_lo", [P, SH, D], F32R)
        sh_s = sb("sh_s", [P, SUP])
        sh_g = sb("sh_g", [P, SUP])
        sh_hi = sb("sh_hi", [P, SH, SUP], F32R)
        sh_lo = sb("sh_lo", [P, SH, SUP], F32R)
        shared.close()

        routed = ExitStack()
        sb = tensors(routed)
        wgu = sb("wgu", [P, E, DC, 2 * H1])
        wdn = sb("wdn", [P, E, HC, D])
        xg = [sb(f"xg{u}", [P, D]) for u in range(2)]
        xg_t = [sb(f"xg_t{u}", [P, DC, P]) for u in range(2)]
        rs = sb("rs", [P, H1])
        rg = sb("rg", [P, H1])
        rg_t = sb("rg_t", [P, HC, P])
        yt = [sb(f"yt{u}", [P, D]) for u in range(2)]
        routed.close()

        final = ExitStack()
        sb = tensors(final)
        yk = [[sb(f"yk{k}{u}", [P, D]) for u in range(4)] for k in range(2)]
        final.close()
        l1.close()

        const_set = sem("const_set")
        small_in = sem("small_in")
        idx_done = sem("idx_done")
        cw_in = sem("cw_in")
        bd_zero = sem("bd_zero")
        bd_done = sem("bd_done")
        split_small = sem("split_small")
        x_in_s = sem("x_in_s")
        cond_done = sem("cond_done")
        xt_hi_done = sem("xt_hi_done")
        xt_lo_done = sem("xt_lo_done")
        xt_st = [sem(f"xt_st{u}") for u in range(2)]
        lg_done = sem("lg_done")
        lu_done = sem("lu_done")
        rch = sem("rch")
        r_max = sem("r_max")
        r_exp = sem("r_exp")
        zt_done = sem("zt_done")
        zt_read = sem("zt_read")
        w01_ok = sem("w01_ok")
        wt_sb = sem("wt_sb")
        wrow_st = sem("wrow_st")
        w2_in = [sem(f"w2_in{u}") for u in range(2)]
        w2_hi_done = sem("w2_hi_done")
        w2_lo_done = sem("w2_lo_done")
        w1_in = [sem(f"w1_in{u}") for u in range(2)]
        w1_hi_done = sem("w1_hi_done")
        w1_lo_done = sem("w1_lo_done")
        xt_in = [sem(f"xt_in{u}") for u in range(2)]
        wb_in = [sem(f"wb_in{u}") for u in range(2)]
        xres_in = sem("xres_in")
        x1_st = sem("x1_st")
        a_done = sem("a_done")
        z_done = sem("z_done")
        h0_done = sem("h0_done")
        h1_done = sem("h1_done")
        gch = sem("gch")
        g_done = sem("g_done")
        d_done = sem("d_done")
        z2_ok = sem("z2_ok")
        z2_t = sem("z2_t")
        z2_cp = sem("z2_cp")
        y_done = sem("y_done")
        y_read = sem("y_read")
        zero_done = sem("zero_done")
        ech = sem("ech")
        xb_done = sem("xb_done")

        l0_over = sem("l0_over")
        it1_done = sem("it1_done")
        cw1_in = sem("cw1_in")
        gate_in = sem("gate_in")
        gate_done = sem("gate_done")
        acc_in = sem("acc_in")
        bdq_zero = sem("bdq_zero")
        bdq_done = sem("bdq_done")
        c1_done = sem("c1_done")
        xc_done = sem("xc_done")
        xc_st = sem("xc_st")
        xt1_done = sem("xt1_done")
        xs_hi_done = sem("xs_hi_done")
        xs_lo_done = sem("xs_lo_done")
        xs_st = [sem(f"xs_st{u}") for u in range(2)]
        lg1_done = sem("lg1_done")
        lg1_read = sem("lg1_read")
        r1_max = sem("r1_max")
        r1_exp = sem("r1_exp")
        mask_ok = sem("mask_ok")
        cnt_done = sem("cnt_done")
        pos_ok = sem("pos_ok")
        etab_ok = sem("etab_ok")
        slot_zero = sem("slot_zero")
        slot_z_st = sem("slot_z_st")
        slot_st = sem("slot_st")
        slot_in = sem("slot_in")
        slot_cv = sem("slot_cv")
        slot_tr = sem("slot_tr")
        slot_ok = sem("slot_ok")
        s_in = [sem(f"s_in{u}") for u in range(2)]
        s_hi_done = sem("s_hi_done")
        s_lo_done = sem("s_lo_done")
        pad_done = sem("pad_done")
        xs_in = [sem(f"xs_in{u}") for u in range(2)]
        gu_done = sem("gu_done")
        sil_done = sem("sil_done")
        mul_done = sem("mul_done")
        shi_done = sem("shi_done")
        slo_done = sem("slo_done")
        sy_done = sem("sy_done")
        sy_read = sem("sy_read")
        sh_over = sem("sh_over")
        we_in = [sem(f"we_in{e}") for e in range(E)]
        xg_in = [sem(f"xg_in{u}") for u in range(2)]
        xgt_done = sem("xgt_done")
        xgt_cp = sem("xgt_cp")
        rgu_done = sem("rgu_done")
        rs_done = sem("rs_done")
        rg_done = sem("rg_done")
        rgt_done = sem("rgt_done")
        rgt_cp = sem("rgt_cp")
        ry_done = sem("ry_done")
        ry_cp = sem("ry_cp")
        yg_st = [sem(f"yg_st{u}") for u in range(2)]
        yk_in = [sem(f"yk_in{u}") for u in range(4)]
        yk_done = sem("yk_done")
        out_st = sem("out_st")

        def opened(eng, *sems, by=1):
            for which in sems:
                eng.sem_inc(which, by)

        def through(eng, which, count):
            eng.drain().then_inc(which, 1)
            eng.wait_ge(which, count)

        block = top.enter_context(nc.Block())
        G_OPS = 6

        def shared_halves(n):
            raw = s_raw[n % 2]
            if n < DC:
                return tuple(t[:, n].rearrange("p k n -> p (k n)") for t in (sg_hi, sg_lo)) + (raw[:],)
            q = 2 * (n - DC)
            return tuple(t[:, q:q + 2, :].rearrange("p q n -> p (q n)") for t in (sd_hi, sd_lo)) + (raw[:, 0:2 * D],)

        @block.sync
        def _(sp):
            opened(sp, *xt_st, *yg_st, x1_st, by=16)
            for dst, src in ((it_in[0:SEQ, :], itok0[0:1, :].partition_broadcast(SEQ)),
                             (it_in[SEQ:P, :], itok0[1:2, :].partition_broadcast(SEQ)),
                             (it1_in[0:SEQ, :], itok1[0:1, :].partition_broadcast(SEQ)),
                             (it1_in[SEQ:P, :], itok1[1:2, :].partition_broadcast(SEQ)),
                             (ra_raw[:], router0.rearrange("(c p) n -> p c n", p=P)),
                             (rb_rows[:], router0_b[0:1, :].partition_broadcast(P)),
                             (b2_rows[:], b2[0:1, :].partition_broadcast(P)),
                             (b2s_raw[:], b2s),
                             (a2_raw[:], a2.rearrange("(t p) n -> p t n", p=P))):
                sp.dma_start(dst, src).then_inc(small_in, 16)
            with sp.Fori(0, NS // 2) as s2:
                for u in range(2):
                    s = s2 * 2 + u
                    sp.wait_ge(cond_done, 1 + s * DC)
                    sp.dma_start(x_in[:], x[bass.ds(s * SUP, SUP), :].rearrange("(j p) n -> p j n", p=P))\
                        .then_inc(x_in_s, 16)
                    sp.wait_ge(xt_lo_done, 4 + (s + 1) * DC)
                    sp.dma_start(xt_hi_d[bass.ds(s, 1)].rearrange("a p n -> p (a n)"),
                                 xt_hi[u][:].rearrange("p c n -> p (c n)").bitcast(F32)).then_inc(xt_st[u], 16)
                    sp.dma_start(xt_lo_d[bass.ds(s, 1)].rearrange("a p n -> p (a n)"),
                                 xt_lo[u][:].rearrange("p c n -> p (c n)").bitcast(F32)).then_inc(xt_st[u], 16)
            sp.wait_ge(wt_sb, 1)
            sp.dma_start(wrow_d, w01_t[:]).then_inc(wrow_st, 16)
            sp.wait_ge(wrow_st, 16)

            def load_super(s, v):
                sl = s % NS
                sp.dma_start(xt_hi[v][:].rearrange("p c n -> p (c n)").bitcast(F32),
                             xt_hi_d[bass.ds(sl, 1)].rearrange("a p n -> p (a n)")).then_inc(xt_in[v], 16)
                sp.dma_start(xt_lo[v][:].rearrange("p c n -> p (c n)").bitcast(F32),
                             xt_lo_d[bass.ds(sl, 1)].rearrange("a p n -> p (a n)")).then_inc(xt_in[v], 16)
                for k in range(2):
                    sp.dma_start(wb[:, v, k, :],
                                 wrow_d[bass.ds(k * J + sl * TPS, TPS), :].rearrange("(o j) p -> o (j p)", o=1)
                                 .partition_broadcast(P)).then_inc(wb_in[v], 16)

            def load_w1(i, f, u):
                sp.wait_ge(w1_lo_done, i + 1)
                sp.dma_start(w_raw[u][:],
                             w1b[bass.ds(f, 1)].rearrange("a p n -> p (a n)")).then_inc(w1_in[u], 16)

            for u in range(2):
                sp.wait_ge(xt_st[u], 16 + 2 * 16 * (NS // 2))
            sp.wait_ge(w2_lo_done, FT)
            sp.wait_ge(zt_read, 2 * NS + 1)
            load_w1(0, 0, 0)
            load_w1(1, 1, 1)
            load_super(0, 0)
            with sp.Fori(0, NS // 2) as s2:
                for v in range(2):
                    s = s2 * 2 + v
                    for u in range(2):
                        load_w1(s * FT + 2 + u, 2 + u, u)
                    sp.wait_ge(g_done, 2 + s * FT)
                    load_super(s + 1, 1 - v)
                    sp.wait_ge(x1_st, 16 + 16 * s)
                    sp.dma_start(xres[:], x[bass.ds(s * SUP, SUP), :].rearrange("(j p) n -> p j n", p=P))\
                        .then_inc(xres_in, 16)
                    with sp.Fori(1, FT // 2) as m:
                        for u in range(2):
                            load_w1(s * FT + m * 2 + 2 + u, (m * 2 + 2 + u) % FT, u)
                    sp.wait_ge(y_read, 1 + s + 1)
                    sp.dma_start(x1_d[bass.ds(s * SUP, SUP), :].rearrange("(j p) n -> p j n", p=P), xres[:])\
                        .then_inc(x1_st, 16)
            sp.wait_ge(x1_st, 16 + 16 * NS)
            for v in range(2):
                sp.wait_ge(xt_in[v], 32 * (NS // 2 + (v == 0)))
                sp.wait_ge(wb_in[v], 32 * (NS // 2 + (v == 0)))
                sp.wait_ge(w1_in[v], 16 * (STEPS // 2 + 1))
            if debug == "x1":
                return
            through(sp, l0_over, 5)

            sp.dma_start(gate_raw[:], gate1.rearrange("(c p) n -> p c n", p=P)).then_inc(gate_in, 16)
            for s in range(NS):
                sp.dma_start(acc[:, s * TPS:(s + 1) * TPS, :],
                             x1_d[s * SUP:(s + 1) * SUP, :].rearrange("(j p) n -> p j n", p=P)).then_inc(acc_in, 16)
            sp.wait_ge(slot_zero, 2)
            sp.dma_start(slot_d.rearrange("(t p) o -> t (p o)", p=P), zero_i[:]).then_inc(slot_z_st, 16)
            with sp.Fori(0, NS // 2) as s2:
                for u in range(2):
                    s = s2 * 2 + u
                    sp.wait_ge(xc_done, (s + 1) * TPS)
                    sp.dma_start(xc_d[bass.ds(s * SUP, SUP), :].rearrange("(j p) n -> p j n", p=P), xc[:])\
                        .then_inc(xc_st, 16)
                    sp.wait_ge(xs_lo_done, (s + 1) * DC)
                    for half, dst in ((xs_hi, xt_hi_d), (xs_lo, xt_lo_d)):
                        sp.dma_start(dst[bass.ds(s, 1)].rearrange("a p n -> p (a n)"),
                                     half[u][:].rearrange("p c n -> p (c n)").bitcast(F32)).then_inc(xs_st[u], 16)
            sp.wait_ge(xc_st, 16 * NS)
            sp.wait_ge(slot_st, 16 * 2 * J)
            sp.dma_start(slot_i[:], slot_d.rearrange("(t p) o -> t (p o)", p=P)).then_inc(slot_in, 16)
            with sp.Fori(0, NS // 2) as s2:
                for u in range(2):
                    s = s2 * 2 + u
                    sp.wait_ge(xs_st[u], 32 * (NS // 2))
                    sp.wait_ge(gu_done, 1 + s2 * 2 * SH + (u * SH - SH if u else 0))
                    for half, src in ((xs_hi, xt_hi_d), (xs_lo, xt_lo_d)):
                        sp.dma_start(half[u][:].rearrange("p c n -> p (c n)").bitcast(F32),
                                     src[bass.ds(s, 1)].rearrange("a p n -> p (a n)")).then_inc(xs_in[u], 16)
            through(sp, sh_over, 5)
            for e in range(E):
                sp.dma_start(wgu[:, e], wgu1[e].rearrange("(c p) n -> p c n", p=P)).then_inc(we_in[e], 16)
                full = (H1 // P) * P
                sp.dma_start(wdn[:, e, 0:H1 // P, :],
                             wdn1[e, 0:full, :].rearrange("(c p) n -> p c n", p=P)).then_inc(we_in[e], 16)
                sp.dma_start(wdn[0:H1 - full, e, H1 // P, :], wdn1[e, full:H1, :]).then_inc(we_in[e], 16)

            def store_y(t, u):
                sp.wait_ge(ry_cp, 1 + t + 1)
                sp.dma_start(yg_d[bass.ds(t * P, P), :], yt[u][:]).then_inc(yg_st[u], 16)
            with sp.Fori(0, SLOT_TILES // 2) as m:
                for u in range(2):
                    store_y(m * 2 + u, u)
            store_y(SLOT_TILES - 1, 0)
            for j in range(J):
                sp.wait_ge(yk_done, 2 * (j + 1))
                sp.dma_start(out[j * P:(j + 1) * P, :], acc[:, j, :]).then_inc(out_st, 16)
            sp.wait_ge(out_st, 16 * J)

        @block.gpsimd
        def _(pool):
            pool.sem_inc(w1_lo_done, 2)
            nc.gpsimd.memset(ident[:], 0.0).then_inc(const_set, 1)
            nc.gpsimd.iota(pos64[:], pattern=[[0, 1]], base=0, channel_multiplier=1).then_inc(const_set, 1)
            nc.gpsimd.iota(rev8[:], pattern=[[-1, E]], base=E, channel_multiplier=0,
                           allow_small_or_imprecise_dtypes=True).then_inc(const_set, 1)
            nc.gpsimd.memset(zero16[:], 0.0).then_inc(const_set, 1)
            nc.gpsimd.memset(ones16[:], 1.0).then_inc(const_set, 1)
            nc.gpsimd.iota(tok_id[:], pattern=[[P, J]], base=0, channel_multiplier=1).then_inc(const_set, 1)
            pool.wait_ge(const_set, 6)
            nc.gpsimd.affine_select(out=tri[:], in_=ones16[:], compare_op=ALU.is_gt, fill=0.0,
                                    base=0, pattern=[[1, P]], channel_multiplier=-1).then_inc(const_set, 1)
            nc.gpsimd.affine_select(out=ident[:], in_=ident[:], compare_op=ALU.not_equal, fill=1.0,
                                    base=0, pattern=[[-1, P]], channel_multiplier=1).then_inc(const_set, 1)
            pool.wait_ge(idx_done, 3)
            for j in range(J):
                pool.indirect_dma_start(out=cw[:, j, :], out_offset=None, in_=cond0,
                                        in_offset=bass.IndirectOffsetOnAxis(ap=it_ix[:, j:j + 1], axis=0))\
                    .then_inc(cw_in, 16)

            def load_w2(f, u):
                pool.dma_start(w_raw[u][:, 0:D],
                               w2[bass.ds(f * P, P), :]).then_inc(w2_in[u], 16)

            def low_w2(f, u):
                pool.wait_ge(w2_hi_done, f + 1)
                nc.gpsimd.tensor_tensor(w2_lo[:, bass.ds(f, 1), :].rearrange("p a n -> p (a n)"),
                                        w_raw[u][:, 0:D],
                                        w2_hi[:, bass.ds(f, 1), :].rearrange("p a n -> p (a n)").bitcast(F32),
                                        ALU.subtract).then_inc(w2_lo_done, 1)
            load_w2(0, 0)
            load_w2(1, 1)
            with pool.Fori(0, FT // 2 - 1) as m:
                for u in range(2):
                    f = m * 2 + u
                    low_w2(f, u)
                    pool.wait_ge(w2_lo_done, f + 1)
                    load_w2(f + 2, u)
            low_w2(FT - 2, 0)
            low_w2(FT - 1, 1)
            def low_w1(i, u):
                    pool.wait_ge(w1_hi_done, i + 1)
                    nc.gpsimd.tensor_tensor(w_lo[u][:].rearrange("p c n -> p (c n)"), w_raw[u][:, 0:WT],
                                            w_hi[u][:].rearrange("p c n -> p (c n)").bitcast(F32), ALU.subtract)\
                        .then_inc(w1_lo_done, 1)

            pool.wait_ge(it1_done, 1)
            for j in range(J):
                low_w1(j, j % 2)
                at = bass.IndirectOffsetOnAxis(ap=it1_ix[:, j:j + 1], axis=0)
                pool.indirect_dma_start(out=cw1[:, j, :], out_offset=None, in_=cond1, in_offset=at)\
                    .then_inc(cw1_in, 16)
                pool.indirect_dma_start(out=side_col[:, j:j + 1], out_offset=None, in_=side, in_offset=at)\
                    .then_inc(cw1_in, 16)
            with pool.Fori(J // 2, STEPS // 2 + 1) as m:
                for u in range(2):
                    low_w1(m * 2 + u, u)
            if debug == "x1":
                return
            through(pool, l0_over, 5)

            nc.gpsimd.memset(zero_i[:], 0).then_inc(slot_zero, 1)
            nc.gpsimd.iota(etile[:], pattern=[[1, ETAB]], base=0, channel_multiplier=0,
                           allow_small_or_imprecise_dtypes=True).then_inc(slot_zero, 1)
            for u in range(2):
                nc.gpsimd.memset(s_raw[u][:], 0.0).then_inc(pad_done, 1)
            pool.wait_ge(pad_done, 2)

            def load_s(n):
                u = n % 2
                if n < DC:
                    for k in range(2):
                        pool.dma_start(s_raw[u][:, k * SH * P:k * SH * P + HP],
                                       sgu1[n * P:(n + 1) * P, k * HP:(k + 1) * HP]).then_inc(s_in[u], 16)
                else:
                    q = 2 * (n - DC)
                    rows = min(HP - (q + 1) * P, P)
                    pool.dma_start(s_raw[u][:, 0:D], sdn1[q * P:(q + 1) * P, :]).then_inc(s_in[u], 16)
                    pool.dma_start(s_raw[u][0:rows, D:2 * D], sdn1[(q + 1) * P:(q + 1) * P + rows, :])\
                        .then_inc(s_in[u], 16)
            load_s(0)
            load_s(1)
            for n in range(DC + SH // 2):
                u = n % 2
                pool.wait_ge(s_hi_done, n + 1)
                hi, lo, raw = shared_halves(n)
                nc.gpsimd.tensor_tensor(lo, raw, hi.bitcast(F32), ALU.subtract).then_inc(s_lo_done, 1)
                pool.wait_ge(s_lo_done, n + 1)
                if n + 2 == DC + SH // 2 - 1:
                    nc.gpsimd.memset(s_raw[u][:], 0.0).then_inc(pad_done, 1)
                    pool.wait_ge(pad_done, 3)
                if n + 2 < DC + SH // 2:
                    load_s(n + 2)
            pool.wait_ge(slot_z_st, 16)
            pool.wait_ge(pos_ok, 1)
            for k in range(2):
                for j in range(J):
                    pool.indirect_dma_start(out=slot_d, in_=tok_id[:, j:j + 1], in_offset=None,
                                            out_offset=bass.IndirectOffsetOnAxis(ap=pos_i[:, k, j:j + 1], axis=0))\
                        .then_inc(slot_st, 16)
            through(pool, sh_over, 5)

            pool.wait_ge(xc_st, 16 * NS)
            pool.wait_ge(slot_ok, 1)
            for t in range(SLOT_TILES):
                pool.wait_ge(xgt_done, t)
                pool.indirect_dma_start(out=xg[t % 2][:], out_offset=None, in_=xc_d,
                                        in_offset=bass.IndirectOffsetOnAxis(ap=slot_tok[:, t:t + 1], axis=0))\
                    .then_inc(xg_in[t % 2], 16)
            for u in range(2):
                pool.wait_ge(yg_st[u], 16 + 16 * ((SLOT_TILES + 1 - u) // 2))
            for j in range(J):
                u = j % 4
                if j >= 4:
                    pool.wait_ge(yk_done, 2 * (j - 3))
                for k in range(2):
                    pool.indirect_dma_start(out=yk[k][u][:], out_offset=None, in_=yg_d,
                                            in_offset=bass.IndirectOffsetOnAxis(ap=pos_i[:, k, j:j + 1], axis=0))\
                        .then_inc(yk_in[u], 16)

        @block.scalar
        def _(act):
            act.sem_inc(h1_done, 2)
            opened(act, z2_cp, xgt_cp)
            def high_w2(f, u, n):
                act.wait_ge(w2_in[u], n)
                nc.scalar.copy(w2_hi[:, bass.ds(f, 1), :].rearrange("p a n -> p (a n)"),
                               w_raw[u][:, 0:D]).then_inc(w2_hi_done, 1)
            with act.Fori(0, NS // 2) as s2:
                for u in range(2):
                    s = s2 * 2 + u
                    act.wait_ge(xt_st[u], 16 + s2 * 32)
                    for c in range(DC):
                        act.wait_ge(cond_done, 1 + s * DC + c + 1)
                        nc.scalar.copy(xt_hi[u][:, c, :], ps_y[:, c, :]).then_inc(xt_hi_done, 1)
                    for q in range(FT // NS):
                        high_w2(s * (FT // NS) + q, q % 2, (s * (FT // NS) + (q // 2) * 2 + 2) * 8)
            act.wait_ge(r_max, 1)
            nc.scalar.activation(rt["q"][:], rt["l"][:], ACT.Exp).then_inc(r_exp, 1)

            def high_w1(i, u, n):
                act.wait_ge(w1_in[u], n)
                act.wait_ge(z_done, i + 1)
                act.wait_ge(h1_done, i + 1)
                nc.scalar.copy(bias1[u][:], w_raw[u][:, WT:WT + 1])
                nc.scalar.copy(w_hi[u][:].rearrange("p c n -> p (c n)"), w_raw[u][:, 0:WT]).then_inc(w1_hi_done, 1)

            for n in range(2 * NS):
                dst = (z_base, z_step)[n // NS]
                s = n % NS
                act.wait_ge(zt_done, n + 1)
                if n >= NS:
                    act.wait_ge(w01_ok, 2 * NS + 1)
                nc.scalar.copy(dst[:, s * SUP:(s + 1) * SUP],
                               ps_y[:, n % TPS, :]).then_inc(zt_read, 1)
            act.wait_ge(zt_done, 2 * NS + 1)
            nc.scalar.copy(w01_t[:], ps_t[0:2 * J, 0, :]).then_inc(zt_read, 1)
            act.wait_ge(zt_read, 2 * NS + 1)
            act.sem_inc(wt_sb, 1)
            high_w1(0, 0, 16)
            high_w1(1, 1, 16)
            with act.Fori(0, NS) as s:
                with act.Fori(0, FT // 2) as m:
                    for u in range(2):
                        i = s * FT + m * 2 + u
                        b = bias1[u][:, 0:1]
                        act.wait_ge(a_done, i + 1)
                        act.wait_ge(g_done, i + 1)
                        nc.scalar.activation(h0[u][:], ps_h[:, u, :], ACT.Gelu_apprx_tanh, bias=b)\
                            .then_inc(h0_done, 1)
                        act.wait_ge(z_done, i + 3)
                        nc.scalar.activation(h1[u][:], ps_h[:, u, :], ACT.Gelu_apprx_tanh, bias=b)\
                            .then_inc(h1_done, 1)
                        high_w1(i + 2, u, (s * (FT // 2) + m + 2) * 16)
                act.wait_ge(z2_t, 1 + s + 1)
                nc.scalar.copy(z2t[:], ps_t[:]).then_inc(z2_cp, 1)
            if debug == "x1":
                return
            act.sem_inc(xgt_done, 1)
            through(act, l0_over, 5)

            def high_s(n):
                u = n % 2
                act.wait_ge(s_in[u], 32 * (n // 2 + 1))
                act.wait_ge(pad_done, 3 if n == DC + SH // 2 - 1 else 2)
                hi, lo, raw = shared_halves(n)
                nc.scalar.copy(hi, raw).then_inc(s_hi_done, 1)
            for s in range(NS):
                for c in range(DC):
                    act.wait_ge(xt1_done, s * DC + c + 1)
                    if s >= 2:
                        act.wait_ge(xs_st[s % 2], 32 * (s // 2))
                    nc.scalar.copy(xs_hi[s % 2][:, c, :], ps_h[:, c % 2, :]).then_inc(xs_hi_done, 1)
                for n in range(max(2 * s - 1, 0), 2 * s + 1):
                    high_s(n)
            act.wait_ge(r1_max, 1)
            nc.scalar.activation(q1["q"][:], q1["l"][:], ACT.Exp).then_inc(r1_exp, 1)
            with act.Fori(0, NS) as s:
                for q in range(SH):
                    i = s * SH + q
                    act.wait_ge(mul_done, 1 + i)
                    act.wait_ge(gu_done, 1 + i + 1)
                    nc.scalar.activation(sh_s[:], ps_h[:, q % 2, :], ACT.Silu).then_inc(sil_done, 1)
            through(act, sh_over, 5)

            def routed_copies(t, u, first=False):
                act.wait_ge(xgt_done, t + 2)
                nc.scalar.copy(xg_t[u][:], ps_t[:]).then_inc(xgt_cp, 1)
                act.wait_ge(rg_done, 1 + t)
                act.wait_ge(rgu_done, t + 1)
                nc.scalar.activation(rs[:], ps_h[:, 0, 0:H1], ACT.Silu).then_inc(rs_done, 1)
            with act.Fori(0, SLOT_TILES // 2) as m:
                for u in range(2):
                    routed_copies(m * 2 + u, u)
            routed_copies(SLOT_TILES - 1, 0)

        @block.vector
        def _(dve):
            dve.sem_inc(xt_lo_done, 4)
            dve.sem_inc(lu_done, 1)
            dve.sem_inc(g_done, 2)
            opened(dve, y_read, mul_done, rg_done, slo_done, sy_read, rgt_cp, ry_cp)
            nc.vector.memset(bd[:], 0.0).then_inc(bd_zero, 1)
            dve.wait_ge(const_set, 8)
            dve.wait_ge(small_in, 16 * 9)
            nc.vector.tensor_copy(posf[:], pos64[:]).then_inc(idx_done, 1)
            dve.wait_ge(idx_done, 1)
            nc.vector.tensor_scalar(posf[SEQ:P, :], posf[SEQ:P, :], float(-SEQ), None, ALU.add).then_inc(idx_done, 1)
            dve.wait_ge(idx_done, 2)
            nc.vector.tensor_scalar(it_ix[:], it_in[:], float(SEQ), posf[:, 0:1], ALU.mult, ALU.add)\
                .then_inc(idx_done, 1)
            nc.vector.tensor_scalar(it1_ix[:], it1_in[:], float(SEQ), posf[:, 0:1], ALU.mult, ALU.add)\
                .then_inc(it1_done, 1)
            small = ((ra_hi, ra_lo, ra_raw), (b2s_hi, b2s_lo, b2s_raw), (a2_hi, a2_lo, a2_raw))
            for hi, lo, raw in small:
                nc.vector.tensor_copy(hi[:], raw[:]).then_inc(split_small, 1)
            for n, (hi, lo, raw) in enumerate(small):
                dve.wait_ge(split_small, n + 1)
                nc.vector.tensor_tensor(lo[:], raw[:], hi[:].bitcast(F32), ALU.subtract).then_inc(split_small, 1)
            dve.wait_ge(bd_zero, 1)
            dve.wait_ge(cw_in, 16 * J)
            nc.vector.tensor_copy(bd[0:SEQ, :, 0:SEQ], cw[0:SEQ, :, :]).then_inc(bd_done, 1)
            nc.vector.tensor_copy(bd[SEQ:P, :, SEQ:P], cw[SEQ:P, :, :]).then_inc(bd_done, 1)
            with dve.Fori(0, NS // 2) as s2:
                for u in range(2):
                    s = s2 * 2 + u
                    for c in range(DC):
                        dve.wait_ge(xt_hi_done, s * DC + c + 1)
                        nc.vector.tensor_tensor(xt_lo[u][:, c, :], ps_y[:, c, :], xt_hi[u][:, c, :].bitcast(F32),
                                                ALU.subtract).then_inc(xt_lo_done, 1)
                    dve.wait_ge(lg_done, s + 1)
                    nc.vector.tensor_copy(lu[:, bass.ds(s * TPS, TPS), :],
                                          ps_h[:, 0, 0:TPS * (E + ER)].rearrange("p (j n) -> p j n", j=TPS))\
                        .then_inc(lu_done, 1)

            count = [0]

            def link(ins):
                count[0] += 1
                ins.then_inc(rch, 1)
                dve.wait_ge(rch, count[0])

            def over_e(col):
                return col.unsqueeze(2).to_broadcast([P, J, E])

            tt = nc.vector.tensor_tensor

            def route(rt, rc, logits, bias, oh0, oh1, w_0, w_1, r_max, r_exp):
                l, p, q, m = rt["l"][:], rt["p"][:], rt["q"][:], rc["m"][:]
                if bias is not None:
                    link(tt(p, logits, bias.unsqueeze(1).to_broadcast([P, J, E]), ALU.add))
                else:
                    link(nc.vector.tensor_copy(p, logits))
                link(nc.vector.tensor_reduce(m, p, AX.X, ALU.max))
                tt(l, p, over_e(m), ALU.subtract).then_inc(r_max, 1)
                dve.wait_ge(r_exp, 1)
                link(nc.vector.tensor_reduce(m, q, AX.X, ALU.add))
                link(nc.vector.reciprocal(rc["s"][:], m))
                link(tt(p, q, over_e(rc["s"][:]), ALU.mult))
                rev = rev8[:].unsqueeze(1).to_broadcast([P, J, E])
                for oh, w in ((oh0, w_0), (oh1, w_1)):
                    link(nc.vector.tensor_reduce(w, p, AX.X, ALU.max))
                    link(tt(q, p, over_e(w), ALU.is_equal))
                    link(tt(q, q, rev, ALU.mult))
                    link(nc.vector.tensor_reduce(m, q, AX.X, ALU.max))
                    link(tt(oh, q, over_e(m), ALU.is_equal))
                    if oh is oh0:
                        link(nc.vector.tensor_scalar(q, p, 1.0, None, ALU.add))
                        link(tt(q, q, oh, ALU.mult))
                        link(tt(p, p, q, ALU.subtract))

            dve.wait_ge(lu_done, 1 + NS)
            route(rt, rc, lu[:, :, 0:E], rb_rows[:], rt["oh0"][:], rt["oh1"][:], w01[:, 0, :], w01[:, 1, :],
                  r_max, r_exp)
            tt(wsum[:], w01[:, 0, :], w01[:, 1, :], ALU.add).then_inc(w01_ok, 1)
            link(tt(rt["l"][:], rt["oh1"][:], rt["oh0"][:], ALU.subtract))
            nc.vector.tensor_scalar(rt["ohdx"][:], rt["l"][:], LORA_SCALE, None, ALU.mult)
            link(nc.vector.tensor_scalar(rt["oh0x"][:], rt["oh0"][:], LORA_SCALE, None, ALU.mult))
            u1 = lu[:, :, E:E + ER]
            link(nc.vector.tensor_copy(uhi, u1))
            link(tt(u1, u1, uhi.bitcast(F32), ALU.subtract))
            by_r = lambda ap: ap.rearrange("p j (e r) -> p j e r", r=R)
            for k, mask in ((0, rt["oh0x"]), (1, rt["ohdx"])):
                for j0 in range(0, J, TPS):
                    mk = mask[:, j0:j0 + TPS, :].unsqueeze(3).to_broadcast([P, TPS, E, R])
                    tt(by_r(zc[:, k, j0:j0 + TPS, 0:ER]), by_r(uhi[:, j0:j0 + TPS, :].bitcast(F32)), mk, ALU.mult)
                    tt(by_r(zc[:, k, j0:j0 + TPS, ER:2 * ER]), by_r(u1[:, j0:j0 + TPS, :]), mk, ALU.mult)\
                        .then_inc(w01_ok, 1)

            with dve.Fori(0, NS // 2) as s2:
                for v in range(2):
                    s = s2 * 2 + v
                    with dve.Fori(0, FT // 2) as m:
                        for u in range(2):
                            i = s * FT + m * 2 + u
                            n = i * G_OPS
                            dve.wait_ge(wb_in[v], (s2 + 1) * 32)
                            dve.wait_ge(h0_done, i + 1)
                            tt(h0[u][:], h0[u][:], wb[:, v, 0, :], ALU.mult).then_inc(gch, 1)
                            dve.wait_ge(h1_done, i + 3)
                            tt(h1[u][:], h1[u][:], wb[:, v, 1, :], ALU.mult).then_inc(gch, 1)
                            dve.wait_ge(gch, n + 2)
                            dve.wait_ge(d_done, i + 1)
                            tt(h0[u][:], h0[u][:], h1[u][:], ALU.add).then_inc(gch, 1)
                            nc.vector.tensor_copy(g1_hi[u][:], h1[u][:]).then_inc(gch, 1)
                            dve.wait_ge(gch, n + 3)
                            nc.vector.tensor_copy(g_hi[u][:], h0[u][:]).then_inc(gch, 1)
                            dve.wait_ge(gch, n + 4)
                            tt(g1_lo[u][:], h1[u][:], g1_hi[u][:].bitcast(F32), ALU.subtract).then_inc(gch, 1)
                            dve.wait_ge(gch, n + 5)
                            tt(g_lo[u][:], h0[u][:], g_hi[u][:].bitcast(F32), ALU.subtract).then_inc(g_done, 1)
                    jj = s * TPS
                    dve.wait_ge(xres_in, (s + 1) * 16)
                    for j in range(TPS):
                        last = nc.vector.scalar_tensor_tensor(
                            out=xres[:, j, :], in0=b2_rows[:], scalar=wsum[:, bass.ds(jj + j, 1)],
                            in1=xres[:, j, :], op0=ALU.mult, op1=ALU.add)
                    last.then_inc(xb_done, 1)
                    dve.wait_ge(d_done, 2 + (s + 1) * FT)
                    m0 = rt["oh0x"][:, bass.ds(jj, TPS), :].unsqueeze(3).to_broadcast([P, TPS, E, R])
                    md = rt["ohdx"][:, bass.ds(jj, TPS), :].unsqueeze(3).to_broadcast([P, TPS, E, R])
                    tt(by_r(zz[:]), by_r(ps_u[:, :, 0, :]), m0, ALU.mult).then_inc(ech, 1)
                    tt(by_r(zq[:]), by_r(ps_u[:, :, 1, :]), md, ALU.mult).then_inc(ech, 1)
                    dve.wait_ge(ech, s * 4 + 2)
                    tt(zz[:], zz[:], zq[:], ALU.add).then_inc(ech, 1)
                    dve.wait_ge(ech, s * 4 + 3)
                    dve.wait_ge(z2_t, 1 + s)
                    nc.vector.tensor_copy(z2c[:, :, 0:ER], zz[:]).then_inc(ech, 1)
                    dve.wait_ge(ech, s * 4 + 4)
                    tt(z2c[:, :, ER:2 * ER], zz[:], z2c[:, :, 0:ER].bitcast(F32), ALU.subtract).then_inc(z2_ok, 1)
                    dve.wait_ge(xb_done, s + 1)
                    dve.wait_ge(y_done, s + 1)
                    for j in range(TPS):
                        last = tt(xres[:, j, :], ps_y[:, j, :], xres[:, j, :], ALU.add)
                    last.then_inc(y_read, 1)
            if debug == "x1":
                return
            through(dve, l0_over, 5)

            dve.wait_ge(gate_in, 16)
            nc.vector.tensor_copy(gate_hi[:], gate_raw[:]).then_inc(gate_done, 1)
            dve.wait_ge(gate_done, 1)
            tt(gate_lo[:], gate_raw[:], gate_hi[:].bitcast(F32), ALU.subtract).then_inc(gate_done, 1)
            for u in range(2):
                nc.vector.memset(bdq[u][:], 0.0).then_inc(bdq_zero, 1)
            dve.wait_ge(cw1_in, 16 * 2 * J)
            dve.wait_ge(bdq_zero, 2)

            def diagonals(s):
                u = s % 2
                for h in range(2):
                    rows = slice(h * SEQ, (h + 1) * SEQ)
                    nc.vector.tensor_copy(bdq[u][rows, :, h * SEQ:(h + 1) * SEQ],
                                          cw1[rows, s * TPS:(s + 1) * TPS, :]).then_inc(bdq_done, 1)
            diagonals(0)
            for s in range(NS):
                for j in range(TPS):
                    if s >= 1:
                        dve.wait_ge(xc_st, 16 * s)
                        dve.wait_ge(xt1_done, DC * s)
                    dve.wait_ge(c1_done, s * TPS + j + 1)
                    jj = s * TPS + j
                    nc.vector.tensor_scalar(xc[:, j, :], ps_y[:, j, :], side_col[:, jj:jj + 1], None, ALU.add)\
                        .then_inc(xc_done, 1)
                if s + 1 < NS:
                    diagonals(s + 1)
                for c in range(DC):
                    dve.wait_ge(xs_hi_done, s * DC + c + 1)
                    tt(xs_lo[s % 2][:, c, :], ps_h[:, c % 2, :], xs_hi[s % 2][:, c, :].bitcast(F32),
                       ALU.subtract).then_inc(xs_lo_done, 1)
                dve.wait_ge(lg1_done, s + 1)
                nc.vector.tensor_copy(lg1[:, s * TPS:(s + 1) * TPS, :],
                                      ps_t[:, 0, 0:TPS * E].rearrange("p (j e) -> p j e", e=E)).then_inc(lg1_read, 1)
            dve.wait_ge(lg1_read, NS)
            oh0, oh1 = q1["oh0"][:], q1["oh1"][:]
            route(q1, c1, lg1[:], None, oh0, oh1, w1k[:, 0, :], w1k[:, 1, :], r1_max, r1_exp)
            tt(mask16[:], oh0, oh1, ALU.add).then_inc(mask_ok, 1)
            dve.wait_ge(cnt_done, 1)
            tot = ps_t[:, 1, :].rearrange("p (j e) -> p j e", e=E)
            link(nc.vector.tensor_copy(rank[:], ps_t[:, 0, :].rearrange("p (j e) -> p j e", e=E)))
            link(nc.vector.tensor_copy(cnt[0][:], tot))
            a, b = 0, 1
            d = 1
            while d < J:
                nc.vector.tensor_copy(cnt[b][:, 0:d, :], cnt[a][:, 0:d, :])
                link(tt(cnt[b][:, d:J, :], cnt[a][:, d:J, :], cnt[a][:, 0:J - d, :], ALU.add))
                a, b, d = b, a, 2 * d
            ca = cnt[a]
            link(nc.vector.tensor_scalar(ex_i[:], ca[:, J - 1, :], float(P - 1), None, ALU.add))
            link(nc.vector.tensor_single_scalar(ex_i[:], ex_i[:], 7, ALU.logical_shift_right))
            link(nc.vector.tensor_copy(ex["t"][:], ex_i[:]))
            link(nc.vector.tensor_copy(ex["a"][:], ex["t"][:]))
            xa, xb_, d = ex["a"], ex["b"], 1
            while d < E:
                nc.vector.tensor_copy(xb_[:, 0:d], xa[:, 0:d])
                link(tt(xb_[:, d:E], xa[:, d:E], xa[:, 0:E - d], ALU.add))
                xa, xb_, d = xb_, xa, 2 * d
            dve.wait_ge(slot_zero, 2)
            link(tt(etab3[:], etile[:].unsqueeze(2).to_broadcast([P, ETAB, E]),
                    xa[:].unsqueeze(1).to_broadcast([P, ETAB, E]), ALU.is_ge))
            link(nc.vector.tensor_reduce(etab_f[:], etab3[:], AX.X, ALU.add))
            nc.vector.tensor_scalar(etab[:], etab_f[:], float(E - 1), None, ALU.min).then_inc(etab_ok, 1)
            link(tt(xb_[:], xa[:], ex["t"][:], ALU.subtract))
            link(nc.vector.tensor_scalar(xb_[:], xb_[:], float(P), None, ALU.mult))
            link(tt(ca[:], ca[:], tot, ALU.subtract))
            link(tt(ca[:], ca[:], rank[:], ALU.add))
            link(tt(ca[:], ca[:], xb_[:].unsqueeze(1).to_broadcast([P, J, E]), ALU.add))
            for k, oh in ((0, oh0), (1, oh1)):
                link(tt(rank[:], ca[:], oh, ALU.mult))
                last = nc.vector.tensor_reduce(c1["m" if k else "s"][:], rank[:], AX.X, ALU.add)
                link(last)
                link(nc.vector.tensor_copy(pos_i[:, k, :], c1["m" if k else "s"][:]))
            nc.vector.tensor_copy(rank[:, 0, :], ca[:, 0, :]).then_inc(pos_ok, 1)

            with dve.Fori(0, NS) as s:
                for q in range(SH):
                    i = s * SH + q
                    dve.wait_ge(sil_done, i + 1)
                    dve.wait_ge(slo_done, 1 + i)
                    tt(sh_g[:], sh_s[:], ps_y[:, q % 2, :], ALU.mult).then_inc(mul_done, 1)
                    dve.wait_ge(mul_done, 1 + i + 1)
                    dve.wait_ge(sy_done, 1 + s * TPS)
                    nc.vector.tensor_copy(sh_hi[:, q, :], sh_g[:]).then_inc(shi_done, 1)
                    dve.wait_ge(shi_done, i + 1)
                    tt(sh_lo[:, q, :], sh_g[:], sh_hi[:, q, :].bitcast(F32), ALU.subtract).then_inc(slo_done, 1)
                dve.wait_ge(acc_in, 16 * NS)
                for j in range(TPS):
                    dve.wait_ge(sy_done, 1 + s * TPS + j + 1)
                    a = acc[:, bass.ds(s * TPS + j, 1), :].rearrange("p a n -> p (a n)")
                    tt(a, ps_y[:, 2 + j % 2, :], a, ALU.add).then_inc(sy_read, 1)
            dve.wait_ge(slot_in, 16)
            nc.vector.tensor_copy(slot_f[:], slot_i[:]).then_inc(slot_cv, 1)
            dve.wait_ge(slot_tr, 1)
            nc.vector.tensor_copy(slot_tok[:], ps_u[:, 0, 0, 0:ETAB]).then_inc(slot_ok, 1)
            through(dve, sh_over, 5)

            def routed_products(t, u):
                dve.wait_ge(rs_done, t + 1)
                dve.wait_ge(rgt_done, 1 + t)
                tt(rg[:], rs[:], ps_h[:, 1, 0:H1], ALU.mult).then_inc(rg_done, 1)
                dve.wait_ge(rgt_done, 1 + t + 1)
                dve.wait_ge(ry_done, 1 + t)
                nc.vector.tensor_copy(rg_t[:, 0:HC - 1, :], ps_y[:, 0, 0:(HC - 1) * P].rearrange("p (c n) -> p c n", n=P))
                nc.vector.tensor_copy(rg_t[0:H1 - (HC - 1) * P, HC - 1, :],
                                      ps_y[0:H1 - (HC - 1) * P, 0, (HC - 1) * P:HC * P]).then_inc(rgt_cp, 1)
                dve.wait_ge(ry_done, 1 + t + 1)
                return
            def routed_out(t, u, n):
                dve.wait_ge(yg_st[u], 16 + n)
                nc.vector.tensor_copy(yt[u][:], ps_y[:, 1, :]).then_inc(ry_cp, 1)
            with dve.Fori(0, SLOT_TILES // 2) as m:
                for u in range(2):
                    routed_products(m * 2 + u, u)
                    routed_out(m * 2 + u, u, m * 16)
            routed_products(SLOT_TILES - 1, 0)
            routed_out(SLOT_TILES - 1, 0, (SLOT_TILES // 2) * 16)
            for j in range(J):
                u = j % 4
                dve.wait_ge(yk_in[u], 32 * (j // 4 + 1))
                for k in range(2):
                    dve.wait_ge(yk_done, 2 * j + k)
                    nc.vector.scalar_tensor_tensor(out=acc[:, j, :], in0=yk[k][u][:], scalar=w1k[:, k, j:j + 1],
                                                   in1=acc[:, j, :], op0=ALU.mult, op1=ALU.add).then_inc(yk_done, 1)

        @block.tensor
        def _(pe):
            mm = nc.tensor.matmul
            pe.sem_inc(z_done, 2)
            pe.sem_inc(d_done, 2)
            opened(pe, cond_done, z2_t, gu_done, sy_done, rgt_done, ry_done)
            pe.wait_ge(bd_done, 2)
            pe.wait_ge(split_small, 6)
            with pe.Fori(0, NS // 2) as s2:
                for u in range(2):
                    s = s2 * 2 + u
                    pe.wait_ge(x_in_s, (s + 1) * 16)
                    for c in range(DC):
                        pe.wait_ge(xt_lo_done, s * DC + c + 1)
                        for j in range(TPS):
                            last = mm(ps_y[:, c, j * P:(j + 1) * P], x_in[:, j, c * P:(c + 1) * P],
                                      bd[:, bass.ds(s * TPS + j, 1), :].rearrange("p a n -> p (a n)"),
                                      start=True, stop=True)
                        last.then_inc(cond_done, 1)
                    pe.wait_ge(xt_lo_done, 4 + (s + 1) * DC)
                    pe.wait_ge(lu_done, s + 1)
                    for j in range(TPS):
                        o = ps_h[:, 0, j * (E + ER):(j + 1) * (E + ER)]
                        for c in range(DC):
                            a, b = xt_hi[u][:, c, j * P:(j + 1) * P], xt_lo[u][:, c, j * P:(j + 1) * P]
                            mm(o, a, ra_hi[:, c, :], start=(c == 0), stop=False)
                            mm(o, a, ra_lo[:, c, :], start=False, stop=False)
                            last = mm(o, b, ra_hi[:, c, :], start=False, stop=(c == DC - 1))
                    last.then_inc(lg_done, 1)
            for n in range(2 * NS):
                k, s = n // NS, n % NS
                pe.wait_ge(w01_ok, n + 2)
                if n >= TPS:
                    pe.wait_ge(zt_read, n - TPS + 1)
                for j in range(TPS):
                    last = nc.tensor.transpose(ps_y[:, n % TPS, j * P:(j + 1) * P],
                                               zc[:, k, s * TPS + j, :].bitcast(F32), ident[:])
                last.then_inc(zt_done, 1)
            nc.tensor.transpose(ps_t[0:2 * J, 0, :], w01[:].rearrange("p k j -> p (k j)"), ident[:])\
                .then_inc(zt_done, 1)

            def hidden(i, s, v, u):
                pe.wait_ge(w1_lo_done, i + 3)
                pe.wait_ge(h1_done, i + 1)
                for c in range(DC):
                    mm(ps_h[:, u, :], w_hi[u][:, c, :], xt_hi[v][:, c, :], start=(c == 0), stop=False)
                    mm(ps_h[:, u, :], w_hi[u][:, c, :], xt_lo[v][:, c, :], start=False, stop=False)
                    mm(ps_h[:, u, :], w_lo[u][:, c, :], xt_hi[v][:, c, :], start=False, stop=False)
                zb = z_base[:, bass.ds(s * SUP, SUP)]
                mm(ps_h[:, u, :], w_hi[u][:, DC, :], zb, start=False, stop=False)
                mm(ps_h[:, u, :], w_lo[u][:, DC, :], zb, start=False, stop=True).then_inc(a_done, 1)

            def second(i, s, u):
                pe.wait_ge(h0_done, i + 1)
                zs = z_step[:, bass.ds(s * SUP, SUP)]
                mm(ps_h[:, u, :], w_hi[u][:, DC, :], zs, start=False, stop=False, skip_group_check=True)
                mm(ps_h[:, u, :], w_lo[u][:, DC, :], zs, start=False, stop=True, skip_group_check=True)\
                    .then_inc(z_done, 1)

            def down(i, f, u, half):
                if half == 0:
                    pe.wait_ge(g_done, i + 3)
                kw = dict(start=False, stop=False, skip_group_check=True)
                sl = lambda t: t[:, bass.ds(f, 1), :].rearrange("p a n -> p (a n)")
                for j in range(half * 2, half * 2 + 2):
                    cols = slice(j * P, (j + 1) * P)
                    mm(ps_y[:, j, :], g_hi[u][:, cols], sl(w2_hi), **kw)
                    mm(ps_y[:, j, :], g_hi[u][:, cols], sl(w2_lo), **kw)
                    mm(ps_u[:, j, 0, :], g_hi[u][:, cols], sl(a2_hi), **kw)
                    mm(ps_u[:, j, 0, :], g_hi[u][:, cols], sl(a2_lo), **kw)
                    mm(ps_y[:, j, :], g_lo[u][:, cols], sl(w2_hi), **kw)
                    mm(ps_u[:, j, 0, :], g_lo[u][:, cols], sl(a2_hi), **kw)
                    mm(ps_u[:, j, 1, :], g1_hi[u][:, cols], sl(a2_hi), **kw)
                    mm(ps_u[:, j, 1, :], g1_hi[u][:, cols], sl(a2_lo), **kw)
                    last = mm(ps_u[:, j, 1, :], g1_lo[u][:, cols], sl(a2_hi), **kw)
                if half == 1:
                    last.then_inc(d_done, 1)

            def zero_sums(s):
                pe.wait_ge(y_read, 1 + s)
                for j in range(TPS):
                    mm(ps_y[:, j, :], zero16[:, 0:P], zero16[:], start=True, stop=False, skip_group_check=True)
                mm(ps_u[:].rearrange("p j k n -> p (j k n)"), zero16[:, 0:P], zero16[:], start=True, stop=False,
                   skip_group_check=True)

            def step(i, s, v, f, u):
                hidden(i, s, v, u)
                down(i - 1, f - 1, 1 - u, 0)
                second(i, s, u)
                down(i - 1, f - 1, 1 - u, 1)

            def super_tile(s, s2, v, nxt):
                base = s * FT
                hidden(base + 1, s, v, 1)
                second(base, s, 0)
                zero_sums(s)
                down(base, 0, 0, 0)
                second(base + 1, s, 1)
                down(base, 0, 0, 1)
                with pe.Fori(1, FT // 2) as m:
                    for u in range(2):
                        step(base + m * 2 + u, s, v, m * 2 + u, u)
                if nxt is not None:
                    pe.wait_ge(xt_in[1 - v], nxt)
                    hidden(base + FT, s + 1, 1 - v, 0)
                down(base + FT - 1, FT - 1, 1, 0)
                down(base + FT - 1, FT - 1, 1, 1)
                pe.wait_ge(z2_ok, s + 1)
                pe.wait_ge(z2_cp, 1 + s)
                for j in range(TPS):
                    last = nc.tensor.transpose(ps_t[:, j, :], z2c[:, j, :].bitcast(F32), ident[:])
                last.then_inc(z2_t, 1)
                pe.wait_ge(z2_cp, 1 + s + 1)
                for j in range(TPS):
                    mm(ps_y[:, j, :], z2t[:, j, :], b2s_hi[:], start=False, stop=False, skip_group_check=True)
                    last = mm(ps_y[:, j, :], z2t[:, j, :], b2s_lo[:], start=False, stop=True, skip_group_check=True)
                last.then_inc(y_done, 1)

            pe.wait_ge(zt_read, 2 * NS + 1)
            pe.wait_ge(xt_in[0], 32)
            hidden(0, 0, 0, 0)
            with pe.Fori(0, NS // 2 - 1) as s2:
                super_tile(s2 * 2, s2, 0, s2 * 32 + 32)
                super_tile(s2 * 2 + 1, s2, 1, s2 * 32 + 64)
            super_tile(NS - 2, NS // 2 - 1, 0, 16 * NS)
            super_tile(NS - 1, NS // 2 - 1, 1, None)
            if debug == "x1":
                return
            through(pe, l0_over, 5)

            pe.wait_ge(gate_done, 2)
            for s in range(NS):
                u = s % 2
                pe.wait_ge(acc_in, 16 * NS)
                pe.wait_ge(bdq_done, 2 * (s + 1))
                for j in range(TPS):
                    if s >= 1:
                        pe.wait_ge(xc_done, (s - 1) * TPS + j + 1)
                    mm(ps_y[:, j, :], bdq[u][:, j, :], acc[:, s * TPS + j, :], start=True, stop=True)\
                        .then_inc(c1_done, 1)
                pe.wait_ge(xc_done, (s + 1) * TPS)
                for c in range(DC):
                    if s * DC + c >= 2:
                        pe.wait_ge(xs_lo_done, s * DC + c - 1)
                    for j in range(TPS):
                        last = nc.tensor.transpose(ps_h[:, c % 2, j * P:(j + 1) * P],
                                                   xc[:, j, c * P:(c + 1) * P], ident[:])
                    last.then_inc(xt1_done, 1)
                pe.wait_ge(xs_lo_done, (s + 1) * DC)
                if s >= 1:
                    pe.wait_ge(lg1_read, s)
                for j in range(TPS):
                    o = ps_t[:, 0, j * E:(j + 1) * E]
                    for c in range(DC):
                        a, b = xs_hi[u][:, c, j * P:(j + 1) * P], xs_lo[u][:, c, j * P:(j + 1) * P]
                        mm(o, a, gate_hi[:, c, :], start=(c == 0), stop=False)
                        mm(o, a, gate_lo[:, c, :], start=False, stop=False)
                        last = mm(o, b, gate_hi[:, c, :], start=False, stop=(c == DC - 1))
                last.then_inc(lg1_done, 1)
            pe.wait_ge(mask_ok, 1)
            mask_row = mask16[:].rearrange("p j e -> p (j e)")
            mm(ps_t[:, 0, :], tri[:], mask_row, start=True, stop=True)
            mm(ps_t[:, 1, :], ones16[:], mask_row, start=True, stop=True).then_inc(cnt_done, 1)

            pe.wait_ge(s_lo_done, DC + SH // 2)
            with pe.Fori(0, NS // 2) as s2:
                for u in range(2):
                    s = s2 * 2 + u
                    pe.wait_ge(xs_in[u], (s2 + 1) * 32)
                    for q in range(SH):
                        i = s * SH + q
                        cols = slice(q * P, (q + 1) * P)
                        if q >= 2:
                            pe.wait_ge(mul_done, 1 + i - 1)
                        else:
                            pe.wait_ge(mul_done, 1 + s * SH)
                        for k, o in ((0, ps_h[:, q % 2, :]), (1, ps_y[:, q % 2, :])):
                            for c in range(DC):
                                mm(o, sg_hi[:, c, k, cols], xs_hi[u][:, c, :], start=(c == 0), stop=False)
                                mm(o, sg_hi[:, c, k, cols], xs_lo[u][:, c, :], start=False, stop=False)
                                last = mm(o, sg_lo[:, c, k, cols], xs_hi[u][:, c, :], start=False, stop=(c == DC - 1))
                        last.then_inc(gu_done, 1)
                    pe.wait_ge(slo_done, 1 + (s + 1) * SH)
                    for j in range(TPS):
                        if j >= 2:
                            pe.wait_ge(sy_read, 1 + s * TPS + j - 1)
                        else:
                            pe.wait_ge(sy_read, 1 + s * TPS)
                        cols = slice(j * P, (j + 1) * P)
                        o = ps_y[:, 2 + j % 2, :]
                        for q in range(SH):
                            mm(o, sh_hi[:, q, cols], sd_hi[:, q, :], start=(q == 0), stop=False)
                            mm(o, sh_hi[:, q, cols], sd_lo[:, q, :], start=False, stop=False)
                            last = mm(o, sh_lo[:, q, cols], sd_hi[:, q, :], start=False, stop=(q == SH - 1))
                        last.then_inc(sy_done, 1)
            pe.wait_ge(slot_cv, 1)
            nc.tensor.transpose(ps_u[:, 0, 0, 0:ETAB], slot_f[:], ident[0:ETAB, 0:ETAB]).then_inc(slot_tr, 1)
            through(pe, sh_over, 5)

            pe.wait_ge(etab_ok, 1)

            def turn_x(t, u, n):
                pe.wait_ge(xg_in[u], n)
                pe.wait_ge(xgt_cp, 1 + t)
                for c in range(DC):
                    last = nc.tensor.transpose(ps_t[:, c, :], xg[u][:, c * P:(c + 1) * P], ident[:])
                last.then_inc(xgt_done, 1)

            def gate_up(t, u, e):
                pe.wait_ge(xgt_cp, 1 + t + 1)
                pe.wait_ge(rg_done, 1 + t)
                for k in range(2):
                    for c in range(DC):
                        w = wgu[:, bass.ds(e, 1), c, k * H1:(k + 1) * H1].rearrange("p a n -> p (a n)")
                        last = mm(ps_h[:, k, 0:H1], xg_t[u][:, c, :], w, start=(c == 0), stop=(c == DC - 1))
                last.then_inc(rgu_done, 1)

            def down_r(t, e):
                pe.wait_ge(rg_done, 1 + t + 1)
                pe.wait_ge(rgt_cp, 1 + t)
                for c in range(HC):
                    k = min(P, H1 - c * P)
                    last = nc.tensor.transpose(ps_y[0:k, 0, c * P:(c + 1) * P], rg[:, c * P:c * P + k], ident[:])
                last.then_inc(rgt_done, 1)
                pe.wait_ge(rgt_cp, 1 + t + 1)
                pe.wait_ge(ry_cp, 1 + t)
                for c in range(HC):
                    k = min(P, H1 - c * P)
                    w = wdn[0:k, bass.ds(e, 1), c, :].rearrange("p a n -> p (a n)")
                    last = mm(ps_y[:, 1, :], rg_t[0:k, c, :], w, start=(c == 0), stop=(c == HC - 1))
                last.then_inc(ry_done, 1)

            def slot_tile(t, u, n):
                e = pe.value_load(etab[0:1, bass.ds(t, 1)], min_val=0, max_val=E - 1)
                turn_x(t, u, n)
                gate_up(t, u, e)
                down_r(t, e)
            for e in range(E):
                pe.wait_ge(we_in[e], 48)
            with pe.Fori(0, SLOT_TILES // 2) as m:
                for u in range(2):
                    slot_tile(m * 2 + u, u, (m + 1) * 16)
            slot_tile(SLOT_TILES - 1, 0, (SLOT_TILES // 2 + 1) * 16)


_OUT = (32, 64, 512)


def layouts(v):
    import numpy as np
    g = {k: np.asarray(a) for k, a in v.items()}
    c = np.ascontiguousarray
    f_tiles = 16
    w1t = g["L0_ffn_W1"].T.reshape(4, 128, f_tiles, 128).transpose(2, 1, 0, 3)
    b1t = g["L0_ffn_B1"].transpose(0, 2, 1).reshape(64, f_tiles, 128).transpose(1, 0, 2)
    w1b = np.concatenate([w1t, np.concatenate([b1t, b1t], 1)[:, :, None, :]], 2).reshape(f_tiles, 128, 640)
    bias = g["L0_ffn_b1"].reshape(f_tiles, 128, 1)
    w1b = np.concatenate([w1b, bias, bias], 2)
    b2t = g["L0_ffn_B2"].transpose(0, 2, 1).reshape(64, 512)
    return dict(
        x=c(g["x"].reshape(2048, 512)),
        itok0=c(g["itok_B_1_198"].reshape(16, 2).T),
        itok1=c(g["itok_B_0_7"].reshape(16, 2).T),
        side=c(g["fside_8xS_0"].reshape(512, 1)),
        cond0=c(g["L0_cond_weights"].reshape(200 * 64, 64)),
        router0=c(np.concatenate([g["L0_ffn_W_r"], g["L0_ffn_A1"].reshape(64, 512)], 0).T),
        router0_b=c(g["L0_ffn_b_r"].reshape(1, 8)),
        w1b=c(w1b),
        w2=c(g["L0_ffn_W2"].T),
        b2=c(g["L0_ffn_b2"].reshape(1, 512)),
        a2=c(g["L0_ffn_A2"].reshape(64, 2048).T),
        b2s=c(np.concatenate([b2t, b2t], 0)),
        cond1=c(g["L1_cond_weights"].reshape(8 * 64, 64)),
        gate1=c(g["L1_ffn_gate_w"]),
        wgu1=c(np.concatenate([g["L1_ffn_w_gate"], g["L1_ffn_w_up"]], 2)),
        wdn1=c(g["L1_ffn_w_down"]),
        sgu1=c(np.concatenate([g["L1_ffn_sw_gate"], g["L1_ffn_sw_up"]], 1)),
        sdn1=c(g["L1_ffn_sw_down"]),
    )


def kernel(**inputs):
    import concourse.bacc as _bacc
    from concourse.bass_utils import run_bass_kernel_spmd as _run

    nc = _bacc.Bacc("TRN2", target_bir_lowering=False, num_devices=1)
    arrays, args = {}, []
    for name, a in layouts(inputs).items():
        arrays[f"in_{name}"] = a
        args.append(nc.dram_tensor(f"in_{name}", a.shape, mybir.dt.from_np(a.dtype), kind="ExternalInput").ap())
    out = nc.dram_tensor("out_x", (2048, 512), F32, kind="ExternalOutput").ap()
    adaln_ffn(nc, *args, out)
    r = _run(nc, [arrays], core_ids=[0])
    return r.results[0]["out_x"].reshape(_OUT)
```

```python
from contextlib import ExitStack

import concourse.bass as bass
from concourse import mybir

F32 = mybir.dt.float32
F32R = mybir.dt.float32r
BF16 = mybir.dt.bfloat16
I32 = mybir.dt.int32
ALU = mybir.AluOpType
ACT = mybir.ActivationFunctionType
AX = mybir.AxisListType

P = 128
D = 512
DC = D // P
SEQ = 64
E = 8
SUP = 512
TPS = SUP // P
LORA_SCALE = 2.0


def adaln_ffn(nc, x, itok0, itok1, side, cond0, router0, router0_b, w1b, w2, b2, b2s,
              cond1, gate1, wgu1, wdn1, sgu1, sdn1, out):
    N = x.shape[0]
    J = N // P
    NS = N // SUP
    FT = w1b.shape[0]
    ER = router0.shape[1] - E
    R = ER // E
    STEPS = NS * FT
    H1 = wdn1.shape[1]
    HC = -(-H1 // P)
    HP = sdn1.shape[0]
    SH = -(-HP // P)
    SLOT_TILES = 2 * J + E - 1
    ETAB = SLOT_TILES + 1
    assert STEPS == 4 * J
    PREP = [*range(2, NS), 0, 1]
    WT = (DC + 1) * P + ER
    WROW = w1b.shape[2]

    scr = lambda name, shape, dt=F32: nc.dram_tensor(name, shape, dt, kind="Internal").ap()
    xt_hi_d = scr("xt_hi_d", (NS - 2, P, DC * SUP))
    xt_lo_d = scr("xt_lo_d", (NS - 2, P, DC * SUP))
    wrow_d = scr("wrow_d", (2 * J, P))
    xc_d = scr("xc_d", (N + P, D))
    slot_d = scr("slot_d", (ETAB * P, 2), I32)
    x1_d = scr("x1_d", (N, D))

    with ExitStack() as top:
        def sem(name):
            return top.enter_context(nc.semaphore(name))

        def tensors(stack):
            return lambda name, shape, dt=F32: stack.enter_context(nc.sbuf_tensor(name, shape, dt))

        psum = lambda name, shape, dt=F32: top.enter_context(nc.psum_tensor(name, shape, dt))

        ps_h = psum("ps_h", [P, 2, SUP])
        ps_y = psum("ps_y", [P, TPS, D])
        ps_u = psum("ps_u", [P, 2, SUP])

        sb = tensors(top)
        ident = sb("ident", [P, P])
        zero16 = sb("zero16", [P, SUP], BF16)
        rev8 = sb("rev8", [P, E])
        tri = sb("tri", [P, P], BF16)
        ones16 = sb("ones16", [P, P], BF16)
        tok_id = sb("tok_id", [P, J], I32)
        ident16 = sb("ident16", [P, P], BF16)
        cw1 = sb("cw1", [P, J, SEQ])
        side_col = sb("side_col", [P, J])
        it_row = [sb(f"it_row{k}", [1, 2 * J], I32) for k in range(2)]

        l0 = ExitStack()
        sb = tensors(l0)
        w2_hi = sb("w2_hi", [P, FT, D], F32R)
        w2_lo = sb("w2_lo", [P, FT, D], F32R)
        stage = ExitStack()
        w2_raw = tensors(stage)("w2_raw", [P, FT // 2, D])
        stage.close()
        z_base = sb("z_base", [P, N], F32R)
        z_step = sb("z_step", [P, N], F32R)
        m_base = sb("m_base", [P, N], BF16)
        m_step = sb("m_step", [P, N], BF16)
        xt_hi = [sb(f"xt_hi{u}", [P, DC, SUP], F32R) for u in range(2)]
        xt_lo = [sb(f"xt_lo{u}", [P, DC, SUP], F32R) for u in range(2)]
        w_raw = [sb(f"w_raw{u}", [P, WROW]) for u in range(2)]
        w_hl = [sb(f"w_hl{u}", [P, 2 * WT], F32R) for u in range(2)]
        b2s_hi = sb("b2s_hi", [P, D], F32R)
        b2s_lo = sb("b2s_lo", [P, D], F32R)
        b2_rows = sb("b2_rows", [P, D])
        bias1 = [sb(f"bias1{u}", [P, 1]) for u in range(2)]
        rb_rows = sb("rb_rows", [P, E])
        lg = sb("lg", [P, J, 2, E])
        rt = {n: sb(f"rt_{n}", [P, J, E]) for n in ("l", "p", "q", "oh0", "oh1")}
        rc = {n: sb(f"rc_{n}", [P, J]) for n in ("m", "s")}
        w01 = sb("w01", [P, 2, J])
        wsum = sb("wsum", [P, J])
        w01_t = sb("w01_t", [2 * J, P])

        prep = ExitStack()
        sb = tensors(prep)
        matrices = ExitStack()
        bd = tensors(matrices)("bd", [P, J, P])
        matrices.close()
        mexp = [sb(f"mexp{k}", [P, J, P], BF16) for k in range(2)]
        x_in = [sb(f"x_in{u}", [P, TPS, D]) for u in range(2)]
        u1_raw = sb("u1_raw", [P, DC, P])
        u1_hi = sb("u1_hi", [P, DC, P], F32R)
        u1_lo = sb("u1_lo", [P, DC, P], F32R)
        rw_raw = sb("rw_raw", [P, DC, E])
        rw_hl = sb("rw_hl", [P, DC, 2, E], F32R)
        b2s_raw = sb("b2s_raw", [P, D])
        lg_t = sb("lg_t", [2 * E, SUP])
        u1t = sb("u1t", [P, N])
        zf = [sb(f"zf{u}", [P, SUP]) for u in range(2)]
        prep.close()

        mainp = ExitStack()
        sb = tensors(mainp)
        h0 = [sb(f"h0{u}", [P, SUP]) for u in range(2)]
        h1 = [sb(f"h1{u}", [P, SUP]) for u in range(2)]
        g_hi = [sb(f"g_hi{u}", [P, SUP], F32R) for u in range(2)]
        g_lo = [sb(f"g_lo{u}", [P, SUP], F32R) for u in range(2)]
        g1_hi = [sb(f"g1_hi{u}", [P, SUP], F32R) for u in range(2)]
        g1_lo = [sb(f"g1_lo{u}", [P, SUP], F32R) for u in range(2)]
        wb = sb("wb", [P, 2, 2, SUP])
        xres = sb("xres", [P, TPS, D])
        zz = sb("zz", [P, SUP])
        zq = sb("zq", [P, SUP])
        z2_hi = sb("z2_hi", [P, SUP], F32R)
        z2_lo = sb("z2_lo", [P, SUP], F32R)
        mainp.close()
        l0.close()

        l1 = ExitStack()
        sb = tensors(l1)
        acc = sb("acc", [P, J, D])
        gate_raw = sb("gate_raw", [P, DC, E])
        gate_hl = sb("gate_hl", [P, DC, 2, E], F32R)
        lg1 = sb("lg1", [P, J, 2, E])
        q1 = {n: sb(f"q1_{n}", [P, J, E]) for n in ("l", "p", "q", "oh0", "oh1")}
        c1 = {n: sb(f"c1_{n}", [P, J]) for n in ("m", "s")}
        w1k = sb("w1k", [P, 2, J])
        pos_i = sb("pos_i", [P, 2, J], I32)
        cnt = [sb(f"cnt{u}", [P, J, E]) for u in range(2)]
        rank = sb("rank", [P, J, E])
        mask16 = sb("mask16", [P, J, E], BF16)
        ex = {n: sb(f"ex_{n}", [P, E]) for n in ("t", "a", "b")}
        ex_i = sb("ex_i", [P, E], I32)
        etile = sb("etile", [P, ETAB])
        etab3 = sb("etab3", [P, ETAB, E])
        etab_f = sb("etab_f", [P, ETAB])
        etab = sb("etab", [P, ETAB], I32)
        last_tile = sb("last_tile", [P, E + 2], I32)
        pay = sb("pay", [P, 2, J, 2], I32)
        slot_tab = sb("slot_tab", [ETAB, P, 2], I32)
        slot_f = sb("slot_f", [ETAB, 2, P])
        slot_tok = sb("slot_tok", [P, ETAB], I32)
        slot_w = sb("slot_w", [P, ETAB])

        shared = ExitStack()
        sb = tensors(shared)
        sg_hi = sb("sg_hi", [P, DC, 2, SH * P], F32R)
        sg_lo = sb("sg_lo", [P, DC, 2, SH * P], F32R)
        s_raw = [sb(f"s_raw{u}", [P, 2 * SH * P]) for u in range(2)]
        bdq = [sb(f"bdq{u}", [P, TPS, P]) for u in range(2)]
        xc = sb("xc", [P, TPS, D])
        xs_hi = [sb(f"xs_hi{u}", [P, DC, SUP], F32R) for u in range(2)]
        xs_lo = [sb(f"xs_lo{u}", [P, DC, SUP], F32R) for u in range(2)]
        sd_hi = sb("sd_hi", [P, SH, D], F32R)
        sd_lo = sb("sd_lo", [P, SH, D], F32R)
        sh_s = sb("sh_s", [P, SUP])
        sh_g = sb("sh_g", [P, SUP])
        sh_hi = sb("sh_hi", [P, SH, SUP], F32R)
        sh_lo = sb("sh_lo", [P, SH, SUP], F32R)
        lgt1 = sb("lgt1", [2 * E, SUP])
        shared.close()

        routed = ExitStack()
        sb = tensors(routed)
        eg_hi = sb("eg_hi", [P, 2, DC, 2 * H1], F32R)
        eg_lo = sb("eg_lo", [P, 2, DC, 2 * H1], F32R)
        xg = [sb(f"xg{u}", [P, D]) for u in range(2)]
        e_raw = sb("e_raw", [P, DC * 2 * H1 + HC * D])
        ed_hi = sb("ed_hi", [P, 2, HC, D], F32R)
        ed_lo = sb("ed_lo", [P, 2, HC, D], F32R)
        xg_hi = sb("xg_hi", [P, DC, P], F32R)
        xg_lo = sb("xg_lo", [P, DC, P], F32R)
        xg_f = sb("xg_f", [P, DC * P])
        rs = sb("rs", [P, H1])
        ru = sb("ru", [P, H1])
        rg = sb("rg", [P, HC * P])
        rgt_f = sb("rgt_f", [P, HC * P])
        rgt_hi = sb("rgt_hi", [P, HC, P], F32R)
        rgt_lo = sb("rgt_lo", [P, HC, P], F32R)
        yt = [sb(f"yt{u}", [P, D]) for u in range(2)]
        routed.close()
        l1.close()

        const_set = sem("const_set")
        small_in = sem("small_in")
        it_in = sem("it_in")
        bd_in = [[sem(f"bd_in{s}{h}") for h in range(2)] for s in range(NS)]
        lgt_done = sem("lgt_done")
        lgt_cp = sem("lgt_cp")
        u1_done = sem("u1_done")
        u1_read = sem("u1_read")
        w01t_done = sem("w01t_done")
        mexp_ok = sem("mexp_ok")
        mt_done = sem("mt_done")
        mt_read = sem("mt_read")
        z_hi = sem("z_hi")
        z_ok = sem("z_ok")
        warm = sem("warm")
        bd_zero = sem("bd_zero")
        split_small = sem("split_small")
        x_in_s = [sem(f"x_in_s{u}") for u in range(2)]
        cond_done = sem("cond_done")
        xt_hi_done = sem("xt_hi_done")
        xt_lo_done = sem("xt_lo_done")
        xt_st = [sem(f"xt_st{u}") for u in range(2)]
        lg_done = sem("lg_done")
        lu_done = sem("lu_done")
        rch = sem("rch")
        r_max = sem("r_max")
        r_exp = sem("r_exp")
        w01_ok = sem("w01_ok")
        wt_sb = sem("wt_sb")
        wrow_st = sem("wrow_st")
        w2_in = [sem(f"w2_in{u}") for u in range(FT // 2)]
        w2_hi_done = sem("w2_hi_done")
        w2_lo_done = sem("w2_lo_done")
        w1_in = [sem(f"w1_in{u}") for u in range(2)]
        w1_hi_done = sem("w1_hi_done")
        w1_lo_done = sem("w1_lo_done")
        xt_in = [sem(f"xt_in{u}") for u in range(2)]
        wb_in = [sem(f"wb_in{u}") for u in range(2)]
        xres_in = sem("xres_in")
        x1_st = sem("x1_st")
        a_done = sem("a_done")
        z_done = sem("z_done")
        h0_done = sem("h0_done")
        h1_done = sem("h1_done")
        gch = sem("gch")
        g_done = sem("g_done")
        d_done = sem("d_done")
        z2_ok = sem("z2_ok")
        y_done = sem("y_done")
        y_read = sem("y_read")
        ech = sem("ech")
        xb_done = sem("xb_done")

        l0_over = sem("l0_over")
        cw1_in = [sem(f"cw1_in{h}") for h in range(2)]
        gate_in = sem("gate_in")
        gate_done = sem("gate_done")
        acc_in = [sem(f"acc_in{s}") for s in range(NS)]
        bdq_zero = sem("bdq_zero")
        bdq_done = sem("bdq_done")
        c1_done = sem("c1_done")
        xc_done = sem("xc_done")
        xc_st = sem("xc_st")
        xt1_done = sem("xt1_done")
        xs_hi_done = sem("xs_hi_done")
        xs_lo_done = sem("xs_lo_done")
        lg1_done = sem("lg1_done")
        lgt1_cp = sem("lgt1_cp")
        lgt1_done = sem("lgt1_done")
        lg1_read = sem("lg1_read")
        r1_max = sem("r1_max")
        r1_exp = sem("r1_exp")
        mask_ok = sem("mask_ok")
        cnt_done = sem("cnt_done")
        pos_ok = sem("pos_ok")
        etab_ok = sem("etab_ok")
        slot_set = sem("slot_set")
        slot_z_st = sem("slot_z_st")
        zero_st = sem("zero_st")
        slot_st = sem("slot_st")
        slot_in = sem("slot_in")
        slot_cv = sem("slot_cv")
        slot_tr = sem("slot_tr")
        slot_ok = sem("slot_ok")
        s_in = [sem(f"s_in{u}") for u in range(2)]
        s_hi_done = sem("s_hi_done")
        sg_lo_done = sem("sg_lo_done")
        sd_lo_done = sem("sd_lo_done")
        pad_done = sem("pad_done")
        gu_done = sem("gu_done")
        sil_done = sem("sil_done")
        mul_done = sem("mul_done")
        shi_done = sem("shi_done")
        slo_done = sem("slo_done")
        sy_done = sem("sy_done")
        sy_read = sem("sy_read")
        out_st = sem("out_st")
        sh_over = sem("sh_over")
        e_in = sem("e_in")
        e_ch = sem("e_ch")
        e_done = sem("e_done")
        xg_in = [sem(f"xg_in{u}") for u in range(2)]
        xgt_done = sem("xgt_done")
        xg_hi_done = sem("xg_hi_done")
        xg_lo_done = sem("xg_lo_done")
        rgate_done = sem("rgate_done")
        rup_done = sem("rup_done")
        rs_done = sem("rs_done")
        ru_done = sem("ru_done")
        xg_f_done = sem("xg_f_done")
        rgt_f_done = sem("rgt_f_done")
        rg_zero = sem("rg_zero")
        rg_done = sem("rg_done")
        rgt_done = sem("rgt_done")
        rgt_hi_done = sem("rgt_hi_done")
        rgt_lo_done = sem("rgt_lo_done")
        ry_done = sem("ry_done")
        ry_cp = sem("ry_cp")
        y_st = sem("y_st")

        def opened(eng, *sems, by=1):
            for which in sems:
                eng.sem_inc(which, by)

        def through(eng, which, count):
            eng.drain().then_inc(which, 1)
            eng.wait_ge(which, count)

        block = top.enter_context(nc.Block())
        G_OPS = 6

        ROWS_STEPS = 6

        def rows_step_after_gate_up(s, q):
            k = q if s == 0 else q + 2
            return (s + 1, k) if s + 1 < NS and k < ROWS_STEPS else None

        def rows_step_after_down(s, j):
            return (s + 2, j - 2) if j >= 2 and s + 2 < NS else None

        def mt_bank(n):
            return ps_y[:, n % 4, 0:SUP // 2].bitcast(BF16)

        def shared_halves(n):
            raw = s_raw[n % 2]
            if n < DC:
                return tuple(t[:, n].rearrange("p k n -> p (k n)") for t in (sg_hi, sg_lo)) + (raw[:],)
            q = 2 * (n - DC)
            return tuple(t[:, q:q + 2, :].rearrange("p q n -> p (q n)") for t in (sd_hi, sd_lo)) + (raw[:, 0:2 * D],)

        def load_matrix(eng, dst, k, width, which, j, h):
            table = (cond0, cond1)[k]
            off = h * SEQ if width == P else 0
            b = eng.value_load(it_row[k][0:1, bass.ds(j * 2 + h, 1)], min_val=0, max_val=table.shape[0] // SEQ - 1)
            eng.dma_start(dst[h * SEQ:(h + 1) * SEQ, bass.ds(j, 1), off:off + SEQ]
                          .rearrange("p a n -> p (a n)"), table[bass.ds(b * SEQ, SEQ), :]).then_inc(which, 16)
            if k == 1:
                eng.dma_start(side_col[h * SEQ:(h + 1) * SEQ, bass.ds(j, 1)],
                              side[bass.ds(b * SEQ, SEQ), :]).then_inc(which, 16)

        @block.sync
        def _(sp):
            opened(sp, x1_st, by=16)
            for k, itok in enumerate((itok0, itok1)):
                sp.dma_start(it_row[k][:], itok).then_inc(it_in, 16)

            def load_x(n):
                s = PREP[n]
                sp.dma_start(x_in[n % 2][:], x[s * SUP:(s + 1) * SUP, :].rearrange("(j p) n -> p j n", p=P))\
                    .then_inc(x_in_s[n % 2], 16)

            def load_bd(n):
                with sp.Fori(PREP[n] * TPS, (PREP[n] + 1) * TPS) as j:
                    load_matrix(sp, bd, 0, P, bd_in[n][0], j, 0)

            def load_w2(f):
                if f >= FT // 2:
                    sp.wait_ge(w2_lo_done, f - FT // 2 + 1)
                sp.dma_start(w2_raw[:, f % (FT // 2), :], w2[f * P:(f + 1) * P, :])\
                    .then_inc(w2_in[f % (FT // 2)], 16)

            load_x(0)
            sp.wait_ge(it_in, 32)
            sp.wait_ge(bd_zero, 1)
            load_bd(0)
            for dst, src in ((u1_raw[:, :, 0:ER], router0[:, E:E + ER].rearrange("(c p) n -> p c n", p=P)),
                             (u1_raw[:, :, ER:P], router0[:, E:E + ER].rearrange("(c p) n -> p c n", p=P)),
                             (rw_raw[:], router0[:, 0:E].rearrange("(c p) n -> p c n", p=P)),
                             (b2s_raw[:], b2s),
                             (rb_rows[:], router0_b[0:1, :].partition_broadcast(P)),
                             (b2_rows[:], b2[0:1, :].partition_broadcast(P))):
                sp.dma_start(dst, src).then_inc(small_in, 16)
            load_x(1)
            for n in range(1, NS):
                load_bd(n)
            for f in range(FT // 2):
                load_w2(f)
            for n in range(NS):
                if n + 2 < NS:
                    sp.wait_ge(cond_done, 1 + (n + 1) * DC)
                    load_x(n + 2)
                    sp.wait_ge(xt_lo_done, 4 + (n + 1) * DC)
                    for half, dst in ((xt_hi, xt_hi_d), (xt_lo, xt_lo_d)):
                        sp.dma_start(dst[PREP[n] - 2], half[n % 2][:].rearrange("p c n -> p (c n)").bitcast(F32))\
                            .then_inc(xt_st[n % 2], 16)
                for f in range(FT // 2 + 2 * n, FT // 2 + 2 * n + 2):
                    load_w2(f)

            def load_w1(i, f, u):
                sp.wait_ge(w1_lo_done, i + 1)
                sp.dma_start(w_raw[u][:],
                             w1b[bass.ds(f, 1)].rearrange("a p n -> p (a n)")).then_inc(w1_in[u], 16)
            load_w1(0, 0, 0)
            load_w1(1, 1, 1)
            sp.wait_ge(wt_sb, 1)
            sp.dma_start(wrow_d, w01_t[:]).then_inc(wrow_st, 16)
            sp.wait_ge(wrow_st, 16)

            def load_weights(s):
                for k in range(2):
                    sp.dma_start(wb[:, s % 2, k, :],
                                 wrow_d[k * J + s * TPS:k * J + (s + 1) * TPS, :].rearrange("(o j) p -> o (j p)", o=1)
                                 .partition_broadcast(P)).then_inc(wb_in[s % 2], 16)

            def load_super(s):
                for half, src in ((xt_hi, xt_hi_d), (xt_lo, xt_lo_d)):
                    sp.dma_start(half[s % 2][:].rearrange("p c n -> p (c n)").bitcast(F32), src[s - 2])\
                        .then_inc(xt_in[s % 2], 16)

            sp.wait_ge(u1_done, NS)
            load_weights(0)
            load_weights(1)
            for u in range(2):
                sp.wait_ge(xt_st[u], 32 * (NS // 2 - 1))
            for s in range(NS):
                for u in range(2):
                    load_w1(s * FT + 2 + u, 2 + u, u)
                if s:
                    sp.wait_ge(g_done, 2 + s * FT)
                    if s + 1 < NS:
                        load_super(s + 1)
                        load_weights(s + 1)
                else:
                    sp.wait_ge(z_ok, 2 * NS)
                    sp.wait_ge(u1_read, NS)
                if s == 0:
                    sp.wait_ge(lgt_done, NS)
                sp.wait_ge(x1_st, 16 + 16 * s)
                sp.dma_start(xres[:], x[s * SUP:(s + 1) * SUP, :].rearrange("(j p) n -> p j n", p=P))\
                    .then_inc(xres_in, 16)
                with sp.Fori(1, FT // 2) as m:
                    for u in range(2):
                        load_w1(m * 2 + (s * FT + 2 + u), (m * 2 + 2 + u) % FT, u)
                sp.wait_ge(y_read, 1 + s + 1)
                sp.dma_start(x1_d[s * SUP:(s + 1) * SUP, :].rearrange("(j p) n -> p j n", p=P), xres[:])\
                    .then_inc(x1_st, 16)
            sp.wait_ge(x1_st, 16 + 16 * NS)
            through(sp, l0_over, 5)

            for n in range(2):
                sp.dma_start(acc[:, n * TPS:(n + 1) * TPS, :],
                             x1_d[n * SUP:(n + 1) * SUP, :].rearrange("(j p) n -> p j n", p=P)).then_inc(acc_in[n], 16)
                if n == 0:
                    sp.dma_start(gate_raw[:], gate1.rearrange("(c p) n -> p c n", p=P)).then_inc(gate_in, 16)
            for n in range(2, NS):
                sp.dma_start(acc[:, n * TPS:(n + 1) * TPS, :],
                             x1_d[n * SUP:(n + 1) * SUP, :].rearrange("(j p) n -> p j n", p=P)).then_inc(acc_in[n], 16)
            zero32 = zero16[:].bitcast(F32)
            for dst in (xc_d, out):
                for h in range(2):
                    sp.dma_start(dst[N:N + P, h * (D // 2):(h + 1) * (D // 2)], zero32).then_inc(zero_st, 16)
            sp.wait_ge(slot_set, 3)
            sp.dma_start(slot_d.rearrange("(t p) o -> t p o", p=P), slot_tab[:]).then_inc(slot_z_st, 16)
            for s in range(NS):
                sp.wait_ge(xc_done, (s + 1) * TPS)
                sp.dma_start(xc_d[s * SUP:(s + 1) * SUP, :].rearrange("(j p) n -> p j n", p=P), xc[:])\
                    .then_inc(xc_st, 16)
            sp.wait_ge(slot_st, 16 * 2 * J)
            sp.dma_start(slot_tab[:], slot_d.rearrange("(t p) o -> t p o", p=P)).then_inc(slot_in, 16)

            def load_expert(e):
                if e:
                    sp.wait_ge(e_done, e)
                full = (H1 // P) * P
                gu = DC * 2 * H1
                sp.dma_start(e_raw[:, 0:gu].rearrange("p (c n) -> p c n", c=DC),
                             wgu1[e].rearrange("(c p) n -> p c n", p=P)).then_inc(e_in, 16)
                sp.dma_start(e_raw[:, gu:gu + full // P * D].rearrange("p (c n) -> p c n", n=D),
                             wdn1[e, 0:full, :].rearrange("(c p) n -> p c n", p=P)).then_inc(e_in, 16)
                sp.dma_start(e_raw[0:H1 - full, gu + full // P * D:], wdn1[e, full:H1, :]).then_inc(e_in, 16)

            sp.wait_ge(sd_lo_done, SH // 2)
            sp.wait_ge(xt1_done, DC * NS)
            sp.wait_ge(xc_st, 16 * NS)
            sp.wait_ge(xs_lo_done, DC * NS)
            load_expert(0)
            for s in range(NS):
                sp.wait_ge(sy_read, (s + 1) * TPS)
                sp.dma_start(out[s * SUP:(s + 1) * SUP, :].rearrange("(j p) n -> p j n", p=P),
                             acc[:, s * TPS:(s + 1) * TPS, :]).then_inc(out_st, 16)
            through(sp, sh_over, 5)
            for e in range(1, E):
                load_expert(e)
            sp.wait_ge(out_st, 16 * NS)
            sp.wait_ge(zero_st, 16 * 4)
            sp.wait_ge(y_st, 16 * SLOT_TILES)

        @block.gpsimd
        def _(pool):
            pool.sem_inc(w1_lo_done, 2)
            nc.gpsimd.memset(ident[:], 0.0).then_inc(const_set, 1)
            nc.gpsimd.memset(ident16[:], 0.0).then_inc(const_set, 1)
            nc.gpsimd.iota(rev8[:], pattern=[[-1, E]], base=E, channel_multiplier=0,
                           allow_small_or_imprecise_dtypes=True).then_inc(const_set, 1)
            nc.gpsimd.memset(zero16[:], 0.0).then_inc(const_set, 1)
            nc.gpsimd.memset(ones16[:], 1.0).then_inc(const_set, 1)
            nc.gpsimd.iota(tok_id[:], pattern=[[P, J]], base=0, channel_multiplier=1).then_inc(const_set, 1)
            pool.wait_ge(const_set, 6)
            nc.gpsimd.affine_select(out=tri[:], in_=ones16[:], compare_op=ALU.is_gt, fill=0.0,
                                    base=0, pattern=[[1, P]], channel_multiplier=-1).then_inc(const_set, 1)
            nc.gpsimd.affine_select(out=ident[:], in_=ident[:], compare_op=ALU.not_equal, fill=1.0,
                                    base=0, pattern=[[-1, P]], channel_multiplier=1).then_inc(const_set, 1)
            nc.gpsimd.affine_select(out=ident16[:], in_=ident16[:], compare_op=ALU.not_equal, fill=1.0,
                                    base=0, pattern=[[-1, P]], channel_multiplier=1).then_inc(const_set, 1)
            pool.wait_ge(it_in, 32)
            pool.wait_ge(bd_zero, 1)
            for n in range(NS):
                with pool.Fori(PREP[n] * TPS, (PREP[n] + 1) * TPS) as j:
                    load_matrix(pool, bd, 0, P, bd_in[n][1], j, 1)
            for f in range(FT):
                pool.wait_ge(w2_hi_done, f + 1)
                nc.gpsimd.tensor_tensor(w2_lo[:, f, :], w2_raw[:, f % (FT // 2), :], w2_hi[:, f, :].bitcast(F32),
                                        ALU.subtract).then_inc(w2_lo_done, 1)

            def low_w1(i, u):
                pool.wait_ge(w1_hi_done, i + 1)
                nc.gpsimd.tensor_tensor(w_hl[u][:, WT:WT + ER], w_raw[u][:, WT - ER:WT],
                                        w_hl[u][:, WT - ER:WT].bitcast(F32), ALU.subtract)
                nc.gpsimd.tensor_tensor(w_hl[u][:, WT + ER:2 * WT], w_raw[u][:, 0:WT - ER],
                                        w_hl[u][:, 0:WT - ER].bitcast(F32), ALU.subtract).then_inc(w1_lo_done, 1)
            low_w1(0, 0)
            low_w1(1, 1)
            pool.wait_ge(w1_lo_done, 4)
            for n in range(2 * NS):
                z, cols = (z_base, z_step)[n % 2], slice(n // 2 * SUP, (n // 2 + 1) * SUP)
                pool.wait_ge(z_hi, n + 1)
                nc.gpsimd.tensor_tensor(z[ER:P, cols], zf[n % 2][ER:P, :], z[ER:P, cols].bitcast(F32), ALU.subtract)\
                    .then_inc(z_ok, 1)
            pool.wait_ge(z_ok, 2 * NS)
            with pool.Fori(0, J) as j:
                for h in range(2):
                    for u in range(2):
                        low_w1(j * (STEPS // J) + h * 2 + 2 + u, u)
                    load_matrix(pool, cw1, 1, SEQ, cw1_in[h], j, h)
            through(pool, l0_over, 5)

            pool.wait_ge(pad_done, 2)

            def load_s(n):
                u = n % 2
                if n < DC:
                    for k in range(2):
                        pool.dma_start(s_raw[u][:, k * SH * P:k * SH * P + HP],
                                       sgu1[n * P:(n + 1) * P, k * HP:(k + 1) * HP]).then_inc(s_in[u], 16)
                else:
                    q = 2 * (n - DC)
                    rows = min(HP - (q + 1) * P, P)
                    pool.dma_start(s_raw[u][:, 0:D], sdn1[q * P:(q + 1) * P, :]).then_inc(s_in[u], 16)
                    pool.dma_start(s_raw[u][0:rows, D:2 * D], sdn1[(q + 1) * P:(q + 1) * P + rows, :])\
                        .then_inc(s_in[u], 16)
            load_s(0)
            load_s(1)
            nc.gpsimd.iota(slot_tab[:, :, 0], pattern=[[1, P]], base=N, channel_multiplier=0).then_inc(slot_set, 1)
            nc.gpsimd.memset(slot_tab[:, :, 1], 0).then_inc(slot_set, 1)
            nc.gpsimd.iota(etile[:], pattern=[[1, ETAB]], base=0, channel_multiplier=0,
                           allow_small_or_imprecise_dtypes=True).then_inc(slot_set, 1)
            for n in range(2, DC + SH // 2):
                if n - 2 < DC:
                    pool.wait_ge(sg_lo_done, n - 1)
                else:
                    pool.wait_ge(s_hi_done, n - 1)
                    hi, lo, raw = shared_halves(n - 2)
                    nc.gpsimd.tensor_tensor(lo, raw, hi.bitcast(F32), ALU.subtract).then_inc(sd_lo_done, 1)
                    pool.wait_ge(sd_lo_done, n - 1 - DC)
                if n == DC + SH // 2 - 1:
                    nc.gpsimd.memset(s_raw[n % 2][:], 0.0).then_inc(pad_done, 1)
                    pool.wait_ge(pad_done, 3)
                load_s(n)
            for n in range(DC + SH // 2 - 2, DC + SH // 2):
                pool.wait_ge(s_hi_done, n + 1)
                hi, lo, raw = shared_halves(n)
                nc.gpsimd.tensor_tensor(lo, raw, hi.bitcast(F32), ALU.subtract).then_inc(sd_lo_done, 1)
            pool.wait_ge(slot_z_st, 16)
            pool.wait_ge(pos_ok, 1)
            for k in range(2):
                for j in range(J):
                    pool.indirect_dma_start(out=slot_d, in_=pay[:, k, j, :], in_offset=None,
                                            out_offset=bass.IndirectOffsetOnAxis(ap=pos_i[:, k, j:j + 1], axis=0))\
                        .then_inc(slot_st, 16)

            def gather(t):
                if t >= 2:
                    pool.wait_ge(xgt_done, t - 1)
                pool.indirect_dma_start(out=xg[t % 2][:], out_offset=None, in_=xc_d,
                                        in_offset=bass.IndirectOffsetOnAxis(ap=slot_tok[:, t:t + 1], axis=0))\
                    .then_inc(xg_in[t % 2], 16)

            def scatter_add(t):
                pool.wait_ge(ry_cp, t + 1)
                if t:
                    pool.wait_ge(y_st, 16 * t)
                pool.indirect_dma_start(out=out, in_=yt[t % 2][:], in_offset=None,
                                        out_offset=bass.IndirectOffsetOnAxis(ap=slot_tok[:, t:t + 1], axis=0),
                                        compute_op=ALU.add).then_inc(y_st, 16)

            def x_low(t):
                pool.wait_ge(xg_f_done, t + 1)
                nc.gpsimd.tensor_tensor(xg_lo[:].rearrange("p c n -> p (c n)"), xg_f[:],
                                        xg_hi[:].rearrange("p c n -> p (c n)").bitcast(F32), ALU.subtract)                    .then_inc(xg_lo_done, 1)

            def products(t):
                pool.wait_ge(ru_done, t + 1)
                if t:
                    pool.wait_ge(rgt_done, t)
                nc.gpsimd.tensor_tensor(rg[:, 0:H1], rs[:], ru[:], ALU.mult).then_inc(rg_done, 1)

            def g_low(t):
                pool.wait_ge(rgt_f_done, t + 1)
                nc.gpsimd.tensor_tensor(rgt_lo[:].rearrange("p c n -> p (c n)"), rgt_f[:],
                                        rgt_hi[:].rearrange("p c n -> p (c n)").bitcast(F32), ALU.subtract)                    .then_inc(rgt_lo_done, 1)

            pool.wait_ge(xc_st, 16 * NS)
            pool.wait_ge(zero_st, 16 * 4)
            pool.wait_ge(slot_ok, 1)
            pool.wait_ge(gu_done, NS * SH)
            gather(0)
            gather(1)
            through(pool, sh_over, 5)
            pool.wait_ge(out_st, 16 * NS)
            nc.gpsimd.memset(rg[:, H1:HC * P], 0.0).then_inc(rg_zero, 1)
            x_low(0)
            products(0)
            gather(2)
            x_low(1)
            for t in range(SLOT_TILES):
                g_low(t)
                if t + 1 < SLOT_TILES:
                    products(t + 1)
                if t + 3 < SLOT_TILES:
                    gather(t + 3)
                if t + 2 < SLOT_TILES:
                    x_low(t + 2)
                scatter_add(t)

        @block.scalar
        def _(act):
            act.sem_inc(h1_done, 2)

            def high_w2(f):
                act.wait_ge(w2_in[f % (FT // 2)], 16 * (f // (FT // 2) + 1))
                nc.scalar.copy(w2_hi[:, f, :], w2_raw[:, f % (FT // 2), :]).then_inc(w2_hi_done, 1)
            for s in range(NS):
                if s >= 2:
                    act.wait_ge(xt_st[s % 2], 32 * (s // 2))
                for c in range(DC):
                    act.wait_ge(cond_done, 1 + s * DC + c + 1)
                    nc.scalar.copy(xt_hi[s % 2][:, c, :], ps_y[:, c, :]).then_inc(xt_hi_done, 1)
                act.wait_ge(lg_done, s + 1)
                act.wait_ge(lgt_done, s)
                nc.scalar.copy(lg_t[:], ps_h[0:2 * E, 0, :]).then_inc(lgt_cp, 1)
                for f in range(s * (FT // NS), (s + 1) * (FT // NS)):
                    high_w2(f)
            def high_w1(i, u, n):
                act.wait_ge(w1_in[u], n)
                if not isinstance(i, int):
                    act.wait_ge(d_done, i)
                    act.wait_ge(h1_done, i + 1)
                nc.scalar.copy(bias1[u][:], w_raw[u][:, WT:WT + 1])
                nc.scalar.copy(w_hl[u][:, 0:WT], w_raw[u][:, 0:WT]).then_inc(w1_hi_done, 1)
            high_w1(0, 0, 16)
            high_w1(1, 1, 16)
            act.wait_ge(r_max, 1)
            nc.scalar.activation(rt["q"][:], rt["l"][:], ACT.Exp).then_inc(r_exp, 1)

            act.wait_ge(w01t_done, 1)
            nc.scalar.copy(w01_t[:], ps_h[0:2 * J, 1, 0:P]).then_inc(wt_sb, 1)
            for n in range(2 * NS):
                s, k = n // 2, n % 2
                act.wait_ge(mt_done, n + 1)
                nc.scalar.copy((m_base, m_step)[k][:, s * SUP:(s + 1) * SUP], mt_bank(n)).then_inc(mt_read, 1)
            nc.scalar.activation(h0[0][:], zero16[:], ACT.Gelu_apprx_tanh).then_inc(warm, 1)
            act.wait_ge(warm, 1)
            with act.Fori(0, NS) as s:
                with act.Fori(0, FT // 2) as m:
                    for u in range(2):
                        i = s * FT + m * 2 + u
                        b = bias1[u][:, 0:1]
                        act.wait_ge(a_done, i + 1)
                        act.wait_ge(g_done, i + 1)
                        nc.scalar.activation(h0[u][:], ps_h[:, u, :], ACT.Gelu_apprx_tanh, bias=b)\
                            .then_inc(h0_done, 1)
                        act.wait_ge(z_done, i + 3)
                        nc.scalar.activation(h1[u][:], ps_h[:, u, :], ACT.Gelu_apprx_tanh, bias=b)\
                            .then_inc(h1_done, 1)
                        high_w1(i + 2, u, (s * (FT // 2) + m + 2) * 16)
            through(act, l0_over, 5)

            def high_s(n):
                u = n % 2
                act.wait_ge(s_in[u], 32 * (n // 2 + 1))
                act.wait_ge(pad_done, 3 if n == DC + SH // 2 - 1 else 2)
                hi, lo, raw = shared_halves(n)
                nc.scalar.copy(hi, raw).then_inc(s_hi_done, 1)

            def rows_step(s, k):
                if k in (2, 3):
                    for c in (2 * k - 4, 2 * k - 3):
                        act.wait_ge(xt1_done, s * DC + c + 1)
                        if s >= 2:
                            act.wait_ge(gu_done, (s - 1) * SH)
                        nc.scalar.copy(xs_hi[s % 2][:, c, :], ps_u[:, c % 2, :]).then_inc(xs_hi_done, 1)
                if k == 4:
                    act.wait_ge(lg1_done, s + 1)
                    if s:
                        act.wait_ge(lgt1_done, s)
                    nc.scalar.copy(lgt1[:], ps_u[0:2 * E, 0, :]).then_inc(lgt1_cp, 1)

            high_s(0)
            high_s(1)
            rows_step(0, 2)
            high_s(2)
            rows_step(0, 3)
            high_s(3)
            rows_step(0, 4)
            for s in range(NS):
                for q in range(SH):
                    i = s * SH + q
                    if i:
                        act.wait_ge(mul_done, i)
                    act.wait_ge(gu_done, i + 1)
                    nc.scalar.activation(sh_s[:], ps_h[:, q % 2, :], ACT.Silu).then_inc(sil_done, 1)
                    if rows_step_after_gate_up(s, q):
                        rows_step(*rows_step_after_gate_up(s, q))
                    if s == 0 and q < SH // 2:
                        high_s(DC + q)
                    if (s, q) == (NS - 2, ROWS_STEPS - 2):
                        act.wait_ge(r1_max, 1)
                        nc.scalar.activation(q1["q"][:], q1["l"][:], ACT.Exp).then_inc(r1_exp, 1)
                for j in range(TPS):
                    if rows_step_after_down(s, j):
                        rows_step(*rows_step_after_down(s, j))
            through(act, sh_over, 5)

            def x_high(t, first=False):
                act.wait_ge(xgt_done, t + 1)
                nc.scalar.copy(xg_hi[:].rearrange("p c n -> p (c n)"), ps_u[:, 0, :]).then_inc(xg_hi_done, 1)
                if not first:
                    act.wait_ge(xg_lo_done, t)
                nc.scalar.copy(xg_f[:], ps_u[:, 0, :]).then_inc(xg_f_done, 1)

            def silu(t, u, first=False):
                if not first:
                    act.wait_ge(rg_done, t)
                act.wait_ge(rgate_done, t + 1)
                nc.scalar.activation(rs[:], ps_h[:, u, 0:H1], ACT.Silu).then_inc(rs_done, 1)

            def up(t, u):
                act.wait_ge(rup_done, t + 1)
                nc.scalar.copy(ru[:], ps_y[:, u, 0:H1]).then_inc(ru_done, 1)

            def g_high(t, first=False):
                act.wait_ge(rgt_done, t + 1)
                nc.scalar.copy(rgt_hi[:].rearrange("p c n -> p (c n)"), ps_u[:, 1, 0:HC * P]).then_inc(rgt_hi_done, 1)
                if not first:
                    act.wait_ge(rgt_lo_done, t)
                nc.scalar.copy(rgt_f[:], ps_u[:, 1, 0:HC * P]).then_inc(rgt_f_done, 1)

            def weigh(t, u, stored):
                if stored is not None:
                    act.wait_ge(y_st, stored)
                act.wait_ge(ry_done, 1 + t + 1)
                nc.scalar.activation(yt[u][:], ps_y[:, 2 + u, :], ACT.Copy, scale=slot_w[:, bass.ds(t, 1)])\
                    .then_inc(ry_cp, 1)

            def copies(t, u, stored, nxt=True, nxt2=True):
                if nxt:
                    silu(t + 1, 1 - u)
                g_high(t, first=stored is None and u == 0)
                if nxt:
                    up(t + 1, 1 - u)
                if nxt2:
                    x_high(t + 2)
                weigh(t, u, stored)
            x_high(0, first=True)
            silu(0, 0, first=True)
            up(0, 0)
            x_high(1)
            copies(0, 0, None)
            copies(1, 1, None)
            with act.Fori(1, SLOT_TILES // 2 - 1) as m:
                for u in range(2):
                    copies(m * 2 + u, u, (m * 2 + u - 1) * 16)
            for t in range(SLOT_TILES - 3, SLOT_TILES):
                copies(t, t % 2, (t - 1) * 16, t + 1 < SLOT_TILES, t + 2 < SLOT_TILES)

        @block.vector
        def _(dve):
            dve.sem_inc(xt_lo_done, 4)
            dve.sem_inc(lu_done, 1)
            dve.sem_inc(g_done, 2)
            opened(dve, y_read)
            nc.vector.memset(bd[:], 0.0).then_inc(bd_zero, 1)
            dve.wait_ge(const_set, 9)
            dve.wait_ge(small_in, 16 * 6)
            small = ((u1_hi[:], u1_lo[:], u1_raw[:]), (b2s_hi[:], b2s_lo[:], b2s_raw[:]),
                     (rw_hl[:, :, 0, :], rw_hl[:, :, 1, :], rw_raw[:]))
            for hi, lo, raw in small:
                nc.vector.tensor_copy(hi, raw).then_inc(split_small, 1)
            for n, (hi, lo, raw) in enumerate(small):
                dve.wait_ge(split_small, n + 1)
                nc.vector.tensor_tensor(lo, raw, hi.bitcast(F32), ALU.subtract).then_inc(split_small, 1)
            for s in range(NS):
                for c in range(DC):
                    dve.wait_ge(xt_hi_done, s * DC + c + 1)
                    nc.vector.tensor_tensor(xt_lo[s % 2][:, c, :], ps_y[:, c, :], xt_hi[s % 2][:, c, :].bitcast(F32),
                                            ALU.subtract).then_inc(xt_lo_done, 1)
                dve.wait_ge(u1_done, s + 1)
                nc.vector.tensor_copy(u1t[:, PREP[s] * SUP:(PREP[s] + 1) * SUP], ps_h[:, 1, :]).then_inc(u1_read, 1)
            dve.wait_ge(lgt_done, NS)
            nc.vector.tensor_copy(lg[:].rearrange("p j k e -> p (j k e)"), ps_u[:, 0, 0:J * 2 * E]).then_inc(lu_done, 1)

            count = [0]

            def link(ins):
                count[0] += 1
                ins.then_inc(rch, 1)
                dve.wait_ge(rch, count[0])

            def over_e(col):
                return col.unsqueeze(2).to_broadcast([P, J, E])

            tt = nc.vector.tensor_tensor

            def route(rt, rc, parts, bias, oh0, oh1, w_0, w_1, r_max, r_exp):
                l, p, q, m = rt["l"][:], rt["p"][:], rt["q"][:], rc["m"][:]
                link(tt(p, parts[:, :, 0, :], parts[:, :, 1, :], ALU.add))
                if bias is not None:
                    link(tt(p, p, bias.unsqueeze(1).to_broadcast([P, J, E]), ALU.add))
                link(nc.vector.tensor_reduce(m, p, AX.X, ALU.max))
                tt(l, p, over_e(m), ALU.subtract).then_inc(r_max, 1)
                dve.wait_ge(r_exp, 1)
                link(nc.vector.tensor_reduce(m, q, AX.X, ALU.add))
                link(nc.vector.reciprocal(rc["s"][:], m))
                link(tt(p, q, over_e(rc["s"][:]), ALU.mult))
                rev = rev8[:].unsqueeze(1).to_broadcast([P, J, E])
                for oh, w in ((oh0, w_0), (oh1, w_1)):
                    link(nc.vector.tensor_reduce(w, p, AX.X, ALU.max))
                    link(tt(q, p, over_e(w), ALU.is_equal))
                    link(tt(q, q, rev, ALU.mult))
                    link(nc.vector.tensor_reduce(m, q, AX.X, ALU.max))
                    link(tt(oh, q, over_e(m), ALU.is_equal))
                    if oh is oh0:
                        link(nc.vector.tensor_scalar(q, p, 1.0, None, ALU.add))
                        link(tt(q, q, oh, ALU.mult))
                        link(tt(p, p, q, ALU.subtract))

            dve.wait_ge(lu_done, 2)
            route(rt, rc, lg[:], rb_rows[:], rt["oh0"][:], rt["oh1"][:], w01[:, 0, :], w01[:, 1, :],
                  r_max, r_exp)
            tt(wsum[:], w01[:, 0, :], w01[:, 1, :], ALU.add).then_inc(w01_ok, 1)
            link(tt(rt["l"][:], rt["oh1"][:], rt["oh0"][:], ALU.subtract))
            for s in range(NS):
                for k, oh in ((0, rt["oh0"]), (1, rt["l"])):
                    for h in range(2):
                        js = slice(s * TPS, (s + 1) * TPS)
                        last = nc.vector.tensor_scalar(
                            mexp[k][:, js, h * ER:(h + 1) * ER].rearrange("p j (e r) -> p j e r", r=R),
                            oh[:, js, :].unsqueeze(3).to_broadcast([P, TPS, E, R]), LORA_SCALE, None, ALU.mult)
                    last.then_inc(mexp_ok, 1)
            for n in range(2 * NS):
                s, k = n // 2, n % 2
                z, cols = (z_base, z_step)[k], slice(s * SUP, (s + 1) * SUP)
                dve.wait_ge(mt_read, n + 1)
                if n == 0:
                    dve.wait_ge(w2_lo_done, FT)
                if n >= 2:
                    dve.wait_ge(z_ok, n - 1)
                link(tt(zf[n % 2][:], u1t[:, cols], (m_base, m_step)[k][:, cols], ALU.mult))
                nc.vector.tensor_copy(z[:, cols], zf[n % 2][:]).then_inc(z_hi, 1)

            with dve.Fori(0, NS // 2) as s2:
                for v in range(2):
                    s = s2 * 2 + v
                    with dve.Fori(0, FT // 2) as m:
                        for u in range(2):
                            i = s * FT + m * 2 + u
                            n = i * G_OPS
                            dve.wait_ge(wb_in[v], (s2 + 1) * 32)
                            dve.wait_ge(h0_done, i + 1)
                            tt(h0[u][:], h0[u][:], wb[:, v, 0, :], ALU.mult).then_inc(gch, 1)
                            dve.wait_ge(h1_done, i + 3)
                            tt(h1[u][:], h1[u][:], wb[:, v, 1, :], ALU.mult).then_inc(gch, 1)
                            dve.wait_ge(gch, n + 2)
                            dve.wait_ge(d_done, i + 1)
                            tt(h0[u][:], h0[u][:], h1[u][:], ALU.add).then_inc(gch, 1)
                            nc.vector.tensor_copy(g1_hi[u][:], h1[u][:]).then_inc(gch, 1)
                            dve.wait_ge(gch, n + 3)
                            nc.vector.tensor_copy(g_hi[u][:], h0[u][:]).then_inc(gch, 1)
                            dve.wait_ge(gch, n + 4)
                            tt(g1_lo[u][:], h1[u][:], g1_hi[u][:].bitcast(F32), ALU.subtract).then_inc(gch, 1)
                            dve.wait_ge(gch, n + 5)
                            tt(g_lo[u][:], h0[u][:], g_hi[u][:].bitcast(F32), ALU.subtract).then_inc(g_done, 1)
                    jj = s * TPS
                    dve.wait_ge(xres_in, (s + 1) * 16)
                    for j in range(TPS):
                        last = nc.vector.scalar_tensor_tensor(
                            out=xres[:, j, :], in0=b2_rows[:], scalar=wsum[:, bass.ds(jj + j, 1)],
                            in1=xres[:, j, :], op0=ALU.mult, op1=ALU.add)
                    last.then_inc(xb_done, 1)
                    dve.wait_ge(d_done, 2 + (s + 1) * FT)
                    cols = bass.ds(s * SUP, SUP)
                    tt(zz[:], ps_u[:, 0, :], m_base[:, cols], ALU.mult).then_inc(ech, 1)
                    tt(zq[:], ps_u[:, 1, :], m_step[:, cols], ALU.mult).then_inc(ech, 1)
                    dve.wait_ge(ech, s * 4 + 2)
                    tt(zz[:], zz[:], zq[:], ALU.add).then_inc(ech, 1)
                    dve.wait_ge(ech, s * 4 + 3)
                    dve.wait_ge(y_done, 1 + s)
                    nc.vector.tensor_copy(z2_hi[:], zz[:]).then_inc(ech, 1)
                    dve.wait_ge(ech, s * 4 + 4)
                    tt(z2_lo[:], zz[:], z2_hi[:].bitcast(F32), ALU.subtract).then_inc(z2_ok, 1)
                    dve.wait_ge(xb_done, s + 1)
                    dve.wait_ge(y_done, 1 + s + 1)
                    for j in range(TPS):
                        last = tt(xres[:, j, :], ps_y[:, j, :], xres[:, j, :], ALU.add)
                    last.then_inc(y_read, 1)
            through(dve, l0_over, 5)

            for u in range(2):
                nc.vector.memset(s_raw[u][:], 0.0).then_inc(pad_done, 1)
            for u in range(2):
                nc.vector.memset(bdq[u][:], 0.0).then_inc(bdq_zero, 1)
            for h in range(2):
                dve.wait_ge(cw1_in[h], 16 * 2 * J)
            dve.wait_ge(bdq_zero, 2)

            def diagonals(s):
                u = s % 2
                for h in range(2):
                    rows = slice(h * SEQ, (h + 1) * SEQ)
                    nc.vector.tensor_copy(bdq[u][rows, :, h * SEQ:(h + 1) * SEQ],
                                          cw1[rows, s * TPS:(s + 1) * TPS, :]).then_inc(bdq_done, 1)

            def low_s(n):
                dve.wait_ge(s_hi_done, n + 1)
                hi, lo, raw = shared_halves(n)
                tt(lo, raw, hi.bitcast(F32), ALU.subtract).then_inc(sg_lo_done, 1)

            def rows_step(s, k):
                if k < 2:
                    for j in (2 * k, 2 * k + 1):
                        if s:
                            dve.wait_ge(xc_st, 16 * s)
                            dve.wait_ge(xt1_done, DC * s)
                        dve.wait_ge(c1_done, s * TPS + j + 1)
                        jj = s * TPS + j
                        nc.vector.tensor_scalar(xc[:, j, :], ps_u[:, j % 2, :], side_col[:, jj:jj + 1], None, ALU.add)\
                            .then_inc(xc_done, 1)
                    if k == 1 and s + 1 < NS:
                        diagonals(s + 1)
                elif k < 4:
                    for c in (2 * k - 4, 2 * k - 3):
                        dve.wait_ge(xs_hi_done, s * DC + c + 1)
                        tt(xs_lo[s % 2][:, c, :], ps_u[:, c % 2, :], xs_hi[s % 2][:, c, :].bitcast(F32),
                           ALU.subtract).then_inc(xs_lo_done, 1)
                elif k == 5:
                    dve.wait_ge(lgt1_done, s + 1)
                    nc.vector.tensor_copy(lg1[:, s * TPS:(s + 1) * TPS].rearrange("p j k e -> p (j k e)"),
                                          ps_u[:, 1, 0:TPS * 2 * E]).then_inc(lg1_read, 1)

            def route_tokens():
                dve.wait_ge(lg1_read, NS)
                route(q1, c1, lg1[:], None, q1["oh0"][:], q1["oh1"][:], w1k[:, 0, :], w1k[:, 1, :], r1_max, r1_exp)
                for k in range(2):
                    nc.vector.tensor_copy(pay[:, k, :, 0], tok_id[:])
                tt(mask16[:], q1["oh0"][:], q1["oh1"][:], ALU.add).then_inc(mask_ok, 1)

            def place_tokens():
                oh0, oh1 = q1["oh0"][:], q1["oh1"][:]
                dve.wait_ge(cnt_done, 1)
                tot = ps_u[:, 0, P:2 * P].rearrange("p (j e) -> p j e", e=E)
                link(nc.vector.tensor_copy(rank[:], ps_u[:, 0, 0:P].rearrange("p (j e) -> p j e", e=E)))
                link(nc.vector.tensor_copy(cnt[0][:], tot))
                a, b = 0, 1
                d = 1
                while d < J:
                    nc.vector.tensor_copy(cnt[b][:, 0:d, :], cnt[a][:, 0:d, :])
                    link(tt(cnt[b][:, d:J, :], cnt[a][:, d:J, :], cnt[a][:, 0:J - d, :], ALU.add))
                    a, b, d = b, a, 2 * d
                ca = cnt[a]
                link(nc.vector.tensor_scalar(ex_i[:], ca[:, J - 1, :], 1.0, float(P - 1), ALU.max, ALU.add))
                link(nc.vector.tensor_single_scalar(ex_i[:], ex_i[:], 7, ALU.logical_shift_right))
                link(nc.vector.tensor_copy(ex["t"][:], ex_i[:]))
                link(nc.vector.tensor_copy(ex["a"][:], ex["t"][:]))
                xa, xb_, d = ex["a"], ex["b"], 1
                while d < E:
                    nc.vector.tensor_copy(xb_[:, 0:d], xa[:, 0:d])
                    link(tt(xb_[:, d:E], xa[:, d:E], xa[:, 0:E - d], ALU.add))
                    xa, xb_, d = xb_, xa, 2 * d
                dve.wait_ge(slot_set, 3)
                link(tt(etab3[:], etile[:].unsqueeze(2).to_broadcast([P, ETAB, E]),
                        xa[:].unsqueeze(1).to_broadcast([P, ETAB, E]), ALU.is_ge))
                link(nc.vector.tensor_reduce(etab_f[:], etab3[:], AX.X, ALU.add))
                link(nc.vector.memset(last_tile[:], 0))
                nc.vector.tensor_copy(last_tile[:, 2:E + 2], xa[:])
                nc.vector.tensor_scalar(etab[:], etab_f[:], float(E - 1), None, ALU.min).then_inc(etab_ok, 1)
                link(tt(xb_[:], xa[:], ex["t"][:], ALU.subtract))
                link(nc.vector.tensor_scalar(xb_[:], xb_[:], float(P), None, ALU.mult))
                link(tt(ca[:], ca[:], tot, ALU.subtract))
                link(tt(ca[:], ca[:], rank[:], ALU.add))
                link(tt(ca[:], ca[:], xb_[:].unsqueeze(1).to_broadcast([P, J, E]), ALU.add))
                for k, oh in ((0, oh0), (1, oh1)):
                    link(tt(rank[:], ca[:], oh, ALU.mult))
                    last = nc.vector.tensor_reduce(c1["m" if k else "s"][:], rank[:], AX.X, ALU.add)
                    link(last)
                    link(nc.vector.tensor_copy(pos_i[:, k, :], c1["m" if k else "s"][:]))
                nc.vector.tensor_copy(pay[:, :, :, 1].bitcast(F32), w1k[:]).then_inc(pos_ok, 1)


            def split_expert(e, u, k):
                gu, full = DC * 2 * H1, H1 // P
                raw_g = e_raw[:, 0:gu].rearrange("p (c n) -> p c n", c=DC)
                raw_d = e_raw[:, gu:gu + full * D].rearrange("p (c n) -> p c n", n=D)
                tail, raw_t = H1 - full * P, e_raw[0:H1 - full * P, gu + full * D:]
                if k == 0:
                    nc.vector.tensor_copy(eg_hi[:, u], raw_g).then_inc(e_ch, 1)
                elif k == 1:
                    dve.wait_ge(e_ch, 2 * e + 1)
                    tt(eg_lo[:, u], raw_g, eg_hi[:, u].bitcast(F32), ALU.subtract)
                elif k == 2:
                    nc.vector.tensor_copy(ed_hi[:, u, 0:full], raw_d)
                    nc.vector.tensor_copy(ed_hi[0:tail, u, full], raw_t).then_inc(e_ch, 1)
                else:
                    dve.wait_ge(e_ch, 2 * e + 2)
                    tt(ed_lo[:, u, 0:full], raw_d, ed_hi[:, u, 0:full].bitcast(F32), ALU.subtract)
                    tt(ed_lo[0:tail, u, full], raw_t, ed_hi[0:tail, u, full].bitcast(F32), ALU.subtract)\
                        .then_inc(e_done, 1)

            diagonals(0)
            low_s(0)
            rows_step(0, 0)
            rows_step(0, 1)
            dve.wait_ge(gate_in, 16)
            nc.vector.tensor_copy(gate_hl[:, :, 0, :], gate_raw[:]).then_inc(gate_done, 1)
            dve.wait_ge(gate_done, 1)
            tt(gate_hl[:, :, 1, :], gate_raw[:], gate_hl[:, :, 0, :].bitcast(F32), ALU.subtract).then_inc(gate_done, 1)
            low_s(1)
            rows_step(0, 2)
            low_s(2)
            rows_step(0, 3)
            low_s(3)
            rows_step(0, 5)

            for s in range(NS):
                for q in range(SH):
                    i = s * SH + q
                    dve.wait_ge(sil_done, i + 1)
                    if i:
                        dve.wait_ge(slo_done, i)
                    tt(sh_g[:], sh_s[:], ps_y[:, q % 2, :], ALU.mult).then_inc(mul_done, 1)
                    dve.wait_ge(mul_done, i + 1)
                    if s:
                        dve.wait_ge(sy_done, s * TPS)
                    nc.vector.tensor_copy(sh_hi[:, q, :], sh_g[:]).then_inc(shi_done, 1)
                    dve.wait_ge(shi_done, i + 1)
                    tt(sh_lo[:, q, :], sh_g[:], sh_hi[:, q, :].bitcast(F32), ALU.subtract).then_inc(slo_done, 1)
                    if rows_step_after_gate_up(s, q):
                        rows_step(*rows_step_after_gate_up(s, q))
                    if (s, q) == (NS - 2, ROWS_STEPS - 2):
                        route_tokens()
                    if (s, q) == (NS - 2, ROWS_STEPS - 1):
                        place_tokens()
                for j in range(TPS):
                    dve.wait_ge(sy_done, s * TPS + j + 1)
                    a = acc[:, s * TPS + j, :]
                    tt(a, ps_y[:, 2 + j % 2, :], a, ALU.add).then_inc(sy_read, 1)
                    if rows_step_after_down(s, j):
                        rows_step(*rows_step_after_down(s, j))
                    if s == NS - 1:
                        if j == 0:
                            dve.wait_ge(e_in, 48)
                        split_expert(0, 0, j)
                    if (s, j) == (NS - 1, 0):
                        dve.wait_ge(slot_in, 16)
                        for k in range(2):
                            src = slot_tab[:, :, k]
                            last = nc.vector.tensor_copy(slot_f[:, k, :], src.bitcast(F32) if k else src)
                        last.then_inc(slot_cv, 1)
                    if (s, j) == (NS - 1, 1):
                        dve.wait_ge(slot_tr, 1)
                        nc.vector.tensor_copy(slot_w[:], ps_u[:, 1, ETAB:2 * ETAB])
                        nc.vector.tensor_copy(slot_tok[:], ps_u[:, 1, 0:ETAB]).then_inc(slot_ok, 1)
            through(dve, sh_over, 5)

            for e in range(1, E):
                dve.wait_ge(e_in, 48 * (e + 1))
                if e >= 2:
                    tiles = dve.value_load(last_tile[0:1, e:e + 1], min_val=0, max_val=SLOT_TILES)
                    dve.wait_ge(ry_done, 1 + tiles)
                for k in range(4):
                    split_expert(e, e % 2, k)

        @block.tensor
        def _(pe):
            mm = nc.tensor.matmul

            def logit_rows(s):
                pe.wait_ge(lgt_cp, s + 1)
                for j in range(TPS):
                    at = (PREP[s] * TPS + j) * 2 * E
                    last = nc.tensor.transpose(ps_u[:, 0, at:at + 2 * E], lg_t[:, j * P:(j + 1) * P],
                                               ident[0:2 * E, 0:2 * E])
                last.then_inc(lgt_done, 1)

            pe.sem_inc(z_done, 2)
            pe.sem_inc(d_done, 2)
            opened(pe, cond_done, y_done, ry_done)
            pe.wait_ge(bd_zero, 1)
            for s in range(NS):
                u = s % 2
                for h in range(2):
                    pe.wait_ge(bd_in[s][h], 16 * TPS)
                pe.wait_ge(x_in_s[u], (s // 2 + 1) * 16)
                for c in range(DC):
                    pe.wait_ge(xt_lo_done, s * DC + c + 1)
                    for j in range(TPS):
                        last = mm(ps_y[:, c, j * P:(j + 1) * P], x_in[u][:, j, c * P:(c + 1) * P],
                                  bd[:, PREP[s] * TPS + j, :], start=True, stop=True)
                    last.then_inc(cond_done, 1)
                if s:
                    logit_rows(s - 1)
                pe.wait_ge(xt_lo_done, 4 + (s + 1) * DC)
                pe.wait_ge(split_small, 6)
                if s:
                    pe.wait_ge(lgt_cp, s)
                    pe.wait_ge(u1_read, s)
                for c in range(DC):
                    mm(ps_h[0:2 * E, 0, :], rw_hl[:, c].rearrange("p k e -> p (k e)"), xt_hi[u][:, c, :],
                       start=(c == 0), stop=False)
                    last = mm(ps_h[0:2 * E, 0, :], rw_hl[:, c].rearrange("p k e -> p (k e)"), xt_lo[u][:, c, :],
                              start=False, stop=(c == DC - 1))
                last.then_inc(lg_done, 1)
                for c in range(DC):
                    mm(ps_h[:, 1, :], u1_hi[:, c, :], xt_hi[u][:, c, :], start=(c == 0), stop=False)
                    mm(ps_h[:, 1, :], u1_hi[:, c, :], xt_lo[u][:, c, :], start=False, stop=False)
                    last = mm(ps_h[:, 1, :], u1_lo[:, c, :], xt_hi[u][:, c, :], start=False, stop=(c == DC - 1))
                last.then_inc(u1_done, 1)
            logit_rows(NS - 1)
            pe.wait_ge(w01_ok, 1)
            pe.wait_ge(u1_read, NS)
            nc.tensor.transpose(ps_h[0:2 * J, 1, 0:P], w01[:].rearrange("p k j -> p (k j)"), ident[:])\
                .then_inc(w01t_done, 1)
            for n in range(2 * NS):
                s, k = n // 2, n % 2
                pe.wait_ge(mexp_ok, n + 1)
                if n >= 4:
                    pe.wait_ge(mt_read, n - 3)
                for j in range(TPS):
                    last = nc.tensor.transpose(mt_bank(n)[:, j * P:(j + 1) * P], mexp[k][:, s * TPS + j, :], ident16[:])
                last.then_inc(mt_done, 1)

            def w_chunk(u, half, c):
                at = half * (WT + ER) + c * P
                return w_hl[u][:, at:at + P]

            def hidden(i, s, v, u):
                pe.wait_ge(w1_lo_done, i + 3)
                pe.wait_ge(h1_done, i + 1)
                chunk = lambda half, c: w_chunk(u, half, c)
                for c in range(DC):
                    mm(ps_h[:, u, :], chunk(0, c), xt_hi[v][:, c, :], start=(c == 0), stop=False)
                    mm(ps_h[:, u, :], chunk(0, c), xt_lo[v][:, c, :], start=False, stop=False)
                    mm(ps_h[:, u, :], chunk(1, c), xt_hi[v][:, c, :], start=False, stop=False)
                if s == 0 and isinstance(i, int):
                    pe.wait_ge(z_ok, 1)
                zb = z_base[:, s * SUP:(s + 1) * SUP]
                mm(ps_h[:, u, :], chunk(0, DC), zb, start=False, stop=False)
                mm(ps_h[:, u, :], chunk(1, DC), zb, start=False, stop=True).then_inc(a_done, 1)

            def second(i, s, u):
                pe.wait_ge(h0_done, i + 1)
                chunk = lambda half, c: w_chunk(u, half, c)
                pe.wait_ge(z_ok, 2 * (s + 1))
                zs = z_step[:, s * SUP:(s + 1) * SUP]
                mm(ps_h[:, u, :], chunk(0, DC), zs, start=False, stop=False, skip_group_check=True)
                mm(ps_h[:, u, :], chunk(1, DC), zs, start=False, stop=True, skip_group_check=True)\
                    .then_inc(z_done, 1)

            def down(i, f, u, half):
                if half == 0:
                    pe.wait_ge(g_done, i + 3)
                kw = dict(start=False, stop=False, skip_group_check=True)
                sl = lambda t: t[:, bass.ds(f, 1), :].rearrange("p a n -> p (a n)")
                for j in range(half * 2, half * 2 + 2):
                    cols = slice(j * P, (j + 1) * P)
                    mm(ps_y[:, j, :], g_hi[u][:, cols], sl(w2_hi), **kw)
                    mm(ps_y[:, j, :], g_hi[u][:, cols], sl(w2_lo), **kw)
                    last = mm(ps_y[:, j, :], g_lo[u][:, cols], sl(w2_hi), **kw)
                if half == 0:
                    a2 = w_hl[1 - u][:, WT - ER:WT + ER]
                    for k, g in ((0, g_hi), (0, g_lo), (1, g1_hi), (1, g1_lo)):
                        mm(ps_u[:, k, :], a2, g[u][:], **kw)
                if half == 1:
                    last.then_inc(d_done, 1)

            def zero_sums(s):
                pe.wait_ge(y_read, 1 + s)
                for j in range(TPS):
                    mm(ps_y[:, j, :], zero16[:, 0:P], zero16[:], start=True, stop=False, skip_group_check=True)
                for k in range(2):
                    mm(ps_u[:, k, :], zero16[:, 0:P], zero16[:], start=True, stop=False, skip_group_check=True)

            def step(i, s, v, f, u):
                hidden(i, s, v, u)
                down(i - 1, f - 1, 1 - u, 0)
                second(i, s, u)
                down(i - 1, f - 1, 1 - u, 1)

            def super_tile(s, v):
                base = s * FT
                hidden(base + 1, s, v, 1)
                second(base, s, 0)
                zero_sums(s)
                down(base, 0, 0, 0)
                second(base + 1, s, 1)
                down(base, 0, 0, 1)
                pe.wait_ge(z_ok, 2 * NS)
                with pe.Fori(1, FT // 2) as m:
                    for u in range(2):
                        step(m * 2 + (base + u), s, v, m * 2 + u, u)
                if s + 1 < NS:
                    if s + 1 >= 2:
                        pe.wait_ge(xt_in[1 - v], 32 * ((s + 1) // 2))
                    hidden(base + FT, s + 1, 1 - v, 0)
                else:
                    pe.wait_ge(w1_lo_done, base + FT + 3)
                down(base + FT - 1, FT - 1, 1, 0)
                down(base + FT - 1, FT - 1, 1, 1)
                pe.wait_ge(z2_ok, s + 1)
                for j in range(TPS):
                    cols = slice(j * P, (j + 1) * P)
                    mm(ps_y[:, j, :], z2_hi[:, cols], b2s_hi[:], start=False, stop=False, skip_group_check=True)
                    mm(ps_y[:, j, :], z2_hi[:, cols], b2s_lo[:], start=False, stop=False, skip_group_check=True)
                    last = mm(ps_y[:, j, :], z2_lo[:, cols], b2s_hi[:], start=False, stop=True, skip_group_check=True)
                last.then_inc(y_done, 1)

            hidden(0, 0, 0, 0)
            for s in range(NS):
                super_tile(s, s % 2)
            through(pe, l0_over, 5)

            def rows_step(s, k):
                u = s % 2
                if k < 2:
                    pe.wait_ge(acc_in[s], 16)
                    pe.wait_ge(bdq_done, 2 * (s + 1))
                    if k == 0 and s:
                        pe.wait_ge(lg1_read, s)
                    for j in (2 * k, 2 * k + 1):
                        if j >= 2:
                            pe.wait_ge(xc_done, s * TPS + j - 1)
                        mm(ps_u[:, j % 2, :], bdq[u][:, j, :], acc[:, s * TPS + j, :], start=True, stop=True)\
                            .then_inc(c1_done, 1)
                elif k < 4:
                    pe.wait_ge(xc_done, (s + 1) * TPS)
                    for c in (2 * k - 4, 2 * k - 3):
                        if c >= 2:
                            pe.wait_ge(xs_lo_done, s * DC + c - 1)
                        for j in range(TPS):
                            last = nc.tensor.transpose(ps_u[:, c % 2, j * P:(j + 1) * P],
                                                       xc[:, j, c * P:(c + 1) * P], ident[:])
                        last.then_inc(xt1_done, 1)
                elif k == 4:
                    pe.wait_ge(gate_done, 2)
                    pe.wait_ge(xs_lo_done, (s + 1) * DC)
                    for c in range(DC):
                        w = gate_hl[:, c].rearrange("p k e -> p (k e)")
                        mm(ps_u[0:2 * E, 0, :], w, xs_hi[u][:, c, :], start=(c == 0), stop=False)
                        last = mm(ps_u[0:2 * E, 0, :], w, xs_lo[u][:, c, :], start=False, stop=(c == DC - 1))
                    last.then_inc(lg1_done, 1)
                else:
                    pe.wait_ge(lgt1_cp, s + 1)
                    for j in range(TPS):
                        last = nc.tensor.transpose(ps_u[:, 1, j * 2 * E:(j + 1) * 2 * E], lgt1[:, j * P:(j + 1) * P],
                                                   ident[0:2 * E, 0:2 * E])
                    last.then_inc(lgt1_done, 1)

            def gate_up_shared(s, q):
                u, i, cols = s % 2, s * SH + q, slice(q * P, (q + 1) * P)
                if i >= 2:
                    pe.wait_ge(mul_done, i - 1)
                for k, o in ((0, ps_h[:, q % 2, :]), (1, ps_y[:, q % 2, :])):
                    for c in range(DC):
                        if i == 0 and k == 0:
                            pe.wait_ge(sg_lo_done, c + 1)
                        mm(o, sg_hi[:, c, k, cols], xs_hi[u][:, c, :], start=(c == 0), stop=False)
                        mm(o, sg_hi[:, c, k, cols], xs_lo[u][:, c, :], start=False, stop=False)
                        last = mm(o, sg_lo[:, c, k, cols], xs_hi[u][:, c, :], start=False, stop=(c == DC - 1))
                last.then_inc(gu_done, 1)

            def down_shared(s, j):
                if s == 0 and j == 0:
                    pe.wait_ge(sd_lo_done, SH // 2)
                if s * TPS + j >= 2:
                    pe.wait_ge(sy_read, s * TPS + j - 1)
                cols = slice(j * P, (j + 1) * P)
                o = ps_y[:, 2 + j % 2, :]
                for q in range(SH):
                    if j == 0:
                        pe.wait_ge(slo_done, s * SH + q + 1)
                    mm(o, sh_hi[:, q, cols], sd_hi[:, q, :], start=(q == 0), stop=False)
                    mm(o, sh_hi[:, q, cols], sd_lo[:, q, :], start=False, stop=False)
                    last = mm(o, sh_lo[:, q, cols], sd_hi[:, q, :], start=False, stop=(q == SH - 1))
                last.then_inc(sy_done, 1)

            for k in range(ROWS_STEPS):
                rows_step(0, k)
            for s in range(NS):
                for q in range(SH):
                    gate_up_shared(s, q)
                    if rows_step_after_gate_up(s, q):
                        rows_step(*rows_step_after_gate_up(s, q))
                    if (s, q) == (NS - 2, ROWS_STEPS - 1):
                        pe.wait_ge(mask_ok, 1)
                        mask_row = mask16[:].rearrange("p j e -> p (j e)")
                        mm(ps_u[:, 0, 0:P], tri[:], mask_row, start=True, stop=True)
                        mm(ps_u[:, 0, P:2 * P], ones16[:], mask_row, start=True, stop=True).then_inc(cnt_done, 1)
                for j in range(TPS):
                    down_shared(s, j)
                    if rows_step_after_down(s, j):
                        rows_step(*rows_step_after_down(s, j))
                    if (s, j) == (NS - 1, 0):
                        pe.wait_ge(slot_cv, 1)
                        for k in range(2):
                            last = nc.tensor.transpose(ps_u[:, 1, k * ETAB:(k + 1) * ETAB], slot_f[:, k, :],
                                                       ident[0:ETAB, 0:ETAB])
                        last.then_inc(slot_tr, 1)
            through(pe, sh_over, 5)

            pe.wait_ge(etab_ok, 1)

            def expert(t):
                e = pe.value_load(etab[0:1, bass.ds(t, 1)], min_val=0, max_val=E - 1)
                return e, e % 2

            def turn_x(t, n):
                pe.wait_ge(xg_in[n[0]], n[1])
                if not n[2]:
                    pe.wait_ge(xg_f_done, t)
                for c in range(DC):
                    last = nc.tensor.transpose(ps_u[:, 0, c * P:(c + 1) * P], xg[n[0]][:, c * P:(c + 1) * P], ident[:])
                last.then_inc(xgt_done, 1)

            def gate_or_up(t, u, eb, k):
                e, b = eb
                if k == 0:
                    pe.wait_ge(e_done, e + 1)
                    pe.wait_ge(xg_hi_done, t + 1)
                    if not isinstance(t, int) or t >= 2:
                        pe.wait_ge(ru_done, t - 1)
                o = (ps_h, ps_y)[k][:, u, 0:H1]
                w = lambda half, c: half[:, bass.ds(b, 1), c, k * H1:(k + 1) * H1].rearrange("p a n -> p (a n)")
                for c in range(DC):
                    mm(o, xg_hi[:, c, :], w(eg_hi, c), start=(c == 0), stop=False)
                    mm(o, xg_hi[:, c, :], w(eg_lo, c), start=False, stop=False)
                if k == 0:
                    pe.wait_ge(xg_lo_done, t + 1)
                for c in range(DC):
                    last = mm(o, xg_lo[:, c, :], w(eg_hi, c), start=False, stop=(c == DC - 1))
                last.then_inc((rgate_done, rup_done)[k], 1)

            def turn_g(t):
                pe.wait_ge(rg_done, t + 1)
                if not isinstance(t, int) or t:
                    pe.wait_ge(rgt_f_done, t)
                for c in range(HC):
                    last = nc.tensor.transpose(ps_u[:, 1, c * P:(c + 1) * P], rg[:, c * P:(c + 1) * P], ident[:])
                last.then_inc(rgt_done, 1)

            def down_routed(t, u, eb):
                e, b = eb
                pe.wait_ge(rgt_hi_done, t + 1)
                if not isinstance(t, int) or t >= 2:
                    pe.wait_ge(ry_cp, t - 1)
                w = lambda half, c, k: half[0:k, bass.ds(b, 1), c, :].rearrange("p a n -> p (a n)")
                o = ps_y[:, 2 + u, :]
                for c in range(HC):
                    k = min(P, H1 - c * P)
                    mm(o, rgt_hi[0:k, c, :], w(ed_hi, c, k), start=(c == 0), stop=False)
                    mm(o, rgt_hi[0:k, c, :], w(ed_lo, c, k), start=False, stop=False)
                pe.wait_ge(rgt_lo_done, t + 1)
                for c in range(HC):
                    k = min(P, H1 - c * P)
                    last = mm(o, rgt_lo[0:k, c, :], w(ed_hi, c, k), start=False, stop=(c == HC - 1))
                last.then_inc(ry_done, 1)

            def slot_tile(t, u, n, nxt=True, nxt2=True):
                if nxt:
                    after = expert(t + 1)
                    gate_or_up(t + 1, 1 - u, after, 0)
                turn_g(t)
                if nxt:
                    gate_or_up(t + 1, 1 - u, after, 1)
                if nxt2:
                    turn_x(t + 2, (u, n, False))
                down_routed(t, u, expert(t))

            pe.wait_ge(rg_zero, 1)
            turn_x(0, (0, 16, True))
            first = expert(0)
            gate_or_up(0, 0, first, 0)
            gate_or_up(0, 0, first, 1)
            turn_x(1, (1, 16, False))
            slot_tile(0, 0, 32)
            slot_tile(1, 1, 32)
            with pe.Fori(1, SLOT_TILES // 2 - 1) as m:
                for u in range(2):
                    slot_tile(m * 2 + u, u, (m + 2) * 16)
            for t in range(SLOT_TILES - 3, SLOT_TILES):
                slot_tile(t, t % 2, (t // 2 + 2) * 16, t + 1 < SLOT_TILES, t + 2 < SLOT_TILES)


_OUT = (32, 64, 512)


def layouts(v):
    import numpy as np
    g = {k: np.asarray(a) for k, a in v.items()}
    c = np.ascontiguousarray
    f_tiles = 16
    w1t = g["L0_ffn_W1"].T.reshape(4, 128, f_tiles, 128).transpose(2, 1, 0, 3)
    b1t = g["L0_ffn_B1"].transpose(0, 2, 1).reshape(64, f_tiles, 128).transpose(1, 0, 2)
    w1b = np.concatenate([w1t, np.concatenate([b1t, b1t], 1)[:, :, None, :]], 2).reshape(f_tiles, 128, 640)
    bias = g["L0_ffn_b1"].reshape(f_tiles, 128, 1)
    a2t = np.roll(g["L0_ffn_A2"].reshape(64, f_tiles, 128).transpose(1, 2, 0), 1, 0)
    w1b = np.concatenate([w1b, a2t, bias, bias], 2)
    b2t = g["L0_ffn_B2"].transpose(0, 2, 1).reshape(64, 512)
    return dict(
        x=c(g["x"].reshape(2048, 512)),
        itok0=c(g["itok_B_1_198"].reshape(1, 32)),
        itok1=c(g["itok_B_0_7"].reshape(1, 32)),
        side=c(g["fside_8xS_0"].reshape(512, 1)),
        cond0=c(g["L0_cond_weights"].reshape(200 * 64, 64)),
        router0=c(np.concatenate([g["L0_ffn_W_r"], g["L0_ffn_A1"].reshape(64, 512)], 0).T),
        router0_b=c(g["L0_ffn_b_r"].reshape(1, 8)),
        w1b=c(w1b),
        w2=c(g["L0_ffn_W2"].T),
        b2=c(g["L0_ffn_b2"].reshape(1, 512)),
        b2s=c(np.concatenate([b2t, b2t], 0)),
        cond1=c(g["L1_cond_weights"].reshape(8 * 64, 64)),
        gate1=c(g["L1_ffn_gate_w"]),
        wgu1=c(np.concatenate([g["L1_ffn_w_gate"], g["L1_ffn_w_up"]], 2)),
        wdn1=c(g["L1_ffn_w_down"]),
        sgu1=c(np.concatenate([g["L1_ffn_sw_gate"], g["L1_ffn_sw_up"]], 1)),
        sdn1=c(g["L1_ffn_sw_down"]),
    )


def kernel(**inputs):
    import concourse.bacc as _bacc
    from concourse.bass_utils import run_bass_kernel_spmd as _run

    nc = _bacc.Bacc("TRN2", target_bir_lowering=False, num_devices=1)
    arrays, args = {}, []
    for name, a in layouts(inputs).items():
        arrays[f"in_{name}"] = a
        args.append(nc.dram_tensor(f"in_{name}", a.shape, mybir.dt.from_np(a.dtype), kind="ExternalInput").ap())
    out = nc.dram_tensor("out_x", (2048 + P, 512), F32, kind="ExternalOutput").ap()
    adaln_ffn(nc, *args, out)
    r = _run(nc, [arrays], core_ids=[0])
    return r.results[0]["out_x"][:2048].reshape(_OUT)
```

```python
from contextlib import ExitStack

import concourse.bass as bass
from concourse import mybir

F32 = mybir.dt.float32
F32R = mybir.dt.float32r
BF16 = mybir.dt.bfloat16
I32 = mybir.dt.int32
ALU = mybir.AluOpType
ACT = mybir.ActivationFunctionType
AX = mybir.AxisListType

P = 128
D = 512
DC = D // P
SEQ = 64
E = 8
SUP = 512
TPS = SUP // P
LORA_SCALE = 2.0


def adaln_ffn(nc, x, itok0, itok1, side, cond0, router0, router0_b, w1b, w2, b2, b2s,
              cond1, gate1, wgu1, wdn1, sgu1, sdn1, out):
    N = x.shape[0]
    J = N // P
    NS = N // SUP
    FT = w1b.shape[0]
    ER = router0.shape[1] - E
    R = ER // E
    STEPS = NS * FT
    H1 = wdn1.shape[1]
    HC = -(-H1 // P)
    HP = sdn1.shape[0]
    SH = -(-HP // P)
    SLOT_TILES = 2 * J + E - 1
    ETAB = SLOT_TILES + 1
    WINDOW = 5
    assert STEPS == 4 * J
    PREP = [*range(2, NS), 0, 1]
    WT = (DC + 1) * P + ER
    WROW = w1b.shape[2]

    scr = lambda name, shape, dt=F32: nc.dram_tensor(name, shape, dt, kind="Internal").ap()
    xt_hi_d = scr("xt_hi_d", (NS - 2, P, DC * SUP))
    xt_lo_d = scr("xt_lo_d", (NS - 2, P, DC * SUP))
    wrow_d = scr("wrow_d", (2 * J, P))
    xc_d = scr("xc_d", (N + P, D))
    slot_d = scr("slot_d", (ETAB * P, 2), I32)
    x1_d = scr("x1_d", (N, D))

    with ExitStack() as top:
        def sem(name):
            return top.enter_context(nc.semaphore(name))

        def tensors(stack):
            return lambda name, shape, dt=F32: stack.enter_context(nc.sbuf_tensor(name, shape, dt))

        psum = lambda name, shape, dt=F32: top.enter_context(nc.psum_tensor(name, shape, dt))

        ps_h = psum("ps_h", [P, 2, SUP])
        ps_y = psum("ps_y", [P, TPS, D])
        ps_u = psum("ps_u", [P, 2, SUP])

        sb = tensors(top)
        ident = sb("ident", [P, P])
        zero16 = sb("zero16", [P, SUP], BF16)
        rev8 = sb("rev8", [P, E])
        tri = sb("tri", [P, P], BF16)
        ones16 = sb("ones16", [P, P], BF16)
        tok_id = sb("tok_id", [P, J], I32)
        ident16 = sb("ident16", [P, P], BF16)
        cw1 = sb("cw1", [P, J, SEQ])
        side_col = sb("side_col", [P, J])
        bdq = [sb(f"bdq{u}", [P, TPS, P]) for u in range(2)]
        it_row = [sb(f"it_row{k}", [1, 2 * J], I32) for k in range(2)]

        l0 = ExitStack()
        sb = tensors(l0)
        w2_hi = sb("w2_hi", [P, FT, D], F32R)
        w2_lo = sb("w2_lo", [P, FT, D], F32R)
        stage = ExitStack()
        w2_raw = tensors(stage)("w2_raw", [P, FT // 2, D])
        stage.close()
        z_base = sb("z_base", [P, N], F32R)
        z_step = sb("z_step", [P, N], F32R)
        m_base = sb("m_base", [P, N], BF16)
        m_step = sb("m_step", [P, N], BF16)
        xt_hi, xt_lo = zip(*[[sb(f"xt_{half}{u}", [P, DC, SUP], F32R) for half in ("hi", "lo")]
                             for u in range(2)])
        w_raw = [sb(f"w_raw{u}", [P, WROW]) for u in range(2)]
        w_hl = [sb(f"w_hl{u}", [P, 2 * WT], F32R) for u in range(2)]
        b2s_hi = sb("b2s_hi", [P, D], F32R)
        b2s_lo = sb("b2s_lo", [P, D], F32R)
        b2_rows = sb("b2_rows", [P, D])
        bias1 = [sb(f"bias1{u}", [P, 1]) for u in range(2)]
        rb_rows = sb("rb_rows", [P, E])
        lg = sb("lg", [P, J, 2, E])
        rt = {n: sb(f"rt_{n}", [P, J, E]) for n in ("l", "p", "q", "oh0", "oh1")}
        rc = {n: sb(f"rc_{n}", [P, J]) for n in ("m", "s")}
        w01 = sb("w01", [P, 2, J])
        wsum = sb("wsum", [P, J])
        w01_t = sb("w01_t", [2 * J, P])

        prep = ExitStack()
        sb = tensors(prep)
        matrices = ExitStack()
        bd = tensors(matrices)("bd", [P, J, P])
        matrices.close()
        mexp = [sb(f"mexp{k}", [P, J, P], BF16) for k in range(2)]
        x_in = [sb(f"x_in{u}", [P, TPS, D]) for u in range(2)]
        u1_raw = sb("u1_raw", [P, DC, P])
        u1_hi = sb("u1_hi", [P, DC, P], F32R)
        u1_lo = sb("u1_lo", [P, DC, P], F32R)
        rw_raw = sb("rw_raw", [P, DC, E])
        rw_hl = sb("rw_hl", [P, DC, 2, E], F32R)
        b2s_raw = sb("b2s_raw", [P, D])
        lg_t = sb("lg_t", [2 * E, SUP])
        u1t = sb("u1t", [P, N])
        zf = [sb(f"zf{u}", [P, SUP]) for u in range(2)]
        prep.close()

        mainp = ExitStack()
        sb = tensors(mainp)
        h0 = [sb(f"h0{u}", [P, SUP]) for u in range(2)]
        h1 = [sb(f"h1{u}", [P, SUP]) for u in range(2)]
        g_hi = [sb(f"g_hi{u}", [P, SUP], F32R) for u in range(2)]
        g_lo = [sb(f"g_lo{u}", [P, SUP], F32R) for u in range(2)]
        g1_hi = [sb(f"g1_hi{u}", [P, SUP], F32R) for u in range(2)]
        g1_lo = [sb(f"g1_lo{u}", [P, SUP], F32R) for u in range(2)]
        wb = sb("wb", [P, 2, 2, SUP])
        xres = sb("xres", [P, TPS, D])
        zz = sb("zz", [P, SUP])
        zq = sb("zq", [P, SUP])
        z2_hi = sb("z2_hi", [P, SUP], F32R)
        z2_lo = sb("z2_lo", [P, SUP], F32R)
        mainp.close()
        l0.close()

        l1 = ExitStack()
        sb = tensors(l1)
        acc = sb("acc", [P, J, D])
        gate_raw = sb("gate_raw", [P, DC, E])
        gate_hl = sb("gate_hl", [P, DC, 2, E], F32R)
        lg1 = sb("lg1", [P, J, 2, E])
        q1 = {n: sb(f"q1_{n}", [P, J, E]) for n in ("l", "p", "q", "oh0", "oh1")}
        c1 = {n: sb(f"c1_{n}", [P, J]) for n in ("m", "s")}
        w1k = sb("w1k", [P, 2, J])
        pos_i = sb("pos_i", [P, 2, J], I32)
        cnt = [sb(f"cnt{u}", [P, J, E]) for u in range(2)]
        rank = sb("rank", [P, J, E])
        mask16 = sb("mask16", [P, J, E], BF16)
        ex = {n: sb(f"ex_{n}", [P, E]) for n in ("t", "a", "b")}
        ex_i = sb("ex_i", [P, E], I32)
        etile = sb("etile", [P, ETAB])
        etab3 = sb("etab3", [P, ETAB, E])
        etab_f = sb("etab_f", [P, ETAB])
        etab_g = sb("etab_g", [P, ETAB])
        etab = sb("etab", [P, ETAB], I32)
        last_tile = sb("last_tile", [P, E + 2], I32)
        pay = sb("pay", [P, 2, J, 2], I32)
        slot_tab = sb("slot_tab", [ETAB, P, 2], I32)
        slot_f = sb("slot_f", [ETAB, 2, P])
        slot_tok = sb("slot_tok", [P, ETAB], I32)
        slot_w = sb("slot_w", [P, ETAB])

        shared = ExitStack()
        sb = tensors(shared)
        sg_hi = sb("sg_hi", [P, DC, 2, SH * P], F32R)
        sg_lo = sb("sg_lo", [P, DC, 2, SH * P], F32R)
        s_raw = [sb(f"s_raw{u}", [P, 2 * SH * P]) for u in range(2)]
        xc = sb("xc", [P, TPS, D])
        xs_hi = [sb(f"xs_hi{u}", [P, DC, SUP], F32R) for u in range(2)]
        xs_lo = [sb(f"xs_lo{u}", [P, DC, SUP], F32R) for u in range(2)]
        sd_hi = sb("sd_hi", [P, SH, D], F32R)
        sd_lo = sb("sd_lo", [P, SH, D], F32R)
        sh_s = sb("sh_s", [P, SUP])
        sh_g = sb("sh_g", [P, SUP])
        sh_hi = sb("sh_hi", [P, SH, SUP], F32R)
        sh_lo = sb("sh_lo", [P, SH, SUP], F32R)
        lgt1 = sb("lgt1", [2 * E, SUP])
        shared.close()

        routed = ExitStack()
        sb = tensors(routed)
        eg_hi = sb("eg_hi", [P, 2, DC, 2 * H1], F32R)
        eg_lo = sb("eg_lo", [P, 2, DC, 2 * H1], F32R)
        xg = [sb(f"xg{u}", [P, D]) for u in range(2)]
        e_raw = sb("e_raw", [P, DC * 2 * H1 + HC * D])
        ed_hi = sb("ed_hi", [P, 2, HC, D], F32R)
        ed_lo = sb("ed_lo", [P, 2, HC, D], F32R)
        xg_hi = sb("xg_hi", [P, DC, P], F32R)
        xg_lo = sb("xg_lo", [P, DC, P], F32R)
        xg_f = sb("xg_f", [P, DC * P])
        rs = sb("rs", [P, H1])
        ru = sb("ru", [P, H1])
        rg = sb("rg", [P, HC * P])
        xg += [sb(f"xg{u}", [P, D]) for u in range(2, 4)]
        rgt_hi = sb("rgt_hi", [P, HC, P], F32R)
        rgt_lo = sb("rgt_lo", [P, HC, P], F32R)
        rgt_f = sb("rgt_f", [P, HC * P])
        yt = [sb(f"yt{u}", [P, D]) for u in range(2)]
        routed.close()
        l1.close()

        const_set = sem("const_set")
        small_in = sem("small_in")
        it_in = sem("it_in")
        bd_in = [[sem(f"bd_in{s}{h}") for h in range(2)] for s in range(NS)]
        lgt_done = sem("lgt_done")
        lgt_cp = sem("lgt_cp")
        u1_done = sem("u1_done")
        u1_read = sem("u1_read")
        w01t_done = sem("w01t_done")
        mexp_ok = sem("mexp_ok")
        mt_done = sem("mt_done")
        mt_read = sem("mt_read")
        z_hi = sem("z_hi")
        z_ok = sem("z_ok")
        warm = sem("warm")
        bd_zero = sem("bd_zero")
        split_small = sem("split_small")
        x_in_s = [sem(f"x_in_s{u}") for u in range(2)]
        cond_done = sem("cond_done")
        xt_hi_done = sem("xt_hi_done")
        xt_lo_done = sem("xt_lo_done")
        xt_st = [sem(f"xt_st{u}") for u in range(2)]
        lg_done = sem("lg_done")
        lu_done = sem("lu_done")
        rch = sem("rch")
        r_max = sem("r_max")
        r_exp = sem("r_exp")
        w01_ok = sem("w01_ok")
        wt_sb = sem("wt_sb")
        wrow_st = sem("wrow_st")
        w2_in = [sem(f"w2_in{u}") for u in range(FT // 2)]
        w2_hi_done = sem("w2_hi_done")
        w2_lo_done = sem("w2_lo_done")
        w1_in = [sem(f"w1_in{u}") for u in range(2)]
        w1_hi_done = sem("w1_hi_done")
        w1_lo_done = sem("w1_lo_done")
        xt_in = [sem(f"xt_in{u}") for u in range(2)]
        wb_in = [sem(f"wb_in{u}") for u in range(2)]
        xres_in = sem("xres_in")
        x1_st = sem("x1_st")
        a_done = sem("a_done")
        z_done = sem("z_done")
        h0_done = sem("h0_done")
        h1_done = sem("h1_done")
        gch = sem("gch")
        g_done = sem("g_done")
        d_done = sem("d_done")
        z2_ok = sem("z2_ok")
        y_done = sem("y_done")
        y_read = sem("y_read")
        ech = sem("ech")
        xb_done = sem("xb_done")

        l0_over = sem("l0_over")
        cw1_in = [sem(f"cw1_in{h}") for h in range(2)]
        gate_in = sem("gate_in")
        gate_done = sem("gate_done")
        acc_in = [sem(f"acc_in{s}") for s in range(NS)]
        bdq_zero = sem("bdq_zero")
        bdq_done = sem("bdq_done")
        c1_done = sem("c1_done")
        xc_done = sem("xc_done")
        xc_st = sem("xc_st")
        xt1_done = sem("xt1_done")
        xs_hi_done = sem("xs_hi_done")
        xs_lo_done = sem("xs_lo_done")
        lg1_done = sem("lg1_done")
        lgt1_cp = sem("lgt1_cp")
        lgt1_done = sem("lgt1_done")
        lg1_read = sem("lg1_read")
        r1_max = sem("r1_max")
        r1_exp = sem("r1_exp")
        mask_ok = sem("mask_ok")
        cnt_done = sem("cnt_done")
        pos_ok = sem("pos_ok")
        etab_ok = sem("etab_ok")
        slot_set = sem("slot_set")
        slot_z_st = sem("slot_z_st")
        zero_st = sem("zero_st")
        slot_st = sem("slot_st")
        slot_in = sem("slot_in")
        slot_cv = sem("slot_cv")
        slot_tr = sem("slot_tr")
        slot_ok = sem("slot_ok")
        s_in = [sem(f"s_in{u}") for u in range(2)]
        s_hi_done = sem("s_hi_done")
        sg_lo_done = [sem(f"sg_lo_done{u}") for u in range(2)]
        sd_lo_done = sem("sd_lo_done")
        pad_done = sem("pad_done")
        gu_done = sem("gu_done")
        sil_done = sem("sil_done")
        mul_done = sem("mul_done")
        shi_done = sem("shi_done")
        slo_done = sem("slo_done")
        sy_done = sem("sy_done")
        sy_read = sem("sy_read")
        out_st = sem("out_st")
        e_in = sem("e_in")
        e_ch = sem("e_ch")
        e_done = sem("e_done")
        xg_in = [sem(f"xg_in{u}") for u in range(4)]
        xgt_done = sem("xgt_done")
        xg_hi_done = sem("xg_hi_done")
        xg_lo_done = sem("xg_lo_done")
        rgate_done = sem("rgate_done")
        rup_done = sem("rup_done")
        rs_done = sem("rs_done")
        ru_done = sem("ru_done")
        xg_f_done = sem("xg_f_done")
        rgt_f_done = sem("rgt_f_done")
        rg_zero = sem("rg_zero")
        rg_done = sem("rg_done")
        rgt_done = sem("rgt_done")
        rgt_hi_done = sem("rgt_hi_done")
        rgt_lo_done = sem("rgt_lo_done")
        ry_done = sem("ry_done")
        ry_cp = sem("ry_cp")
        y_st = sem("y_st")

        def opened(eng, *sems, by=1):
            for which in sems:
                eng.sem_inc(which, by)

        def leave(eng, which):
            eng.drain().then_inc(which, 1)

        def through(eng, which, count):
            leave(eng, which)
            eng.wait_ge(which, count)

        block = top.enter_context(nc.Block())
        G_OPS = 6

        ROWS_STEPS = 6
        ROUTE_AT = ROWS_STEPS - TPS - 1

        def rows_step_after_gate_up(s, q):
            k = q if s == 0 else q + TPS
            return (s + 1, k) if s + 1 < NS and k < ROWS_STEPS else None

        def rows_step_after_down(s, j):
            return (s + 2, j) if s + 2 < NS else None

        def mt_bank(n):
            return ps_y[:, n % 4, 0:SUP // 2].bitcast(BF16)

        def shared_halves(n):
            raw = s_raw[n % 2]
            if n < DC:
                return tuple(t[:, n].rearrange("p k n -> p (k n)") for t in (sg_hi, sg_lo)) + (raw[:],)
            q = 2 * (n - DC)
            return tuple(t[:, q:q + 2, :].rearrange("p q n -> p (q n)") for t in (sd_hi, sd_lo)) + (raw[:, 0:2 * D],)

        def load_matrix(eng, dst, k, width, which, j, h):
            table = (cond0, cond1)[k]
            off = h * SEQ if width == P else 0
            b = eng.value_load(it_row[k][0:1, bass.ds(j * 2 + h, 1)], min_val=0, max_val=table.shape[0] // SEQ - 1)
            eng.dma_start(dst[h * SEQ:(h + 1) * SEQ, bass.ds(j, 1), off:off + SEQ]
                          .rearrange("p a n -> p (a n)"), table[bass.ds(b * SEQ, SEQ), :]).then_inc(which, 16)
            if k == 1:
                eng.dma_start(side_col[h * SEQ:(h + 1) * SEQ, bass.ds(j, 1)],
                              side[bass.ds(b * SEQ, SEQ), :]).then_inc(which, 16)

        @block.sync
        def _(sp):
            opened(sp, x1_st, by=16)
            for k, itok in enumerate((itok0, itok1)):
                sp.dma_start(it_row[k][:], itok).then_inc(it_in, 16)

            def load_x(n):
                s = PREP[n]
                sp.dma_start(x_in[n % 2][:], x[s * SUP:(s + 1) * SUP, :].rearrange("(j p) n -> p j n", p=P))\
                    .then_inc(x_in_s[n % 2], 16)

            def load_bd(n):
                with sp.Fori(PREP[n] * TPS, (PREP[n] + 1) * TPS) as j:
                    load_matrix(sp, bd, 0, P, bd_in[n][0], j, 0)

            def load_w2(f):
                sp.wait_ge(w2_lo_done, f - FT // 2 + 1)
                sp.dma_start(w2_raw[:, f % (FT // 2), :], w2[f * P:(f + 1) * P, :])\
                    .then_inc(w2_in[f % (FT // 2)], 16)

            def load_w1(i, f, u):
                sp.wait_ge(w1_lo_done, i + 1)
                sp.dma_start(w_raw[u][:],
                             w1b[bass.ds(f, 1)].rearrange("a p n -> p (a n)")).then_inc(w1_in[u], 16)

            load_x(0)
            sp.wait_ge(it_in, 32)
            sp.wait_ge(bd_zero, 1)
            load_bd(0)
            load_x(1)
            load_bd(1)
            for n in range(NS):
                if n == 1:
                    load_w1(0, 0, 0)
                    load_w1(1, 1, 1)
                if n + 2 < NS:
                    sp.wait_ge(cond_done, 1 + (n + 1) * DC)
                    load_x(n + 2)
                    sp.wait_ge(xt_lo_done, 4 + (n + 1) * DC)
                    for half, dst in ((xt_hi, xt_hi_d), (xt_lo, xt_lo_d)):
                        sp.dma_start(dst[PREP[n] - 2], half[n % 2][:].rearrange("p c n -> p (c n)").bitcast(F32))\
                            .then_inc(xt_st[n % 2], 16)
                    load_bd(n + 2)
                if n == 1:
                    load_w2(FT // 2)
                    load_w2(FT // 2 + 1)
            for f in range(FT // 2 + 2, FT):
                load_w2(f)

            sp.wait_ge(wt_sb, 1)
            sp.dma_start(wrow_d, w01_t[:]).then_inc(wrow_st, 16)
            sp.wait_ge(wrow_st, 16)

            def load_weights(s):
                for k in range(2):
                    sp.dma_start(wb[:, s % 2, k, :],
                                 wrow_d[k * J + s * TPS:k * J + (s + 1) * TPS, :].rearrange("(o j) p -> o (j p)", o=1)
                                 .partition_broadcast(P)).then_inc(wb_in[s % 2], 16)

            def load_super(s):
                for half, src in ((xt_hi, xt_hi_d), (xt_lo, xt_lo_d)):
                    sp.dma_start(half[s % 2][:].rearrange("p c n -> p (c n)").bitcast(F32), src[s - 2])\
                        .then_inc(xt_in[s % 2], 16)

            def load_acc(n):
                sp.dma_start(acc[:, n * TPS:(n + 1) * TPS, :],
                             x1_d[n * SUP:(n + 1) * SUP, :].rearrange("(j p) n -> p j n", p=P)).then_inc(acc_in[n], 16)

            def store_x1(s):
                sp.wait_ge(y_read, (s + 1) * TPS)
                sp.dma_start(x1_d[s * SUP:(s + 1) * SUP, :].rearrange("(j p) n -> p j n", p=P), xres[:])\
                    .then_inc(x1_st, 16)

            sp.wait_ge(u1_done, NS)
            load_weights(0)
            load_weights(1)
            for u in range(2):
                sp.wait_ge(xt_st[u], 32 * (NS // 2 - 1))
            for s in range(NS):
                for u in range(2):
                    load_w1(s * FT + 2 + u, 2 + u, u)
                if s:
                    store_x1(s - 1)

                def load_w1_pair(m):
                    for u in range(2):
                        load_w1(m * 2 + (s * FT + 2 + u), (m * 2 + 2 + u) % FT, u)
                with sp.Fori(1, FT // 4) as m:
                    load_w1_pair(m)
                if s == 0:
                    sp.wait_ge(z_ok, 2 * NS)
                    sp.wait_ge(u1_read, NS)
                    sp.wait_ge(lgt_done, NS)
                sp.wait_ge(x1_st, 16 + 16 * s)
                sp.dma_start(xres[:], x[s * SUP:(s + 1) * SUP, :].rearrange("(j p) n -> p j n", p=P))\
                    .then_inc(xres_in, 16)
                if s and s + 1 < NS:
                    sp.wait_ge(g_done, 2 + s * FT)
                    load_super(s + 1)
                    load_weights(s + 1)
                with sp.Fori(FT // 4, FT // 2) as m:
                    load_w1_pair(m)
            sp.wait_ge(d_done, 2 + STEPS)
            sp.wait_ge(x1_st, 16 + 16 * (NS - 1))
            for n in range(2):
                load_acc(n)
            sp.dma_start(gate_raw[:], gate1.rearrange("(c p) n -> p c n", p=P)).then_inc(gate_in, 16)
            leave(sp, l0_over)
            store_x1(NS - 1)
            sp.wait_ge(l0_over, 5)

            zero32 = zero16[:].bitcast(F32)
            for dst in (xc_d, out):
                for h in range(2):
                    sp.dma_start(dst[N:N + P, h * (D // 2):(h + 1) * (D // 2)], zero32).then_inc(zero_st, 16)
            sp.wait_ge(slot_set, 3)
            sp.dma_start(slot_d.rearrange("(t p) o -> t p o", p=P), slot_tab[:]).then_inc(slot_z_st, 16)
            for s in range(NS):
                if s == 1:
                    sp.wait_ge(x1_st, 16 + 16 * NS)
                if s in (1, 2):
                    load_acc(s + 1)
                sp.wait_ge(xc_done, (s + 1) * TPS)
                sp.dma_start(xc_d[s * SUP:(s + 1) * SUP, :].rearrange("(j p) n -> p j n", p=P), xc[:])\
                    .then_inc(xc_st, 16)

            def load_expert(e):
                if e:
                    sp.wait_ge(e_done, e)
                full = (H1 // P) * P
                gu = DC * 2 * H1
                sp.dma_start(e_raw[:, 0:gu].rearrange("p (c n) -> p c n", c=DC),
                             wgu1[e].rearrange("(c p) n -> p c n", p=P)).then_inc(e_in, 16)
                sp.dma_start(e_raw[:, gu:gu + full // P * D].rearrange("p (c n) -> p c n", n=D),
                             wdn1[e, 0:full, :].rearrange("(c p) n -> p c n", p=P)).then_inc(e_in, 16)
                sp.dma_start(e_raw[0:H1 - full, gu + full // P * D:], wdn1[e, full:H1, :]).then_inc(e_in, 16)

            sp.wait_ge(sd_lo_done, SH // 2)
            sp.wait_ge(xt1_done, DC * NS)
            sp.wait_ge(xc_st, 16 * NS)
            sp.wait_ge(xs_lo_done, DC * NS)
            load_expert(0)

            def store_acc(s):
                sp.wait_ge(sy_read, (s + 1) * TPS)
                sp.dma_start(out[s * SUP:(s + 1) * SUP, :].rearrange("(j p) n -> p j n", p=P),
                             acc[:, s * TPS:(s + 1) * TPS, :]).then_inc(out_st, 16)
            for s in range(NS - 2):
                store_acc(s)
            sp.wait_ge(slot_st, 16 * 2 * J)
            sp.dma_start(slot_tab[:], slot_d.rearrange("(t p) o -> t p o", p=P)).then_inc(slot_in, 16)
            for s in range(NS - 2, NS):
                store_acc(s)
            for e in range(1, E):
                load_expert(e)
            sp.wait_ge(out_st, 16 * NS)
            sp.wait_ge(zero_st, 16 * 4)
            sp.wait_ge(y_st, 16 * SLOT_TILES)

        @block.gpsimd
        def _(pool):
            pool.sem_inc(w1_lo_done, 2)
            nc.gpsimd.memset(ident[:], 0.0).then_inc(const_set, 1)
            nc.gpsimd.memset(ident16[:], 0.0).then_inc(const_set, 1)
            nc.gpsimd.iota(rev8[:], pattern=[[-1, E]], base=E, channel_multiplier=0,
                           allow_small_or_imprecise_dtypes=True).then_inc(const_set, 1)
            nc.gpsimd.memset(zero16[:], 0.0).then_inc(const_set, 1)
            nc.gpsimd.memset(ones16[:], 1.0).then_inc(const_set, 1)
            nc.gpsimd.iota(tok_id[:], pattern=[[P, J]], base=0, channel_multiplier=1).then_inc(const_set, 1)
            pool.wait_ge(const_set, 6)
            nc.gpsimd.affine_select(out=tri[:], in_=ones16[:], compare_op=ALU.is_gt, fill=0.0,
                                    base=0, pattern=[[1, P]], channel_multiplier=-1).then_inc(const_set, 1)
            nc.gpsimd.affine_select(out=ident[:], in_=ident[:], compare_op=ALU.not_equal, fill=1.0,
                                    base=0, pattern=[[-1, P]], channel_multiplier=1).then_inc(const_set, 1)
            nc.gpsimd.affine_select(out=ident16[:], in_=ident16[:], compare_op=ALU.not_equal, fill=1.0,
                                    base=0, pattern=[[-1, P]], channel_multiplier=1).then_inc(const_set, 1)
            pool.wait_ge(it_in, 32)
            pool.wait_ge(bd_zero, 1)
            for n in range(NS):
                with pool.Fori(PREP[n] * TPS, (PREP[n] + 1) * TPS) as j:
                    load_matrix(pool, bd, 0, P, bd_in[n][1], j, 1)

            def low_w1(i, u):
                pool.wait_ge(w1_hi_done, i + 1)
                nc.gpsimd.tensor_tensor(w_hl[u][:, WT:WT + ER], w_raw[u][:, WT - ER:WT],
                                        w_hl[u][:, WT - ER:WT].bitcast(F32), ALU.subtract)
                nc.gpsimd.tensor_tensor(w_hl[u][:, WT + ER:2 * WT], w_raw[u][:, 0:WT - ER],
                                        w_hl[u][:, 0:WT - ER].bitcast(F32), ALU.subtract).then_inc(w1_lo_done, 1)

            for f in range(FT):
                if f == FT // NS:
                    low_w1(0, 0)
                    low_w1(1, 1)
                pool.wait_ge(w2_hi_done, f + 1)
                nc.gpsimd.tensor_tensor(w2_lo[:, f, :], w2_raw[:, f % (FT // 2), :], w2_hi[:, f, :].bitcast(F32),
                                        ALU.subtract).then_inc(w2_lo_done, 1)
            pool.wait_ge(w2_lo_done, FT)
            for n in range(2 * NS):
                z, cols = (z_base, z_step)[n % 2], slice(n // 2 * SUP, (n // 2 + 1) * SUP)
                pool.wait_ge(z_hi, n + 1)
                nc.gpsimd.tensor_tensor(z[ER:P, cols], zf[n % 2][ER:P, :], z[ER:P, cols].bitcast(F32), ALU.subtract)\
                    .then_inc(z_ok, 1)
            pool.wait_ge(z_ok, 2 * NS)

            def low_and_matrices(j):
                for h in range(2):
                    for u in range(2):
                        low_w1(j * (STEPS // J) + h * 2 + 2 + u, u)
                    load_matrix(pool, cw1, 1, SEQ, cw1_in[h], j, h)
            with pool.Fori(0, J - 2) as j:
                low_and_matrices(j)

            pool.wait_ge(g_done, 2 + (NS - 1) * FT)
            for u in range(2):
                nc.gpsimd.memset(s_raw[u][:].rearrange("p (k n) -> p k n", k=2)[:, :, HP:], 0.0).then_inc(pad_done, 1)
            pool.wait_ge(pad_done, 2)

            def load_s(n):
                u = n % 2
                if n < DC:
                    for k in range(2):
                        pool.dma_start(s_raw[u][:, k * SH * P:k * SH * P + HP],
                                       sgu1[n * P:(n + 1) * P, k * HP:(k + 1) * HP]).then_inc(s_in[u], 16)
                else:
                    q = 2 * (n - DC)
                    rows = min(HP - (q + 1) * P, P)
                    pool.dma_start(s_raw[u][:, 0:D], sdn1[q * P:(q + 1) * P, :]).then_inc(s_in[u], 16)
                    pool.dma_start(s_raw[u][0:rows, D:2 * D], sdn1[(q + 1) * P:(q + 1) * P + rows, :])\
                        .then_inc(s_in[u], 16)
            load_s(0)
            load_s(1)
            with pool.Fori(J - 2, J) as j:
                low_and_matrices(j)
            through(pool, l0_over, 5)

            nc.gpsimd.iota(slot_tab[:, :, 0], pattern=[[1, P]], base=N, channel_multiplier=0).then_inc(slot_set, 1)
            nc.gpsimd.memset(slot_tab[:, :, 1], 0).then_inc(slot_set, 1)
            nc.gpsimd.iota(etile[:], pattern=[[1, ETAB]], base=0, channel_multiplier=0,
                           allow_small_or_imprecise_dtypes=True).then_inc(slot_set, 1)
            for n in range(2, DC + SH // 2):
                if n - 2 < DC and n % 2 == 0:
                    pool.wait_ge(sg_lo_done[0], n // 2)
                elif n - 2 < DC:
                    pool.wait_ge(s_hi_done, n - 1)
                    hi, lo, raw = shared_halves(n - 2)
                    nc.gpsimd.tensor_tensor(lo, raw, hi.bitcast(F32), ALU.subtract).then_inc(sg_lo_done[1], 1)
                    pool.wait_ge(sg_lo_done[1], n // 2)
                else:
                    pool.wait_ge(s_hi_done, n - 1)
                    hi, lo, raw = shared_halves(n - 2)
                    nc.gpsimd.tensor_tensor(lo, raw, hi.bitcast(F32), ALU.subtract).then_inc(sd_lo_done, 1)
                    pool.wait_ge(sd_lo_done, n - 1 - DC)
                if n == DC + SH // 2 - 1:
                    nc.gpsimd.memset(s_raw[n % 2][:], 0.0).then_inc(pad_done, 1)
                    pool.wait_ge(pad_done, 3)
                load_s(n)
            for n in range(DC + SH // 2 - 2, DC + SH // 2):
                pool.wait_ge(s_hi_done, n + 1)
                hi, lo, raw = shared_halves(n)
                nc.gpsimd.tensor_tensor(lo, raw, hi.bitcast(F32), ALU.subtract).then_inc(sd_lo_done, 1)
            pool.wait_ge(slot_z_st, 16)
            pool.wait_ge(pos_ok, 1)
            for k in range(2):
                for j in range(J):
                    pool.indirect_dma_start(out=slot_d, in_=pay[:, k, j, :], in_offset=None,
                                            out_offset=bass.IndirectOffsetOnAxis(ap=pos_i[:, k, j:j + 1], axis=0))\
                        .then_inc(slot_st, 16)

            def gather(t):
                if t >= 4:
                    pool.wait_ge(xgt_done, t - 3)
                pool.indirect_dma_start(out=xg[t % 4][:], out_offset=None, in_=xc_d,
                                        in_offset=bass.IndirectOffsetOnAxis(ap=slot_tok[:, t:t + 1], axis=0))\
                    .then_inc(xg_in[t % 4], 16)

            def scatter_add(t):
                pool.wait_ge(ry_cp, t + 1)
                if t:
                    pool.wait_ge(y_st, 16 * t)
                else:
                    pool.wait_ge(out_st, 16 * NS)
                pool.indirect_dma_start(out=out, in_=yt[t % 2][:], in_offset=None,
                                        out_offset=bass.IndirectOffsetOnAxis(ap=slot_tok[:, t:t + 1], axis=0),
                                        compute_op=ALU.add).then_inc(y_st, 16)

            def x_low(t):
                pool.wait_ge(xg_f_done, t + 1)
                nc.gpsimd.tensor_tensor(xg_lo[:].rearrange("p c n -> p (c n)"), xg_f[:],
                                        xg_hi[:].rearrange("p c n -> p (c n)").bitcast(F32), ALU.subtract)\
                    .then_inc(xg_lo_done, 1)

            def products(t):
                pool.wait_ge(ru_done, t + 1)
                if t:
                    pool.wait_ge(rgt_done, t)
                nc.gpsimd.tensor_tensor(rg[:, 0:H1], rs[:], ru[:], ALU.mult).then_inc(rg_done, 1)

            def g_low(t):
                pool.wait_ge(rgt_f_done, t + 1)
                nc.gpsimd.tensor_tensor(rgt_lo[:].rearrange("p c n -> p (c n)"), rgt_f[:],
                                        rgt_hi[:].rearrange("p c n -> p (c n)").bitcast(F32), ALU.subtract)\
                    .then_inc(rgt_lo_done, 1)

            pool.wait_ge(xc_st, 16 * NS)
            pool.wait_ge(zero_st, 16 * 4)
            pool.wait_ge(slot_ok, 1)
            pool.wait_ge(gu_done, NS * SH)
            gather(0)
            gather(1)
            nc.gpsimd.memset(rg[:, H1:HC * P], 0.0).then_inc(rg_zero, 1)
            x_low(0)
            products(0)
            x_low(1)
            pool.wait_ge(sy_done, NS * TPS)
            for t in range(2, 5):
                gather(t)
            for t in range(SLOT_TILES):
                g_low(t)
                if t + 1 < SLOT_TILES:
                    products(t + 1)
                if t + 2 < SLOT_TILES:
                    x_low(t + 2)
                if t + 5 < SLOT_TILES:
                    gather(t + 5)
                scatter_add(t)

        @block.scalar
        def _(act):
            act.sem_inc(h1_done, 2)
            for dst, src in ((u1_raw[:, :, 0:ER], router0[:, E:E + ER].rearrange("(c p) n -> p c n", p=P)),
                             (u1_raw[:, :, ER:P], router0[:, E:E + ER].rearrange("(c p) n -> p c n", p=P)),
                             (rw_raw[:], router0[:, 0:E].rearrange("(c p) n -> p c n", p=P)),
                             (b2s_raw[:], b2s),
                             (rb_rows[:], router0_b[0:1, :].partition_broadcast(P)),
                             (b2_rows[:], b2[0:1, :].partition_broadcast(P))):
                act.dma_start(dst, src).then_inc(small_in, 16)
            act.wait_ge(x_in_s[0], 16)
            for f in range(FT // 2):
                act.dma_start(w2_raw[:, f, :], w2[f * P:(f + 1) * P, :]).then_inc(w2_in[f], 16)

            def high_w2(f):
                act.wait_ge(w2_in[f % (FT // 2)], 16 * (f // (FT // 2) + 1))
                nc.scalar.copy(w2_hi[:, f, :], w2_raw[:, f % (FT // 2), :]).then_inc(w2_hi_done, 1)

            def high_w1(i, u, n):
                act.wait_ge(w1_in[u], n)
                if not isinstance(i, int):
                    act.wait_ge(d_done, i)
                    act.wait_ge(h1_done, i + 1)
                nc.scalar.copy(bias1[u][:], w_raw[u][:, WT:WT + 1])
                nc.scalar.copy(w_hl[u][:, 0:WT], w_raw[u][:, 0:WT]).then_inc(w1_hi_done, 1)

            for s in range(NS):
                if s >= 2:
                    act.wait_ge(xt_st[s % 2], 32 * (s // 2))
                for c in range(DC):
                    act.wait_ge(cond_done, 1 + s * DC + c + 1)
                    nc.scalar.copy(xt_hi[s % 2][:, c, :], ps_y[:, c, :]).then_inc(xt_hi_done, 1)
                act.wait_ge(lg_done, s + 1)
                act.wait_ge(lgt_done, s)
                nc.scalar.copy(lg_t[:], ps_h[0:2 * E, 0, :]).then_inc(lgt_cp, 1)
                if s == 2:
                    high_w1(0, 0, 16)
                    high_w1(1, 1, 16)
                if s:
                    for f in range((s - 1) * (FT // NS), s * (FT // NS)):
                        high_w2(f)
            for f in range(FT - FT // NS, FT):
                high_w2(f)
            act.wait_ge(r_max, 1)
            nc.scalar.activation(rt["q"][:], rt["l"][:], ACT.Exp).then_inc(r_exp, 1)

            act.wait_ge(w01t_done, 1)
            nc.scalar.copy(w01_t[:], ps_u[0:2 * J, 1, 0:P]).then_inc(wt_sb, 1)
            for n in range(2 * NS):
                s, k = n // 2, n % 2
                act.wait_ge(mt_done, n + 1)
                nc.scalar.copy((m_base, m_step)[k][:, s * SUP:(s + 1) * SUP], mt_bank(n)).then_inc(mt_read, 1)
            nc.scalar.activation(h0[0][:], zero16[:], ACT.Gelu_apprx_tanh).then_inc(warm, 1)
            act.wait_ge(warm, 1)
            with act.Fori(0, NS) as s:
                with act.Fori(0, FT // 2) as m:
                    for u in range(2):
                        i = s * FT + m * 2 + u
                        b = bias1[u][:, 0:1]
                        act.wait_ge(a_done, i + 1)
                        act.wait_ge(g_done, i + 1)
                        nc.scalar.activation(h0[u][:], ps_h[:, u, :], ACT.Gelu_apprx_tanh, bias=b)\
                            .then_inc(h0_done, 1)
                        act.wait_ge(z_done, i + 3)
                        nc.scalar.activation(h1[u][:], ps_h[:, u, :], ACT.Gelu_apprx_tanh, bias=b)\
                            .then_inc(h1_done, 1)
                        high_w1(i + 2, u, (s * (FT // 2) + m + 2) * 16)
            through(act, l0_over, 5)

            def high_s(n):
                u = n % 2
                act.wait_ge(s_in[u], 32 * (n // 2 + 1))
                act.wait_ge(pad_done, 3 if n == DC + SH // 2 - 1 else 2)
                hi, lo, raw = shared_halves(n)
                nc.scalar.copy(hi, raw).then_inc(s_hi_done, 1)

            def rows_step(s, k):
                if k in (2, 3):
                    for c in (2 * k - 4, 2 * k - 3):
                        act.wait_ge(xt1_done, s * DC + c + 1)
                        if s >= 2:
                            act.wait_ge(gu_done, (s - 1) * SH)
                        nc.scalar.copy(xs_hi[s % 2][:, c, :], ps_u[:, c % 2, :]).then_inc(xs_hi_done, 1)
                if k == 4:
                    act.wait_ge(lg1_done, s + 1)
                    if s:
                        act.wait_ge(lgt1_done, s)
                    nc.scalar.copy(lgt1[:], ps_u[0:2 * E, 0, :]).then_inc(lgt1_cp, 1)

            high_s(0)
            high_s(1)
            nc.scalar.activation(c1["m"][:], zero16[:, 0:J], ACT.Silu)
            rows_step(0, 2)
            rows_step(0, 3)
            high_s(2)
            high_s(3)
            rows_step(0, 4)
            for s in range(NS):
                for q in range(SH):
                    i = s * SH + q
                    if i:
                        act.wait_ge(mul_done, i)
                    act.wait_ge(gu_done, i + 1)
                    nc.scalar.activation(sh_s[:], ps_h[:, q % 2, :], ACT.Silu).then_inc(sil_done, 1)
                    if rows_step_after_gate_up(s, q):
                        rows_step(*rows_step_after_gate_up(s, q))
                    if s == 0 and q < SH // 2:
                        high_s(DC + q)
                    if (s, q) == (NS - 2, ROUTE_AT):
                        act.wait_ge(r1_max, 1)
                        nc.scalar.activation(q1["q"][:], q1["l"][:], ACT.Exp).then_inc(r1_exp, 1)
                for j in range(TPS):
                    if rows_step_after_down(s, j):
                        rows_step(*rows_step_after_down(s, j))

            def x_high(t, first=False):
                act.wait_ge(xgt_done, t + 1)
                nc.scalar.copy(xg_hi[:].rearrange("p c n -> p (c n)"), ps_u[:, 0, :]).then_inc(xg_hi_done, 1)
                if not first:
                    act.wait_ge(xg_lo_done, t)
                nc.scalar.copy(xg_f[:], ps_u[:, 0, :]).then_inc(xg_f_done, 1)

            def silu(t, u, first=False):
                if not first:
                    act.wait_ge(rg_done, t)
                act.wait_ge(rgate_done, t + 1)
                nc.scalar.activation(rs[:], ps_h[:, u, 0:H1], ACT.Silu).then_inc(rs_done, 1)

            def up(t, u):
                act.wait_ge(rup_done, t + 1)
                nc.scalar.copy(ru[:], ps_y[:, u, 0:H1]).then_inc(ru_done, 1)

            def g_high(t, first=False):
                act.wait_ge(rgt_done, t + 1)
                nc.scalar.copy(rgt_hi[:].rearrange("p c n -> p (c n)"), ps_u[:, 1, 0:HC * P]).then_inc(rgt_hi_done, 1)
                if not first:
                    act.wait_ge(rgt_lo_done, t)
                nc.scalar.copy(rgt_f[:], ps_u[:, 1, 0:HC * P]).then_inc(rgt_f_done, 1)

            def weigh(t, u, stored):
                if stored is not None:
                    act.wait_ge(y_st, stored)
                act.wait_ge(ry_done, 1 + t + 1)
                nc.scalar.activation(yt[u][:], ps_y[:, 2 + u, :], ACT.Copy, scale=slot_w[:, bass.ds(t, 1)])\
                    .then_inc(ry_cp, 1)

            def copies(t, u, stored, nxt=True, nxt2=True):
                if nxt:
                    silu(t + 1, 1 - u)
                g_high(t, first=stored is None and u == 0)
                if nxt:
                    up(t + 1, 1 - u)
                if nxt2:
                    x_high(t + 2)
                weigh(t, u, stored)
            x_high(0, first=True)
            silu(0, 0, first=True)
            up(0, 0)
            x_high(1)
            act.wait_ge(sy_done, NS * TPS)
            copies(0, 0, None)
            copies(1, 1, None)
            with act.Fori(1, SLOT_TILES // 2 - 1) as m:
                for u in range(2):
                    copies(m * 2 + u, u, (m * 2 + u - 1) * 16)
            for t in range(SLOT_TILES - 3, SLOT_TILES):
                copies(t, t % 2, (t - 1) * 16, t + 1 < SLOT_TILES, t + 2 < SLOT_TILES)

        @block.vector
        def _(dve):
            dve.sem_inc(xt_lo_done, 4)
            dve.sem_inc(lu_done, 1)
            dve.sem_inc(g_done, 2)
            nc.vector.memset(bd[:], 0.0).then_inc(bd_zero, 1)
            for u in range(2):
                nc.vector.memset(bdq[u][:], 0.0).then_inc(bdq_zero, 1)
            dve.wait_ge(const_set, 9)
            dve.wait_ge(small_in, 16 * 6)
            small = ((u1_hi[:], u1_lo[:], u1_raw[:]), (b2s_hi[:], b2s_lo[:], b2s_raw[:]),
                     (rw_hl[:, :, 0, :], rw_hl[:, :, 1, :], rw_raw[:]))
            for hi, lo, raw in small:
                nc.vector.tensor_copy(hi, raw).then_inc(split_small, 1)
            for n, (hi, lo, raw) in enumerate(small):
                dve.wait_ge(split_small, n + 1)
                nc.vector.tensor_tensor(lo, raw, hi.bitcast(F32), ALU.subtract).then_inc(split_small, 1)
            for s in range(NS):
                for c in range(DC):
                    dve.wait_ge(xt_hi_done, s * DC + c + 1)
                    nc.vector.tensor_tensor(xt_lo[s % 2][:, c, :], ps_y[:, c, :], xt_hi[s % 2][:, c, :].bitcast(F32),
                                            ALU.subtract).then_inc(xt_lo_done, 1)
                dve.wait_ge(u1_done, s + 1)
                nc.vector.tensor_copy(u1t[:, PREP[s] * SUP:(PREP[s] + 1) * SUP], ps_h[:, 1, :]).then_inc(u1_read, 1)
            dve.wait_ge(lgt_done, NS)
            nc.vector.tensor_copy(lg[:].rearrange("p j k e -> p (j k e)"), ps_u[:, 0, 0:J * 2 * E]).then_inc(lu_done, 1)

            count = [0]

            def link(ins):
                count[0] += 1
                ins.then_inc(rch, 1)
                dve.wait_ge(rch, count[0])

            def over_e(col):
                return col.unsqueeze(2).to_broadcast([P, J, E])

            tt = nc.vector.tensor_tensor

            def softmax(rt, rc, parts, bias, r_max, r_exp):
                l, p, q, m = rt["l"][:], rt["p"][:], rt["q"][:], rc["m"][:]
                link(tt(p, parts[:, :, 0, :], parts[:, :, 1, :], ALU.add))
                if bias is not None:
                    link(tt(p, p, bias.unsqueeze(1).to_broadcast([P, J, E]), ALU.add))
                link(nc.vector.tensor_reduce(m, p, AX.X, ALU.max))
                tt(l, p, over_e(m), ALU.subtract).then_inc(r_max, 1)
                dve.wait_ge(r_exp, 1)
                link(nc.vector.tensor_reduce(m, q, AX.X, ALU.add))
                link(nc.vector.reciprocal(rc["s"][:], m))
                link(tt(p, q, over_e(rc["s"][:]), ALU.mult))

            def choose(rt, rc, k, w):
                p, q, m, oh = rt["p"][:], rt["q"][:], rc["m"][:], rt[f"oh{k}"][:]
                link(nc.vector.tensor_reduce(w, p, AX.X, ALU.max))
                link(tt(q, p, over_e(w), ALU.is_equal))
                link(tt(q, q, rev8[:].unsqueeze(1).to_broadcast([P, J, E]), ALU.mult))
                link(nc.vector.tensor_reduce(m, q, AX.X, ALU.max))
                link(tt(oh, q, over_e(m), ALU.is_equal))
                if k == 0:
                    link(nc.vector.tensor_scalar(q, p, 1.0, None, ALU.add))
                    link(tt(q, q, oh, ALU.mult))
                    link(tt(p, p, q, ALU.subtract))

            dve.wait_ge(lu_done, 2)
            softmax(rt, rc, lg[:], rb_rows[:], r_max, r_exp)
            for k in range(2):
                choose(rt, rc, k, w01[:, k, :])
            tt(wsum[:], w01[:, 0, :], w01[:, 1, :], ALU.add).then_inc(w01_ok, 1)
            link(tt(rt["l"][:], rt["oh1"][:], rt["oh0"][:], ALU.subtract))
            for s in range(NS):
                for k, oh in ((0, rt["oh0"]), (1, rt["l"])):
                    for h in range(2):
                        js = slice(s * TPS, (s + 1) * TPS)
                        last = nc.vector.tensor_scalar(
                            mexp[k][:, js, h * ER:(h + 1) * ER].rearrange("p j (e r) -> p j e r", r=R),
                            oh[:, js, :].unsqueeze(3).to_broadcast([P, TPS, E, R]), LORA_SCALE, None, ALU.mult)
                    last.then_inc(mexp_ok, 1)
            for n in range(2 * NS):
                s, k = n // 2, n % 2
                z, cols = (z_base, z_step)[k], slice(s * SUP, (s + 1) * SUP)
                dve.wait_ge(mt_read, n + 1)
                if n == 0:
                    dve.wait_ge(w2_lo_done, FT)
                if n >= 2:
                    dve.wait_ge(z_ok, n - 1)
                link(tt(zf[n % 2][:], u1t[:, cols], (m_base, m_step)[k][:, cols], ALU.mult))
                nc.vector.tensor_copy(z[:, cols], zf[n % 2][:]).then_inc(z_hi, 1)

            def hidden_tile(i, v, u):
                n = i * G_OPS
                dve.wait_ge(h0_done, i + 1)
                tt(h0[u][:], h0[u][:], wb[:, v, 0, :], ALU.mult).then_inc(gch, 1)
                dve.wait_ge(h1_done, i + 3)
                tt(h1[u][:], h1[u][:], wb[:, v, 1, :], ALU.mult).then_inc(gch, 1)
                dve.wait_ge(gch, n + 2)
                dve.wait_ge(d_done, i + 1)
                tt(h0[u][:], h0[u][:], h1[u][:], ALU.add).then_inc(gch, 1)
                nc.vector.tensor_copy(g1_hi[u][:], h1[u][:]).then_inc(gch, 1)
                dve.wait_ge(gch, n + 3)
                nc.vector.tensor_copy(g_hi[u][:], h0[u][:]).then_inc(gch, 1)
                dve.wait_ge(gch, n + 4)
                tt(g1_lo[u][:], h1[u][:], g1_hi[u][:].bitcast(F32), ALU.subtract).then_inc(gch, 1)
                dve.wait_ge(gch, n + 5)
                tt(g_lo[u][:], h0[u][:], g_hi[u][:].bitcast(F32), ALU.subtract).then_inc(g_done, 1)

            def bias_rows(s):
                dve.wait_ge(xres_in, (s + 1) * 16)
                for j in range(TPS):
                    jj = s * TPS + j
                    last = nc.vector.scalar_tensor_tensor(out=xres[:, j, :], in0=b2_rows[:], scalar=wsum[:, jj:jj + 1],
                                                          in1=xres[:, j, :], op0=ALU.mult, op1=ALU.add)
                last.then_inc(xb_done, 1)

            def low_rank(s):
                dve.wait_ge(d_done, 2 + (s + 1) * FT)
                cols = slice(s * SUP, (s + 1) * SUP)
                tt(zz[:], ps_u[:, 0, :], m_base[:, cols], ALU.mult).then_inc(ech, 1)
                tt(zq[:], ps_u[:, 1, :], m_step[:, cols], ALU.mult).then_inc(ech, 1)
                dve.wait_ge(ech, s * 4 + 2)
                tt(zz[:], zz[:], zq[:], ALU.add).then_inc(ech, 1)
                dve.wait_ge(ech, s * 4 + 3)
                dve.wait_ge(y_done, 1 + s)
                nc.vector.tensor_copy(z2_hi[:], zz[:]).then_inc(ech, 1)
                dve.wait_ge(ech, s * 4 + 4)
                tt(z2_lo[:], zz[:], z2_hi[:].bitcast(F32), ALU.subtract).then_inc(z2_ok, 1)

            def add_sums(s):
                dve.wait_ge(xb_done, s + 1)
                dve.wait_ge(y_done, 1 + s + 1)
                for j in range(TPS):
                    tt(xres[:, j, :], ps_y[:, j, :], xres[:, j, :], ALU.add).then_inc(y_read, 1)

            for s in range(NS):
                v = s % 2
                dve.wait_ge(wb_in[v], (s // 2 + 1) * 32)
                hidden_tile(s * FT, v, 0)
                if s:
                    add_sums(s - 1)
                hidden_tile(s * FT + 1, v, 1)
                with dve.Fori(1, FT // 2) as m:
                    for u in range(2):
                        hidden_tile(m * 2 + (s * FT + u), v, u)
                bias_rows(s)
                low_rank(s)
            def diagonals(s):
                u = s % 2
                for h in range(2):
                    rows = slice(h * SEQ, (h + 1) * SEQ)
                    nc.vector.tensor_copy(bdq[u][rows, :, h * SEQ:(h + 1) * SEQ],
                                          cw1[rows, s * TPS:(s + 1) * TPS, :]).then_inc(bdq_done, 1)
            for h in range(2):
                dve.wait_ge(cw1_in[h], 16 * 2 * J)
            dve.wait_ge(bdq_zero, 2)
            diagonals(0)
            through(dve, l0_over, 5)

            def low_s(n):
                dve.wait_ge(s_hi_done, n + 1)
                hi, lo, raw = shared_halves(n)
                tt(lo, raw, hi.bitcast(F32), ALU.subtract).then_inc(sg_lo_done[0], 1)

            def rows_step(s, k):
                if k < 2:
                    for j in (2 * k, 2 * k + 1):
                        if s:
                            dve.wait_ge(xc_st, 16 * s)
                            dve.wait_ge(xt1_done, DC * s)
                        dve.wait_ge(c1_done, s * TPS + j + 1)
                        jj = s * TPS + j
                        nc.vector.tensor_scalar(xc[:, j, :], ps_u[:, j % 2, :], side_col[:, jj:jj + 1], None, ALU.add)\
                            .then_inc(xc_done, 1)
                    if k == 1 and s + 1 < NS:
                        diagonals(s + 1)
                elif k < 4:
                    for c in (2 * k - 4, 2 * k - 3):
                        dve.wait_ge(xs_hi_done, s * DC + c + 1)
                        tt(xs_lo[s % 2][:, c, :], ps_u[:, c % 2, :], xs_hi[s % 2][:, c, :].bitcast(F32),
                           ALU.subtract).then_inc(xs_lo_done, 1)
                elif k == 5:
                    dve.wait_ge(lgt1_done, s + 1)
                    nc.vector.tensor_copy(lg1[:, s * TPS:(s + 1) * TPS].rearrange("p j k e -> p (j k e)"),
                                          ps_u[:, 1, 0:TPS * 2 * E]).then_inc(lg1_read, 1)

            def route_tokens(k):
                if k == 0:
                    dve.wait_ge(lg1_read, NS)
                    softmax(q1, c1, lg1[:], None, r1_max, r1_exp)
                choose(q1, c1, k, w1k[:, k, :])
                if k == 1:
                    tt(mask16[:], q1["oh0"][:], q1["oh1"][:], ALU.add).then_inc(mask_ok, 1)

            def count_tokens():
                for k in range(2):
                    nc.vector.tensor_copy(pay[:, k, :, 0], tok_id[:])
                dve.wait_ge(cnt_done, 1)
                tot = ps_u[:, 0, P:2 * P].rearrange("p (j e) -> p j e", e=E)
                link(nc.vector.tensor_copy(rank[:], ps_u[:, 0, 0:P].rearrange("p (j e) -> p j e", e=E)))
                link(nc.vector.tensor_copy(cnt[0][:], tot))
                a, b = 0, 1
                d = 1
                while d < J:
                    nc.vector.tensor_copy(cnt[b][:, 0:d, :], cnt[a][:, 0:d, :])
                    link(tt(cnt[b][:, d:J, :], cnt[a][:, d:J, :], cnt[a][:, 0:J - d, :], ALU.add))
                    a, b, d = b, a, 2 * d
                ca = cnt[a]
                link(nc.vector.tensor_scalar(ex_i[:], ca[:, J - 1, :], 1.0, float(P - 1), ALU.max, ALU.add))
                link(nc.vector.tensor_single_scalar(ex_i[:], ex_i[:], 7, ALU.logical_shift_right))
                link(nc.vector.tensor_copy(ex["t"][:], ex_i[:]))
                link(nc.vector.tensor_copy(ex["a"][:], ex["t"][:]))
                xa, xb_, d = ex["a"], ex["b"], 1
                while d < E:
                    nc.vector.tensor_copy(xb_[:, 0:d], xa[:, 0:d])
                    link(tt(xb_[:, d:E], xa[:, d:E], xa[:, 0:E - d], ALU.add))
                    xa, xb_, d = xb_, xa, 2 * d
                dve.wait_ge(slot_set, 3)
                link(tt(etab3[:], etile[:].unsqueeze(2).to_broadcast([P, ETAB, E]),
                        xa[:].unsqueeze(1).to_broadcast([P, ETAB, E]), ALU.is_ge))
                link(nc.vector.tensor_reduce(etab_f[:], etab3[:], AX.X, ALU.add))
                link(nc.vector.memset(last_tile[:], 0))
                nc.vector.tensor_copy(last_tile[:, 2:E + 2], xa[:])
                link(nc.vector.tensor_scalar(etab_f[:], etab_f[:], float(E - 1), None, ALU.min))
                windows = ETAB - WINDOW + 1
                link(nc.vector.memset(etab_g[:], 0.0))
                link(nc.vector.tensor_copy(etab_g[:, 0:windows], etab_f[:, WINDOW - 1:ETAB]))
                for n in reversed(range(WINDOW - 1)):
                    link(nc.vector.scalar_tensor_tensor(out=etab_g[:, 0:windows], in0=etab_g[:, 0:windows],
                                                        scalar=float(E), in1=etab_f[:, n:n + windows],
                                                        op0=ALU.mult, op1=ALU.add))
                nc.vector.tensor_copy(etab[:], etab_g[:]).then_inc(etab_ok, 1)
                return ca, xa, xb_, tot

            def place_tokens(ca, xa, xb_, tot):
                oh0, oh1 = q1["oh0"][:], q1["oh1"][:]
                link(tt(xb_[:], xa[:], ex["t"][:], ALU.subtract))
                link(nc.vector.tensor_scalar(xb_[:], xb_[:], float(P), None, ALU.mult))
                link(tt(ca[:], ca[:], tot, ALU.subtract))
                link(tt(ca[:], ca[:], rank[:], ALU.add))
                link(tt(ca[:], ca[:], xb_[:].unsqueeze(1).to_broadcast([P, J, E]), ALU.add))
                for k, oh in ((0, oh0), (1, oh1)):
                    link(tt(rank[:], ca[:], oh, ALU.mult))
                    last = nc.vector.tensor_reduce(c1["m" if k else "s"][:], rank[:], AX.X, ALU.add)
                    link(last)
                    link(nc.vector.tensor_copy(pos_i[:, k, :], c1["m" if k else "s"][:]))
                nc.vector.tensor_copy(pay[:, :, :, 1].bitcast(F32), w1k[:]).then_inc(pos_ok, 1)


            def split_expert(e, u, k):
                gu, full = DC * 2 * H1, H1 // P
                raw_g = e_raw[:, 0:gu].rearrange("p (c n) -> p c n", c=DC)
                raw_d = e_raw[:, gu:gu + full * D].rearrange("p (c n) -> p c n", n=D)
                tail, raw_t = H1 - full * P, e_raw[0:H1 - full * P, gu + full * D:]
                if k == 0:
                    nc.vector.tensor_copy(eg_hi[:, u], raw_g).then_inc(e_ch, 1)
                elif k == 1:
                    dve.wait_ge(e_ch, 2 * e + 1)
                    tt(eg_lo[:, u], raw_g, eg_hi[:, u].bitcast(F32), ALU.subtract)
                elif k == 2:
                    nc.vector.tensor_copy(ed_hi[:, u, 0:full], raw_d)
                    nc.vector.tensor_copy(ed_hi[0:tail, u, full], raw_t).then_inc(e_ch, 1)
                else:
                    dve.wait_ge(e_ch, 2 * e + 2)
                    tt(ed_lo[:, u, 0:full], raw_d, ed_hi[:, u, 0:full].bitcast(F32), ALU.subtract)
                    tt(ed_lo[0:tail, u, full], raw_t, ed_hi[0:tail, u, full].bitcast(F32), ALU.subtract)\
                        .then_inc(e_done, 1)

            rows_step(0, 0)
            low_s(0)
            rows_step(0, 1)
            dve.wait_ge(gate_in, 16)
            nc.vector.tensor_copy(gate_hl[:, :, 0, :], gate_raw[:]).then_inc(gate_done, 1)
            dve.wait_ge(gate_done, 1)
            tt(gate_hl[:, :, 1, :], gate_raw[:], gate_hl[:, :, 0, :].bitcast(F32), ALU.subtract).then_inc(gate_done, 1)
            rows_step(0, 2)
            rows_step(0, 3)
            low_s(2)
            add_sums(NS - 1)
            rows_step(0, 5)

            dve.wait_ge(x1_st, 16 + 16 * NS)
            for s in range(NS):
                for q in range(SH):
                    i = s * SH + q
                    dve.wait_ge(sil_done, i + 1)
                    if i:
                        dve.wait_ge(slo_done, i)
                    tt(sh_g[:], sh_s[:], ps_y[:, q % 2, :], ALU.mult).then_inc(mul_done, 1)
                    dve.wait_ge(mul_done, i + 1)
                    if s:
                        dve.wait_ge(sy_done, s * TPS)
                    nc.vector.tensor_copy(sh_hi[:, q, :], sh_g[:]).then_inc(shi_done, 1)
                    dve.wait_ge(shi_done, i + 1)
                    tt(sh_lo[:, q, :], sh_g[:], sh_hi[:, q, :].bitcast(F32), ALU.subtract).then_inc(slo_done, 1)
                    if rows_step_after_gate_up(s, q):
                        rows_step(*rows_step_after_gate_up(s, q))
                    if s == NS - 2 and q in (ROUTE_AT, ROUTE_AT + 1):
                        route_tokens(q - ROUTE_AT)
                    if (s, q) == (NS - 2, ROUTE_AT + 2):
                        counts = count_tokens()
                    if (s, q) == (NS - 2, ROUTE_AT + 3):
                        place_tokens(*counts)
                for j in range(TPS):
                    dve.wait_ge(sy_done, s * TPS + j + 1)
                    a = acc[:, s * TPS + j, :]
                    tt(a, ps_y[:, 2 + j % 2, :], a, ALU.add).then_inc(sy_read, 1)
                    if rows_step_after_down(s, j):
                        rows_step(*rows_step_after_down(s, j))
                    if (s, j) == (NS - 1, 0):
                        dve.wait_ge(slot_in, 16)
                        for k in range(2):
                            src = slot_tab[:, :, k]
                            last = nc.vector.tensor_copy(slot_f[:, k, :], src.bitcast(F32) if k else src)
                        last.then_inc(slot_cv, 1)
                    if (s, j) == (NS - 1, 1):
                        dve.wait_ge(slot_tr, 1)
                        nc.vector.tensor_copy(slot_w[:], ps_u[:, 1, ETAB:2 * ETAB])
                        nc.vector.tensor_copy(slot_tok[:], ps_u[:, 1, 0:ETAB]).then_inc(slot_ok, 1)
                    if s == NS - 1:
                        if j == 0:
                            dve.wait_ge(e_in, 48)
                        for k in ((0, 1), (2,), (3,), ())[j]:
                            split_expert(0, 0, k)

            for e in range(1, E):
                dve.wait_ge(e_in, 48 * (e + 1))
                if e >= 2:
                    tiles = dve.value_load(last_tile[0:1, e:e + 1], min_val=0, max_val=SLOT_TILES)
                    dve.wait_ge(ry_done, 1 + tiles)
                for k in range(4):
                    split_expert(e, e % 2, k)

        @block.tensor
        def _(pe):
            mm = nc.tensor.matmul

            def logit_rows(s):
                pe.wait_ge(lgt_cp, s + 1)
                for j in range(TPS):
                    at = (PREP[s] * TPS + j) * 2 * E
                    last = nc.tensor.transpose(ps_u[:, 0, at:at + 2 * E], lg_t[:, j * P:(j + 1) * P],
                                               ident[0:2 * E, 0:2 * E])
                last.then_inc(lgt_done, 1)

            def keep_warm(bank, count):
                for _ in range(count):
                    mm(bank, zero16[:, 0:P], zero16[:], start=True, stop=True)

            pe.sem_inc(z_done, 2)
            pe.sem_inc(d_done, 2)
            opened(pe, cond_done, y_done, ry_done)
            pe.wait_ge(const_set, 9)
            keep_warm(ps_h[:, 0, :], 38)
            for s in range(NS):
                u = s % 2
                for h in range(2):
                    pe.wait_ge(bd_in[s][h], 16 * TPS)
                pe.wait_ge(x_in_s[u], (s // 2 + 1) * 16)
                for c in range(DC):
                    pe.wait_ge(xt_lo_done, s * DC + c + 1)
                    for j in range(TPS):
                        last = mm(ps_y[:, c, j * P:(j + 1) * P], x_in[u][:, j, c * P:(c + 1) * P],
                                  bd[:, PREP[s] * TPS + j, :], start=True, stop=True)
                    last.then_inc(cond_done, 1)
                if s:
                    logit_rows(s - 1)
                pe.wait_ge(xt_lo_done, 4 + (s + 1) * DC)
                pe.wait_ge(split_small, 6)
                if s:
                    pe.wait_ge(lgt_cp, s)
                    pe.wait_ge(u1_read, s)
                for c in range(DC):
                    mm(ps_h[0:2 * E, 0, :], rw_hl[:, c].rearrange("p k e -> p (k e)"), xt_hi[u][:, c, :],
                       start=(c == 0), stop=False)
                    last = mm(ps_h[0:2 * E, 0, :], rw_hl[:, c].rearrange("p k e -> p (k e)"), xt_lo[u][:, c, :],
                              start=False, stop=(c == DC - 1))
                last.then_inc(lg_done, 1)
                for c in range(DC):
                    mm(ps_h[:, 1, :], u1_hi[:, c, :], xt_hi[u][:, c, :], start=(c == 0), stop=False)
                    mm(ps_h[:, 1, :], u1_hi[:, c, :], xt_lo[u][:, c, :], start=False, stop=False)
                    last = mm(ps_h[:, 1, :], u1_lo[:, c, :], xt_hi[u][:, c, :], start=False, stop=(c == DC - 1))
                last.then_inc(u1_done, 1)
            logit_rows(NS - 1)
            def w_chunk(u, half, c):
                at = half * (WT + ER) + c * P
                return w_hl[u][:, at:at + P]

            def hidden_x(i, v, u):
                pe.wait_ge(w1_lo_done, i + 3)
                pe.wait_ge(h1_done, i + 1)
                for c in range(DC):
                    mm(ps_h[:, u, :], w_chunk(u, 0, c), xt_hi[v][:, c, :], start=(c == 0), stop=False)
                    mm(ps_h[:, u, :], w_chunk(u, 0, c), xt_lo[v][:, c, :], start=False, stop=False)
                    mm(ps_h[:, u, :], w_chunk(u, 1, c), xt_hi[v][:, c, :], start=False, stop=False)

            def hidden_z(s, u):
                if s == 0:
                    pe.wait_ge(z_ok, 1)
                zb = z_base[:, s * SUP:(s + 1) * SUP]
                mm(ps_h[:, u, :], w_chunk(u, 0, DC), zb, start=False, stop=False)
                mm(ps_h[:, u, :], w_chunk(u, 1, DC), zb, start=False, stop=True).then_inc(a_done, 1)

            def hidden(i, s, v, u):
                hidden_x(i, v, u)
                hidden_z(s, u)

            def second(i, s, u):
                pe.wait_ge(h0_done, i + 1)
                chunk = lambda half, c: w_chunk(u, half, c)
                pe.wait_ge(z_ok, 2 * (s + 1))
                zs = z_step[:, s * SUP:(s + 1) * SUP]
                mm(ps_h[:, u, :], chunk(0, DC), zs, start=False, stop=False, skip_group_check=True)
                mm(ps_h[:, u, :], chunk(1, DC), zs, start=False, stop=True, skip_group_check=True)\
                    .then_inc(z_done, 1)

            def down(i, f, u, half):
                if half == 0:
                    pe.wait_ge(g_done, i + 3)
                kw = dict(start=False, stop=False, skip_group_check=True)
                sl = lambda t: t[:, bass.ds(f, 1), :].rearrange("p a n -> p (a n)")
                for j in range(half * 2, half * 2 + 2):
                    cols = slice(j * P, (j + 1) * P)
                    mm(ps_y[:, j, :], g_hi[u][:, cols], sl(w2_hi), **kw)
                    mm(ps_y[:, j, :], g_hi[u][:, cols], sl(w2_lo), **kw)
                    last = mm(ps_y[:, j, :], g_lo[u][:, cols], sl(w2_hi), **kw)
                if half == 0:
                    a2 = w_hl[1 - u][:, WT - ER:WT + ER]
                    for k, g in ((0, g_hi), (0, g_lo), (1, g1_hi), (1, g1_lo)):
                        mm(ps_u[:, k, :], a2, g[u][:], **kw)
                if half == 1:
                    last.then_inc(d_done, 1)

            def zero_sums(s):
                for j in range(TPS):
                    if s:
                        pe.wait_ge(y_read, (s - 1) * TPS + j + 1)
                    mm(ps_y[:, j, :], zero16[:, 0:P], zero16[:], start=True, stop=False, skip_group_check=True)
                for k in range(2):
                    mm(ps_u[:, k, :], zero16[:, 0:P], zero16[:], start=True, stop=False, skip_group_check=True)

            def step(i, s, v, f, u):
                hidden(i, s, v, u)
                down(i - 1, f - 1, 1 - u, 0)
                second(i, s, u)
                down(i - 1, f - 1, 1 - u, 1)

            def sums_end(s):
                pe.wait_ge(z2_ok, s + 1)
                for j in range(TPS):
                    cols = slice(j * P, (j + 1) * P)
                    mm(ps_y[:, j, :], z2_hi[:, cols], b2s_hi[:], start=False, stop=False, skip_group_check=True)
                    mm(ps_y[:, j, :], z2_hi[:, cols], b2s_lo[:], start=False, stop=False, skip_group_check=True)
                    last = mm(ps_y[:, j, :], z2_lo[:, cols], b2s_hi[:], start=False, stop=True, skip_group_check=True)
                last.then_inc(y_done, 1)

            def super_tile(s, v):
                base = s * FT
                if s:
                    hidden_x(base + 1, v, 1)
                hidden_z(s, 1)
                second(base, s, 0)
                if s:
                    sums_end(s - 1)
                second(base + 1, s, 1)
                zero_sums(s)
                down(base, 0, 0, 0)
                down(base, 0, 0, 1)
                pe.wait_ge(z_ok, 2 * NS)
                with pe.Fori(1, FT // 2) as m:
                    for u in range(2):
                        step(m * 2 + (base + u), s, v, m * 2 + u, u)
                if s + 1 < NS:
                    if s + 1 >= 2:
                        pe.wait_ge(xt_in[1 - v], 32 * ((s + 1) // 2))
                    hidden(base + FT, s + 1, 1 - v, 0)
                else:
                    pe.wait_ge(w1_lo_done, base + FT + 3)
                    pe.wait_ge(h1_done, base + FT + 2)
                    keep_warm(ps_h[:, 0, :], 8)
                down(base + FT - 1, FT - 1, 1, 0)
                down(base + FT - 1, FT - 1, 1, 1)

            pe.wait_ge(lgt_cp, NS)
            pe.wait_ge(u1_read, NS)
            for u in range(2):
                hidden_x(u, 0, u)
            keep_warm(ps_y[:, 3, :], 0)
            pe.wait_ge(w01_ok, 1)
            nc.tensor.transpose(ps_u[0:2 * J, 1, 0:P], w01[:].rearrange("p k j -> p (k j)"), ident[:])\
                .then_inc(w01t_done, 1)
            for n in range(2 * NS):
                s, k = n // 2, n % 2
                pe.wait_ge(mexp_ok, n + 1)
                if n >= 4:
                    pe.wait_ge(mt_read, n - 3)
                for j in range(TPS):
                    last = nc.tensor.transpose(mt_bank(n)[:, j * P:(j + 1) * P], mexp[k][:, s * TPS + j, :], ident16[:])
                last.then_inc(mt_done, 1)
            hidden_z(0, 0)
            for s in range(NS):
                super_tile(s, s % 2)
            keep_warm(ps_h[:, 0, :], 12)
            sums_end(NS - 1)
            through(pe, l0_over, 5)

            def rows_step(s, k):
                u = s % 2
                if k < 2:
                    pe.wait_ge(acc_in[s], 16)
                    pe.wait_ge(bdq_done, 2 * (s + 1))
                    if k == 0 and s:
                        pe.wait_ge(lg1_read, s)
                    for j in (2 * k, 2 * k + 1):
                        if j >= 2:
                            pe.wait_ge(xc_done, s * TPS + j - 1)
                        mm(ps_u[:, j % 2, :], bdq[u][:, j, :], acc[:, s * TPS + j, :], start=True, stop=True)\
                            .then_inc(c1_done, 1)
                elif k < 4:
                    pe.wait_ge(xc_done, (s + 1) * TPS)
                    for c in (2 * k - 4, 2 * k - 3):
                        if c >= 2:
                            pe.wait_ge(xs_lo_done, s * DC + c - 1)
                        for j in range(TPS):
                            last = nc.tensor.transpose(ps_u[:, c % 2, j * P:(j + 1) * P],
                                                       xc[:, j, c * P:(c + 1) * P], ident[:])
                        last.then_inc(xt1_done, 1)
                elif k == 4:
                    pe.wait_ge(gate_done, 2)
                    pe.wait_ge(xs_lo_done, (s + 1) * DC)
                    for c in range(DC):
                        w = gate_hl[:, c].rearrange("p k e -> p (k e)")
                        mm(ps_u[0:2 * E, 0, :], w, xs_hi[u][:, c, :], start=(c == 0), stop=False)
                        last = mm(ps_u[0:2 * E, 0, :], w, xs_lo[u][:, c, :], start=False, stop=(c == DC - 1))
                    last.then_inc(lg1_done, 1)
                else:
                    pe.wait_ge(lgt1_cp, s + 1)
                    for j in range(TPS):
                        last = nc.tensor.transpose(ps_u[:, 1, j * 2 * E:(j + 1) * 2 * E], lgt1[:, j * P:(j + 1) * P],
                                                   ident[0:2 * E, 0:2 * E])
                    last.then_inc(lgt1_done, 1)

            def gate_up_shared(s, q):
                u, i, cols = s % 2, s * SH + q, slice(q * P, (q + 1) * P)
                if i == 0:
                    pe.wait_ge(y_read, NS * TPS)
                if i >= 2:
                    pe.wait_ge(mul_done, i - 1)
                for k, o in ((0, ps_h[:, q % 2, :]), (1, ps_y[:, q % 2, :])):
                    for c in range(DC):
                        if i == 0 and k == 0:
                            pe.wait_ge(sg_lo_done[c % 2], c // 2 + 1)
                        mm(o, sg_hi[:, c, k, cols], xs_hi[u][:, c, :], start=(c == 0), stop=False)
                        mm(o, sg_hi[:, c, k, cols], xs_lo[u][:, c, :], start=False, stop=False)
                        last = mm(o, sg_lo[:, c, k, cols], xs_hi[u][:, c, :], start=False, stop=(c == DC - 1))
                last.then_inc(gu_done, 1)

            def down_shared(s, j):
                if s == 0 and j == 0:
                    pe.wait_ge(sd_lo_done, SH // 2)
                if s * TPS + j >= 2:
                    pe.wait_ge(sy_read, s * TPS + j - 1)
                cols = slice(j * P, (j + 1) * P)
                o = ps_y[:, 2 + j % 2, :]
                for q in range(SH):
                    if j == 0:
                        pe.wait_ge(slo_done, s * SH + q + 1)
                    mm(o, sh_hi[:, q, cols], sd_hi[:, q, :], start=(q == 0), stop=False)
                    mm(o, sh_hi[:, q, cols], sd_lo[:, q, :], start=False, stop=False)
                    last = mm(o, sh_lo[:, q, cols], sd_hi[:, q, :], start=False, stop=(q == SH - 1))
                last.then_inc(sy_done, 1)

            for k in range(ROWS_STEPS):
                rows_step(0, k)
                keep_warm(ps_h[:, 0, :], 2)
            for s in range(NS):
                for q in range(SH):
                    gate_up_shared(s, q)
                    if rows_step_after_gate_up(s, q):
                        rows_step(*rows_step_after_gate_up(s, q))
                    if (s, q) == (NS - 2, ROUTE_AT + 2):
                        pe.wait_ge(mask_ok, 1)
                        mask_row = mask16[:].rearrange("p j e -> p (j e)")
                        mm(ps_u[:, 0, 0:P], tri[:], mask_row, start=True, stop=True)
                        mm(ps_u[:, 0, P:2 * P], ones16[:], mask_row, start=True, stop=True).then_inc(cnt_done, 1)
                for j in range(TPS):
                    down_shared(s, j)
                    if rows_step_after_down(s, j):
                        rows_step(*rows_step_after_down(s, j))
                    if (s, j) == (NS - 1, 0):
                        pe.wait_ge(slot_cv, 1)
                        for k in range(2):
                            last = nc.tensor.transpose(ps_u[:, 1, k * ETAB:(k + 1) * ETAB], slot_f[:, k, :],
                                                       ident[0:ETAB, 0:ETAB])
                        last.then_inc(slot_tr, 1)

            pe.wait_ge(etab_ok, 1)

            def experts(t):
                packed = pe.value_load(etab[0:1, bass.ds(t, 1)], min_val=0, max_val=E ** WINDOW - 1)
                return [(packed // E ** n % E, packed // E ** n % 2) for n in range(WINDOW)]

            def turn_x(t, u, n, first=False):
                pe.wait_ge(xg_in[u], n)
                if not first:
                    pe.wait_ge(xg_f_done, t)
                for c in range(DC):
                    last = nc.tensor.transpose(ps_u[:, 0, c * P:(c + 1) * P], xg[u][:, c * P:(c + 1) * P], ident[:])
                last.then_inc(xgt_done, 1)

            def gate_or_up(t, u, eb, k):
                e, b = eb
                if k == 0:
                    pe.wait_ge(e_done, e + 1)
                    pe.wait_ge(xg_hi_done, t + 1)
                    if not isinstance(t, int) or t >= 2:
                        pe.wait_ge(ru_done, t - 1)
                o = (ps_h, ps_y)[k][:, u, 0:H1]
                w = lambda half, c: half[:, bass.ds(b, 1), c, k * H1:(k + 1) * H1].rearrange("p a n -> p (a n)")
                for c in range(DC):
                    mm(o, xg_hi[:, c, :], w(eg_hi, c), start=(c == 0), stop=False)
                    mm(o, xg_hi[:, c, :], w(eg_lo, c), start=False, stop=False)
                if k == 0:
                    pe.wait_ge(xg_lo_done, t + 1)
                for c in range(DC):
                    last = mm(o, xg_lo[:, c, :], w(eg_hi, c), start=False, stop=(c == DC - 1))
                last.then_inc((rgate_done, rup_done)[k], 1)

            def turn_g(t):
                pe.wait_ge(rg_done, t + 1)
                if not isinstance(t, int) or t:
                    pe.wait_ge(rgt_f_done, t)
                for c in range(HC):
                    last = nc.tensor.transpose(ps_u[:, 1, c * P:(c + 1) * P], rg[:, c * P:(c + 1) * P], ident[:])
                last.then_inc(rgt_done, 1)

            def down_routed(t, u, eb):
                e, b = eb
                pe.wait_ge(rgt_hi_done, t + 1)
                if not isinstance(t, int) or t >= 2:
                    pe.wait_ge(ry_cp, t - 1)
                w = lambda half, c, k: half[0:k, bass.ds(b, 1), c, :].rearrange("p a n -> p (a n)")
                o = ps_y[:, 2 + u, :]
                for c in range(HC):
                    k = min(P, H1 - c * P)
                    mm(o, rgt_hi[0:k, c, :], w(ed_hi, c, k), start=(c == 0), stop=False)
                    mm(o, rgt_hi[0:k, c, :], w(ed_lo, c, k), start=False, stop=False)
                pe.wait_ge(rgt_lo_done, t + 1)
                for c in range(HC):
                    k = min(P, H1 - c * P)
                    last = mm(o, rgt_lo[0:k, c, :], w(ed_hi, c, k), start=False, stop=(c == HC - 1))
                last.then_inc(ry_done, 1)

            def slot_tile(t, u, x_buf, n, this, after, nxt=True, nxt2=True):
                if nxt:
                    gate_or_up(t + 1, 1 - u, after, 0)
                turn_g(t)
                if nxt:
                    gate_or_up(t + 1, 1 - u, after, 1)
                if nxt2:
                    turn_x(t + 2, x_buf, n)
                down_routed(t, u, this)

            pe.wait_ge(rg_zero, 1)
            turn_x(0, 0, 16, first=True)
            e = experts(0)
            gate_or_up(0, 0, e[0], 0)
            gate_or_up(0, 0, e[0], 1)
            turn_x(1, 1, 16)
            pe.wait_ge(slot_ok, 1)
            pe.wait_ge(sy_read, NS * TPS)
            ahead = WINDOW - 1
            for t in range(ahead):
                slot_tile(t, t % 2, (t + 2) % 4, ((t + 2) // 4 + 1) * 16, e[t], e[t + 1])
            with pe.Fori(1, (SLOT_TILES - 2) // ahead) as m:
                e = experts(m * ahead)
                for u in range(ahead):
                    slot_tile(m * ahead + u, u % 2, (u + 2) % 4, (m + (u + 2) // 4 + 1) * 16, e[u], e[u + 1])
            rest = range((SLOT_TILES - 2) // ahead * ahead, SLOT_TILES)
            e = experts(SLOT_TILES - WINDOW)[WINDOW - len(rest):] + [None]
            for n, t in enumerate(rest):
                slot_tile(t, t % 2, (t + 2) % 4, ((t + 2) // 4 + 1) * 16, e[n], e[n + 1],
                          t + 1 < SLOT_TILES, t + 2 < SLOT_TILES)


_OUT = (32, 64, 512)


def layouts(v):
    import numpy as np
    g = {k: np.asarray(a) for k, a in v.items()}
    c = np.ascontiguousarray
    f_tiles = 16
    w1t = g["L0_ffn_W1"].T.reshape(4, 128, f_tiles, 128).transpose(2, 1, 0, 3)
    b1t = g["L0_ffn_B1"].transpose(0, 2, 1).reshape(64, f_tiles, 128).transpose(1, 0, 2)
    w1b = np.concatenate([w1t, np.concatenate([b1t, b1t], 1)[:, :, None, :]], 2).reshape(f_tiles, 128, 640)
    bias = g["L0_ffn_b1"].reshape(f_tiles, 128, 1)
    a2t = np.roll(g["L0_ffn_A2"].reshape(64, f_tiles, 128).transpose(1, 2, 0), 1, 0)
    w1b = np.concatenate([w1b, a2t, bias, bias], 2)
    b2t = g["L0_ffn_B2"].transpose(0, 2, 1).reshape(64, 512)
    return dict(
        x=c(g["x"].reshape(2048, 512)),
        itok0=c(g["itok_B_1_198"].reshape(1, 32)),
        itok1=c(g["itok_B_0_7"].reshape(1, 32)),
        side=c(g["fside_8xS_0"].reshape(512, 1)),
        cond0=c(g["L0_cond_weights"].reshape(200 * 64, 64)),
        router0=c(np.concatenate([g["L0_ffn_W_r"], g["L0_ffn_A1"].reshape(64, 512)], 0).T),
        router0_b=c(g["L0_ffn_b_r"].reshape(1, 8)),
        w1b=c(w1b),
        w2=c(g["L0_ffn_W2"].T),
        b2=c(g["L0_ffn_b2"].reshape(1, 512)),
        b2s=c(np.concatenate([b2t, b2t], 0)),
        cond1=c(g["L1_cond_weights"].reshape(8 * 64, 64)),
        gate1=c(g["L1_ffn_gate_w"]),
        wgu1=c(np.concatenate([g["L1_ffn_w_gate"], g["L1_ffn_w_up"]], 2)),
        wdn1=c(g["L1_ffn_w_down"]),
        sgu1=c(np.concatenate([g["L1_ffn_sw_gate"], g["L1_ffn_sw_up"]], 1)),
        sdn1=c(g["L1_ffn_sw_down"]),
    )


def kernel(**inputs):
    import concourse.bacc as _bacc
    from concourse.bass_utils import run_bass_kernel_spmd as _run

    nc = _bacc.Bacc("TRN2", target_bir_lowering=False, num_devices=1)
    arrays, args = {}, []
    for name, a in layouts(inputs).items():
        arrays[f"in_{name}"] = a
        args.append(nc.dram_tensor(f"in_{name}", a.shape, mybir.dt.from_np(a.dtype), kind="ExternalInput").ap())
    out = nc.dram_tensor("out_x", (2048 + P, 512), F32, kind="ExternalOutput").ap()
    adaln_ffn(nc, *args, out)
    r = _run(nc, [arrays], core_ids=[0])
    return r.results[0]["out_x"][:2048].reshape(_OUT)
```
